# Optimizing a Trainium2 kernel written in Bass

```python
import numpy as np
import jax
import jax.numpy as jnp

def _softmax(x, axis=-1):
    return jax.nn.softmax(x, axis=axis)
def _gelu(x):
    return jax.nn.gelu(x, approximate=True)
def _silu(x):
    return jax.nn.silu(x)
def _sigmoid(x):
    return jax.nn.sigmoid(x)
def _layernorm(x, axis=-1, eps=1e-5):
    m = jnp.mean(x, axis=axis, keepdims=True)
    v = jnp.var(x, axis=axis, keepdims=True)
    return (x - m) / jnp.sqrt(v + eps)
def _scatter_add(tgt, idx, src, axis=0):
    return tgt.at[idx].add(src)
def _segment_sum(src, seg, n):
    return jax.ops.segment_sum(src, seg, n)

kernel_name = 'mk_conv_preact_d2_conv_nchw192_10dd82'

def setup_inputs(seed: int = 0):
    np.random.seed(seed)
    _w = jnp.asarray
    def _rec_inputs():
        import jax
        import jax.numpy as jnp
        _gk = jax.random.key(seed)
        x = -0.0005963 + 1.001 * jax.random.normal(jax.random.fold_in(_gk, 1), (4, 192, 64, 64), jnp.float32)
        return x
    x = _rec_inputs()
    def _L0_conv_setup():
        import jax, jax.numpy as jnp
        import numpy as np
        B, C, H, W = (4, 192, 64, 64)
        D_STATE, D_CONV, EXPAND = (16, 4, 2)
        DIN = EXPAND * C
        DT_RANK = (C + 15) // 16
        EPS = 1e-05

        def _silu(v):
            return v * jax.nn.sigmoid(v)

        def _snake(x2d):
            odd = (jnp.arange(x2d.shape[1]) % 2 == 1)[None, :, None, None]
            return jnp.where(odd, jnp.flip(x2d, axis=2), x2d)
        key = jax.random.key(seed)
        ks = jax.random.split(key, 12)
        s = lambda k, shape, sc: jax.random.normal(k, shape, dtype=jnp.float32) * sc
        inp = {'x': jax.random.normal(ks[0], (B, C, H, W), dtype=jnp.float32), 'gn_gamma': jnp.ones((C,), jnp.float32), 'gn_beta': jnp.zeros((C,), jnp.float32), 'in_proj_w': s(ks[1], (2 * DIN, C), 0.05), 'conv1d_w': s(ks[2], (DIN, D_CONV), 0.2), 'conv1d_b': jnp.zeros((DIN,), jnp.float32), 'x_proj_w': s(ks[3], (DT_RANK + 2 * D_STATE, DIN), 0.05), 'dt_proj_w': s(ks[4], (DIN, DT_RANK), 0.1), 'dt_proj_b': s(ks[5], (DIN,), 0.1), 'A_log': jnp.log(jnp.broadcast_to(jnp.arange(1, D_STATE + 1, dtype=jnp.float32), (DIN, D_STATE))), 'Dskip': jnp.ones((DIN,), jnp.float32), 'le_w': s(ks[6], (DIN, 1, 3, 3), 0.1), 'out_proj_w': s(ks[7], (C, DIN), 0.05), 'proj_out_w': s(ks[8], (C, C), 0.05)}
        return inp
    _L0_conv_all = _L0_conv_setup()
    _L0_conv_in = {k: v for k, v in _L0_conv_all.items() if k in ('gn_gamma', 'gn_beta', 'in_proj_w', 'conv1d_w', 'conv1d_b', 'x_proj_w', 'dt_proj_w', 'dt_proj_b', 'A_log', 'Dskip', 'le_w', 'out_proj_w', 'proj_out_w', )}
    del _L0_conv_all

    def _L1_conv_setup():
        import jax, jax.numpy as jnp
        import numpy as np
        from jax import lax
        DIM = 192
        HEADS = 4
        EPS = 1e-12

        def _l2norm(t, axis):
            n = jnp.sqrt(jnp.sum(t * t, axis=axis, keepdims=True))
            return t / jnp.maximum(n, EPS)
        key = jax.random.key(seed)
        ks = jax.random.split(key, 8)
        b, c, h, w = (2, DIM, 64, 64)
        x = jax.random.normal(ks[0], (b, c, h, w), dtype=jnp.float32)
        w_qkv = jax.random.normal(ks[1], (3 * c, c), dtype=jnp.float32) * 0.05
        b_qkv = jax.random.normal(ks[2], (3 * c,), dtype=jnp.float32) * 0.05
        w_dw = jax.random.normal(ks[3], (3 * c, 1, 3, 3), dtype=jnp.float32) * 0.05
        b_dw = jax.random.normal(ks[4], (3 * c,), dtype=jnp.float32) * 0.05
        w_proj = jax.random.normal(ks[5], (c, c), dtype=jnp.float32) * 0.05
        b_proj = jax.random.normal(ks[6], (c,), dtype=jnp.float32) * 0.05
        temperature = jnp.ones((HEADS, 1, 1), dtype=jnp.float32)
        return {'x': x, 'w_qkv': w_qkv, 'b_qkv': b_qkv, 'w_dw': w_dw, 'b_dw': b_dw, 'w_proj': w_proj, 'b_proj': b_proj, 'temperature': temperature}
    _L1_conv_all = _L1_conv_setup()
    _L1_conv_in = {k: v for k, v in _L1_conv_all.items() if k in ('w_qkv', 'b_qkv', 'w_dw', 'b_dw', 'w_proj', 'b_proj', 'temperature', )}
    del _L1_conv_all

    return {
        "x": x,
        "L0_conv_gn_gamma": _L0_conv_in["gn_gamma"],
        "L0_conv_gn_beta": _L0_conv_in["gn_beta"],
        "L0_conv_in_proj_w": _L0_conv_in["in_proj_w"],
        "L0_conv_conv1d_w": _L0_conv_in["conv1d_w"],
        "L0_conv_conv1d_b": _L0_conv_in["conv1d_b"],
        "L0_conv_x_proj_w": _L0_conv_in["x_proj_w"],
        "L0_conv_dt_proj_w": _L0_conv_in["dt_proj_w"],
        "L0_conv_dt_proj_b": _L0_conv_in["dt_proj_b"],
        "L0_conv_A_log": _L0_conv_in["A_log"],
        "L0_conv_Dskip": _L0_conv_in["Dskip"],
        "L0_conv_le_w": _L0_conv_in["le_w"],
        "L0_conv_out_proj_w": _L0_conv_in["out_proj_w"],
        "L0_conv_proj_out_w": _L0_conv_in["proj_out_w"],
        "L1_conv_w_qkv": _L1_conv_in["w_qkv"],
        "L1_conv_b_qkv": _L1_conv_in["b_qkv"],
        "L1_conv_w_dw": _L1_conv_in["w_dw"],
        "L1_conv_b_dw": _L1_conv_in["b_dw"],
        "L1_conv_w_proj": _L1_conv_in["w_proj"],
        "L1_conv_b_proj": _L1_conv_in["b_proj"],
        "L1_conv_temperature": _L1_conv_in["temperature"],
    }

def reference(x, L0_conv_gn_gamma, L0_conv_gn_beta, L0_conv_in_proj_w, L0_conv_conv1d_w, L0_conv_conv1d_b, L0_conv_x_proj_w, L0_conv_dt_proj_w, L0_conv_dt_proj_b, L0_conv_A_log, L0_conv_Dskip, L0_conv_le_w, L0_conv_out_proj_w, L0_conv_proj_out_w, L1_conv_w_qkv, L1_conv_b_qkv, L1_conv_w_dw, L1_conv_b_dw, L1_conv_w_proj, L1_conv_b_proj, L1_conv_temperature):
    import jax
    import jax.numpy as jnp
    def _L0_conv_ref(x, gn_gamma, gn_beta, in_proj_w, conv1d_w, conv1d_b, x_proj_w, dt_proj_w, dt_proj_b, A_log, Dskip, le_w, out_proj_w, proj_out_w):
        import jax, jax.numpy as jnp
        import numpy as np
        B, C, H, W = (4, 192, 64, 64)
        D_STATE, D_CONV, EXPAND = (16, 4, 2)
        DIN = EXPAND * C
        DT_RANK = (C + 15) // 16
        EPS = 1e-05

        def _silu(v):
            return v * jax.nn.sigmoid(v)

        def _snake(x2d):
            odd = (jnp.arange(x2d.shape[1]) % 2 == 1)[None, :, None, None]
            return jnp.where(odd, jnp.flip(x2d, axis=2), x2d)
        b, c, h, w = x.shape
        L = h * w
        din = DIN
        mu = jnp.mean(x, axis=(1, 2, 3), keepdims=True)
        var = jnp.var(x, axis=(1, 2, 3), keepdims=True)
        xn = (x - mu) * jax.lax.rsqrt(var + EPS)
        xn = xn * gn_gamma[None, :, None, None] + gn_beta[None, :, None, None]
        xs = xn.reshape(b, c, L).transpose(0, 2, 1)
        xz = jnp.einsum('blc,dc->bld', xs, in_proj_w)
        u, z = jnp.split(xz, 2, axis=-1)
        u = _snake(u.reshape(b, h, w, din)).reshape(b, L, din)
        u_t = u.transpose(0, 2, 1)
        u_c = jax.lax.conv_general_dilated(u_t, conv1d_w[:, None, :], (1,), [(D_CONV - 1, 0)], feature_group_count=din)
        u_c = _silu(u_c + conv1d_b[None, :, None]).transpose(0, 2, 1)
        dbl = jnp.einsum('bld,ed->ble', u_c, x_proj_w)
        dt, Bm, Cm = jnp.split(dbl, [DT_RANK, DT_RANK + D_STATE], axis=-1)
        delta = jax.nn.softplus(jnp.einsum('blr,dr->bld', dt, dt_proj_w) + dt_proj_b)
        A = -jnp.exp(A_log)

        def step(hc, inp):
            d_t, B_t, C_t, u_t_ = inp
            dA = jnp.exp(d_t[..., None] * A)
            hc = dA * hc + (d_t * u_t_)[..., None] * B_t[:, None, :]
            y_t = jnp.einsum('bdn,bn->bd', hc, C_t)
            return (hc, y_t)
        h0 = jnp.zeros((b, din, D_STATE), delta.dtype)
        xs_scan = (delta.transpose(1, 0, 2), Bm.transpose(1, 0, 2), Cm.transpose(1, 0, 2), u_c.transpose(1, 0, 2))
        _, ys = jax.lax.scan(step, h0, xs_scan)
        y = ys.transpose(1, 0, 2) + u_c * Dskip
        y = _snake(y.reshape(b, h, w, din)).reshape(b, L, din)
        y = y * _silu(z)
        y2d = y.reshape(b, h, w, din).transpose(0, 3, 1, 2)
        y_le = jax.lax.conv_general_dilated(y2d, le_w, (1, 1), [(1, 1), (1, 1)], feature_group_count=din)
        y = y + y_le.transpose(0, 2, 3, 1).reshape(b, L, din)
        out_seq = jnp.einsum('bld,cd->blc', y, out_proj_w)
        out = out_seq.transpose(0, 2, 1).reshape(b, c, h, w)
        out = jnp.einsum('bchw,oc->bohw', out, proj_out_w)
        return out

    def _L1_conv_ref(x, w_qkv, b_qkv, w_dw, b_dw, w_proj, b_proj, temperature):
        import jax, jax.numpy as jnp
        import numpy as np
        from jax import lax
        DIM = 192
        HEADS = 4
        EPS = 1e-12

        def _l2norm(t, axis):
            n = jnp.sqrt(jnp.sum(t * t, axis=axis, keepdims=True))
            return t / jnp.maximum(n, EPS)
        b, c, h, w = x.shape
        heads = temperature.shape[0]
        hd = c // heads
        qkv = jnp.einsum('bchw,oc->bohw', x, w_qkv) + b_qkv[None, :, None, None]
        qkv = lax.conv_general_dilated(qkv, w_dw, window_strides=(1, 1), padding=((1, 1), (1, 1)), dimension_numbers=('NCHW', 'OIHW', 'NCHW'), feature_group_count=3 * c) + b_dw[None, :, None, None]
        q, k, v = jnp.split(qkv, 3, axis=1)
        q = q.reshape(b, heads, hd, h * w)
        k = k.reshape(b, heads, hd, h * w)
        v = v.reshape(b, heads, hd, h * w)
        q = _l2norm(q, axis=2)
        k = _l2norm(k, axis=2)
        attn = jnp.einsum('bhdn,bhdm->bhnm', q, k) * temperature[None]
        attn = jax.nn.softmax(attn, axis=-1)
        out = jnp.einsum('bhnm,bhdm->bhdn', attn, v)
        out = out.reshape(b, c, h, w)
        out = jnp.einsum('bchw,oc->bohw', out, w_proj) + b_proj[None, :, None, None]
        return out

    def _gn(v, G=32, eps=1e-5):
        B_, C_, H_, W_ = v.shape
        g = v.reshape(B_, G, C_ // G, H_, W_)
        m = jnp.mean(g, axis=(2, 3, 4), keepdims=True)
        s = jnp.var(g, axis=(2, 3, 4), keepdims=True)
        return ((g - m) / jnp.sqrt(s + eps)).reshape(v.shape)

    def _ln_c(v, eps=1e-6):
        m = jnp.mean(v, axis=1, keepdims=True)
        s = jnp.var(v, axis=1, keepdims=True)
        return (v - m) / jnp.sqrt(s + eps)

    def _ln_t(v, eps=1e-5):
        m = jnp.mean(v, axis=-1, keepdims=True)
        s = jnp.var(v, axis=-1, keepdims=True)
        return (v - m) / jnp.sqrt(s + eps)

    def _to_tokens(v):
        B_, C_, H_, W_ = v.shape
        return v.reshape(B_, C_, H_ * W_).transpose(0, 2, 1)
    def _from_tokens(t, like):
        B_, C_, H_, W_ = like.shape
        return t.transpose(0, 2, 1).reshape(B_, C_, H_, W_)

    x = x + _L0_conv_ref(_gn(x), L0_conv_gn_gamma, L0_conv_gn_beta, L0_conv_in_proj_w, L0_conv_conv1d_w, L0_conv_conv1d_b, L0_conv_x_proj_w, L0_conv_dt_proj_w, L0_conv_dt_proj_b, L0_conv_A_log, L0_conv_Dskip, L0_conv_le_w, L0_conv_out_proj_w, L0_conv_proj_out_w)
    x = x + _L1_conv_ref(_gn(x), L1_conv_w_qkv, L1_conv_b_qkv, L1_conv_w_dw, L1_conv_b_dw, L1_conv_w_proj, L1_conv_b_proj, L1_conv_temperature)
    return x


_drawn_inputs = setup_inputs


def setup_inputs(seed=0):
    import zlib

    import numpy as np

    out = dict(_drawn_inputs(seed))
    spreads = {'L0_conv_gn_gamma': (1.0, 0.6),
     'L0_conv_gn_beta': (0.0, 0.8),
     'L0_conv_conv1d_b': (0.0, 0.557),
     'L0_conv_Dskip': (1.0, 0.6),
     'L1_conv_temperature': (1.0, 0.6)}
    factors = {'L0_conv_x_proj_w': 8.0,
     'L0_conv_dt_proj_w': 8.0,
     'L0_conv_dt_proj_b': 8.0,
     'L0_conv_A_log': 8.0,
     'L0_conv_le_w': 4.246,
     'L1_conv_w_qkv': 34.966,
     'L1_conv_b_qkv': 64.0,
     'L1_conv_w_dw': 34.381,
     'L1_conv_b_dw': 40.044,
     'L1_conv_w_proj': 3.781,
     'L1_conv_b_proj': 64.0}
    for name, (base, spread) in spreads.items():
        noise = np.random.default_rng([zlib.crc32(name.encode()), seed]).standard_normal(out[name].shape)
        drawn = base * np.exp(spread * noise) if base else spread * noise
        out[name] = jnp.asarray(drawn.astype(out[name].dtype))
    for name, factor in factors.items():
        out[name] = (out[name] * factor).astype(out[name].dtype)
    return out
```

```python
from contextlib import ExitStack

import concourse.bass as bass
import numpy as np
from concourse import mybir

F32 = mybir.dt.float32
F16 = mybir.dt.float16
ALU = mybir.AluOpType
ACT = mybir.ActivationFunctionType
ds = bass.ds

C = 192
H = W = 64
L = H * W
CB = 96
NCB = C // CB
DIN = 2 * C
DB = DIN // 128
NST = 16
DTR = 12
GROUP = C // 32
HEADS = 4
HD = C // HEADS
BANK = 512
NCH = L // BANK
ROWS = BANK // W
TC = 1024
NTC = L // TC
KT = L // 128
PADW = W + 2
QSCALE = 64.0
VROW = 64
SHIFT_FREE = 60.0


class Count:

    def __init__(self, sem):
        self.sem, self.n = sem, 0

    def on(self, ins, by=1):
        ins.then_inc(self.sem, by)
        self.n += by
        return self.n


def end_phase(nc, sems):
    for s in sems:
        nc.sync.sem_clear(s)
    nc.all_engine_barrier()


class Phase:

    def __init__(self, nc, name):
        self.nc, self.name, self.ctx, self.sems = nc, f"{name}{nc.next_id()}", ExitStack(), []

    def __enter__(self):
        self.ctx.__enter__()
        return self

    def __exit__(self, *e):
        if e[0] is None:
            end_phase(self.nc, self.sems)
        return self.ctx.__exit__(*e)

    def sb(self, name, shape, dt=F32):
        return self.ctx.enter_context(self.nc.sbuf_tensor(f"{self.name}_{name}", shape, dt))

    def ps(self, name, shape):
        return self.ctx.enter_context(self.nc.psum_tensor(f"{self.name}_ps_{name}", shape, F32))

    def sem(self, name):
        s = self.ctx.enter_context(self.nc.semaphore(f"{self.name}_{name}"))
        self.sems.append(s)
        return s


def setup(nc, io, keep):
    with Phase(nc, "setup") as ph:
        op_w = ph.sb("out_proj", [CB, NCB, DIN])
        po_w = ph.sb("proj_out", [CB, NCB, C])
        temp = ph.sb("temp", [128, HEADS])
        tabs = ph.sb("tabs", [128, HEADS])
        comb_ps = ph.ps("comb", [128, DB, BANK])
        loaded, combined, a_exp, tmp = ph.sem("loaded"), ph.sem("combined"), ph.sem("a_exp"), ph.sem("tmp")
        loads = [
            (keep["ident"][:, :], io["ident"]),
            (keep["group_mean"][:, :], io["group_mean"]),
            (keep["all_mean"][:, :], io["all_mean"]),
            (keep["head_sum"][:, :], io["head_sum"]),
            (keep["x_proj"][:, :, :], io["x_proj_t"]),
            (keep["dt_proj"][:, :, :], io["dt_proj_t"]),
            (keep["w_proj"][:, :, :], io["w_proj_t"]),
            (keep["chan"][:, :, :], io["chan"]),
            (keep["inner"][:, :, :], io["inner"]),
            (keep["le"][:, :, :], io["le"]),
            (keep["a"][:, :, :], io["a_log"]),
            (keep["dw"][:, :, :], io["dw"]),
            (op_w[:, :, :], io["out_proj"]),
            (po_w[:, :, :], io["proj_out_t"]),
            (temp[:, :], io["temperature"].partition_broadcast(128)),
        ]
        with nc.Block() as block:

            @block.sync
            def _(sp):
                for dst, src in loads:
                    sp.dma_start(dst, src).then_inc(loaded, 16)

            @block.tensor
            def _(pe):
                pe.wait_ge(loaded, 16 * len(loads))
                for m in range(DB):
                    for k in range(NCB):
                        mm = pe.matmul(comb_ps[:, m, 0:C], op_w[:, k, m * 128:(m + 1) * 128], po_w[:, k, :],
                                       start=(k == 0), stop=(k == NCB - 1))
                mm.then_inc(combined, 1)

            @block.scalar
            def _(act):
                act.wait_ge(loaded, 16 * len(loads))
                act.activation(keep["a"][:, :, :], keep["a"][:, :, :], ACT.Exp).then_inc(a_exp, 1)

            @block.vector
            def _(dve):
                dve.wait_ge(loaded, 16 * len(loads))
                dve.tensor_scalar(keep["le"][:, :, 4:5], keep["le"][:, :, 4:5], 1.0, None, ALU.add)
                dve.tensor_scalar(keep["temp"][:, 0, :], temp[:, :], 1.0 / QSCALE ** 2, None, ALU.mult)
                dve.tensor_scalar(tabs[:, :], temp[:, :], -1.0, None, ALU.mult).then_inc(tmp, 1)
                dve.wait_ge(tmp, 1)
                dve.tensor_tensor(tabs[:, :], tabs[:, :], temp[:, :], ALU.max).then_inc(tmp, 1)
                dve.wait_ge(tmp, 2)
                dve.tensor_scalar(tabs[:, :], tabs[:, :], -1.0, SHIFT_FREE, ALU.mult, ALU.add).then_inc(tmp, 1)
                dve.wait_ge(tmp, 3)
                dve.tensor_scalar(keep["temp"][:, 1, :], tabs[:, :], 0.0, None, ALU.min)
                dve.wait_ge(a_exp, 1)
                dve.tensor_scalar(keep["a"][:, :, :], keep["a"][:, :, :], -1.0, None, ALU.mult)
                dve.wait_ge(combined, 1)
                dve.tensor_copy(keep["w_out"][:, :, :], comb_ps[:, :, 0:C])


class GroupNorm:

    EPS = 1e-5

    def __init__(self, ph, keep, x, ps, whole):
        self.keep, self.x, self.ps, self.whole = keep, x, ps, whole
        self.chunk_stats = ph.sb("chunk_stats", [CB, NCB, NCH, 6])
        self.mv = ph.sb("mean_var", [CB, NCB, 2])
        self.chan = ph.sb("chan_stats", [CB, 2, NCB])
        self.grp = ph.sb("group_stats", [CB, 2, NCB])
        self.tmp = ph.sb("stats_tmp", [CB, NCB])
        self.std = ph.sb("std", [CB, NCB])
        self.scale = ph.sb("gn_scale", [CB, NCB])
        self.shift = ph.sb("gn_shift", [CB, NCB])
        self.tot = ph.sb("total", [CB, 2])
        self.rows = ph.sem("chan_stats_ready")
        self.means = ph.sem("means_ready")
        self.var = ph.sem("var_ready")
        self.root = ph.sem("root_ready")
        self.step = ph.sem("stats_step")

    def tensor(self, pe):
        pe.wait_ge(self.rows, 1)
        pe.matmul(self.ps[0:CB, 0:2 * NCB], self.keep["group_mean"][:, :],
                  self.chan[:, :, :].rearrange("p a b -> p (a b)"), start=True, stop=True).then_inc(self.means, 1)
        if self.whole:
            pe.wait_ge(self.rows, 2)
            for k in range(NCB):
                mm = pe.matmul(self.ps[0:CB, 0:2], self.keep["all_mean"][:, :], self.chan[:, :, k],
                               start=(k == 0), stop=(k == NCB - 1))
            mm.then_inc(self.means, 1)

    def scalar(self, act):
        act.wait_ge(self.var, 1)
        act.activation(self.std[:, :], self.tmp[:, :], ACT.Sqrt).then_inc(self.root, 1)
        if self.whole:
            act.wait_ge(self.var, 2)
            act.activation(self.std[:, 0:1], self.tmp[:, 0:1], ACT.Sqrt).then_inc(self.root, 1)

    def vector(self, dve):
        step = Count(self.step)

        def then(ins):
            dve.wait_ge(self.step, step.on(ins))

        for k in range(NCB):
            for c in range(NCH):
                ins = dve.bn_stats(self.chunk_stats[:, k, c, :], self.x[:, k, c * BANK:(c + 1) * BANK])
        then(ins)
        for k in range(NCB):
            ins = dve.bn_aggr(self.mv[:, k, :], self.chunk_stats[:, k, :, :].rearrange("p c s -> p (c s)"))
        then(ins)
        mean, var = self.mv[:, :, 0], self.mv[:, :, 1]
        step.on(dve.tensor_copy(self.chan[:, 0, :], mean))
        then(dve.tensor_tensor(self.tmp[:, :], mean, mean, ALU.mult))
        dve.tensor_tensor(self.chan[:, 1, :], self.tmp[:, :], var, ALU.add).then_inc(self.rows, 1)
        dve.wait_ge(self.rows, 1)
        dve.wait_ge(self.means, 1)
        then(dve.tensor_copy(self.grp[:, :, :], self.ps[0:CB, 0:2 * NCB].rearrange("p (a b) -> p a b", a=2)))
        gm, gsq = self.grp[:, 0, :], self.grp[:, 1, :]
        then(dve.tensor_tensor(self.std[:, :], gm, gm, ALU.mult))
        dve.scalar_tensor_tensor(self.tmp[:, :], gsq, self.EPS, self.std[:, :], ALU.add, ALU.subtract).then_inc(self.var, 1)
        dve.wait_ge(self.var, 1)
        dve.wait_ge(self.root, 1)
        then(dve.reciprocal(self.scale[:, :], self.std[:, :]))
        then(dve.scalar_tensor_tensor(self.shift[:, :], gm, -1.0, self.scale[:, :], ALU.mult, ALU.mult))
        if not self.whole:
            return
        then(dve.tensor_tensor(self.tmp[:, :], mean, self.scale[:, :], ALU.mult))
        then(dve.tensor_tensor(self.chan[:, 0, :], self.tmp[:, :], self.shift[:, :], ALU.add))
        then(dve.tensor_tensor(self.tmp[:, :], self.chan[:, 0, :], self.chan[:, 0, :], ALU.mult))
        then(dve.tensor_tensor(self.chan[:, 1, :], self.scale[:, :], self.scale[:, :], ALU.mult))
        then(dve.tensor_tensor(self.chan[:, 1, :], self.chan[:, 1, :], var, ALU.mult))
        dve.tensor_tensor(self.chan[:, 1, :], self.chan[:, 1, :], self.tmp[:, :], ALU.add).then_inc(self.rows, 1)
        dve.wait_ge(self.rows, 2)
        dve.wait_ge(self.means, 2)
        then(dve.tensor_copy(self.tot[:, :], self.ps[0:CB, 0:2]))
        then(dve.tensor_tensor(self.std[:, 0:1], self.tot[:, 0:1], self.tot[:, 0:1], ALU.mult))
        dve.scalar_tensor_tensor(self.tmp[:, 0:1], self.tot[:, 1:2], self.EPS, self.std[:, 0:1],
                                 ALU.add, ALU.subtract).then_inc(self.var, 1)
        dve.wait_ge(self.var, 2)
        dve.wait_ge(self.root, 2)
        then(dve.reciprocal(self.std[:, 1:2], self.std[:, 0:1]))
        gamma, beta = self.keep["chan"][:, 0, :], self.keep["chan"][:, 1, :]
        r = self.std[:, 1:2]
        then(dve.scalar_tensor_tensor(self.scale[:, :], self.scale[:, :], r, gamma, ALU.mult, ALU.mult))
        then(dve.tensor_scalar(self.shift[:, :], self.shift[:, :], self.tot[:, 0:1], r, ALU.subtract, ALU.mult))
        then(dve.tensor_tensor(self.shift[:, :], self.shift[:, :], gamma, ALU.mult))
        then(dve.tensor_tensor(self.shift[:, :], self.shift[:, :], beta, ALU.add))


def layer0_project(nc, io, keep, dram, b):
    with Phase(nc, "l0pre") as ph:
        x = ph.sb("x", [CB, NCB, L])
        w_in = ph.sb("in_proj", [CB, NCB, 2 * DIN])
        u_raw = ph.sb("u_raw", [128, 2, L + 3])
        u_c = ph.sb("u_conv", [128, DB, L])
        z_s = ph.sb("z_silu", [128, 2, L])
        dbl = ph.sb("dbl", [DTR + 2 * NST, L])
        ps = ph.ps("ps", [128, 8, BANK])
        gn = GroupNorm(ph, keep, x, ps[:, 0, :], True)
        x_in, x_norm = ph.sem("x_in"), ph.sem("x_norm")
        tile_done, tile_read = ph.sem("tile_done"), ph.sem("tile_read")
        pads, conv, u_ready = ph.sem("pads"), ph.sem("conv"), ph.sem("u_ready")
        z_stored = [ph.sem("z_stored0"), ph.sem("z_stored1")]
        xp_done, dbl_ready = ph.sem("x_proj_done"), ph.sem("dbl_ready")
        dt_done, dt_read, dt_abs = ph.sem("dt_done"), ph.sem("dt_read"), ph.sem("dt_abs")
        e_ready, w_ready, ln_ready = ph.sem("e_ready"), ph.sem("w_ready"), ph.sem("ln_ready")
        res, half_ready, delta_ready = ph.sem("res"), ph.sem("half_ready"), ph.sem("delta_ready")
        delta_stored = [ph.sem("delta_stored0"), ph.sem("delta_stored1")]
        other_stored = ph.sem("other_stored")
        NT = 2 * DB * NCH
        HALF = L // 2
        NQ = 2 * DB
        views = [
            [u_raw[:, i // 2, (i % 2) * HALF:(i % 2 + 1) * HALF] for i in range(4)],
            [z_s[:, i // 2, (i % 2) * HALF:(i % 2 + 1) * HALF] for i in range(4)],
        ]
        conv_b, dt_b = keep["inner"][:, 0, :], keep["inner"][:, 1, :]
        conv_w = keep["inner"][:, 3:7, :]

        with nc.Block() as block:

            @block.sync
            def _(sp):
                sp.dma_start(x[:, :, :], io["x"][ds(b, 1)].rearrange("a (k p) l -> p (a k) l", p=CB)).then_inc(x_in, 16)
                sp.dma_start(w_in[:, :, :], io["in_proj_t"]).then_inc(x_in, 16)
                for m in range(DB):
                    sp.wait_ge(u_ready, m + 1)
                    sp.dma_start(dram["u"][m], u_c[:, m, :]).then_inc(other_stored, 16)
                for m in range(DB):
                    sp.wait_ge(tile_read, NCH * (DB + m + 1))
                    sp.dma_start(dram["z"][m], z_s[:, m % 2, :]).then_inc(z_stored[m % 2], 16)
                sp.wait_ge(dbl_ready, NCH)
                sp.dma_start(dram["bc"], dbl[DTR:, :]).then_inc(other_stored, 16)
                for q in range(NQ):
                    sp.wait_ge(delta_ready, q + 1)
                    sp.dma_start(dram["delta"][q // 2][:, (q % 2) * HALF:(q % 2 + 1) * HALF],
                                 views[q % 2][2]).then_inc(delta_stored[q % 2], 16)
                sp.wait_ge(other_stored, 16 * (DB + 1))
                sp.wait_ge(z_stored[0], 32)
                sp.wait_ge(z_stored[1], 16)
                for s in delta_stored:
                    sp.wait_ge(s, 16 * NQ // 2)

            @block.tensor
            def _(pe):
                pe.wait_ge(x_in, 32)
                gn.tensor(pe)
                pe.wait_ge(x_norm, NCB)
                for t in range(NT):
                    m, c = divmod(t, NCH)
                    if t >= 8:
                        pe.wait_ge(tile_read, t - 7)
                    for k in range(NCB):
                        mm = pe.matmul(ps[:, t % 8, :], w_in[:, k, m * 128:(m + 1) * 128],
                                       x[:, k, c * BANK:(c + 1) * BANK], start=(k == 0), stop=(k == NCB - 1))
                    mm.then_inc(tile_done, 1)
                pe.wait_ge(u_ready, DB)
                for c in range(NCH):
                    pe.wait_ge(tile_read, NT - 7 + c)
                    for k in range(DB):
                        mm = pe.matmul(ps[0:DTR + 2 * NST, c, :], keep["x_proj"][:, k, :],
                                       u_c[:, k, c * BANK:(c + 1) * BANK], start=(k == 0), stop=(k == DB - 1))
                    mm.then_inc(xp_done, 1)
                pe.wait_ge(dbl_ready, NCH)
                for q in range(NQ):
                    m, half = divmod(q, 2)
                    if q >= 2:
                        pe.wait_ge(dt_read, q - 1)
                    for c in range(4):
                        col = half * HALF + c * BANK
                        mm = pe.matmul(ps[:, 4 * (q % 2) + c, :], keep["dt_proj"][:, m, :],
                                       dbl[0:DTR, col:col + BANK], start=True, stop=True)
                    mm.then_inc(dt_done, 1)

            @block.scalar
            def _(act):
                gn.scalar(act)

                def unload_u(m):
                    if m == 0:
                        act.wait_ge(pads, 1)
                    if m >= 2:
                        act.wait_ge(conv, m - 1)
                    for c in range(NCH):
                        t = m * NCH + c
                        act.wait_ge(tile_done, t + 1)
                        src = ps[:, t % 8, :].rearrange("p (r two w) -> p r two w", two=2, w=W)
                        dst = u_raw[:, m % 2, 3 + c * BANK:3 + (c + 1) * BANK].rearrange(
                            "p (r two w) -> p r two w", two=2, w=W)
                        act.activation(dst[:, :, 0, :], src[:, :, 0, :], ACT.Copy)
                        act.activation(dst[:, :, 1, :], src[:, :, 1, ::-1], ACT.Copy).then_inc(tile_read, 1)

                def silu_u(m):
                    act.wait_ge(conv, m + 1)
                    act.activation(u_c[:, m, :], u_c[:, m, :], ACT.Silu, bias=conv_b[:, m:m + 1]).then_inc(u_ready, 1)

                def silu_z(m):
                    if m >= 2:
                        act.wait_ge(z_stored[m % 2], 16)
                    for c in range(NCH):
                        t = (DB + m) * NCH + c
                        act.wait_ge(tile_done, t + 1)
                        act.activation(z_s[:, m % 2, c * BANK:(c + 1) * BANK], ps[:, t % 8, :],
                                       ACT.Silu).then_inc(tile_read, 1)

                unload_u(0)
                unload_u(1)
                silu_u(0)
                unload_u(2)
                silu_u(1)
                for m in range(DB):
                    silu_z(m)
                    if m == 0:
                        silu_u(2)

                def softplus_front(q):
                    m, buf = q // 2, views[q % 2]
                    v = ps[:, 4 * (q % 2):4 * (q % 2) + 4, :].rearrange("p a b -> p (a b)")
                    act.wait_ge(dt_done, q + 1)
                    if q >= 2:
                        act.wait_ge(delta_ready, q - 1)
                    elif q == 1:
                        act.wait_ge(z_stored[0], 32)
                        act.wait_ge(z_stored[1], 16)
                    act.activation(buf[0], v, ACT.Abs, bias=dt_b[:, m:m + 1]).then_inc(dt_abs, 1)
                    act.activation(buf[3], v, ACT.Relu, bias=dt_b[:, m:m + 1]).then_inc(dt_read, 1)
                    act.wait_ge(dt_abs, q + 1)
                    act.activation(buf[0], buf[0], ACT.Exp, scale=-1.0).then_inc(e_ready, 1)

                def softplus_ln(q):
                    buf = views[q % 2]
                    act.wait_ge(w_ready, q + 1)
                    if q >= 2:
                        act.wait_ge(delta_stored[q % 2], 16 * (q // 2))
                    act.activation(buf[2], buf[1], ACT.Ln).then_inc(ln_ready, 1)

                for q in range(NQ + 1):
                    if q < NQ:
                        softplus_front(q)
                    if q >= 1:
                        softplus_ln(q - 1)

            @block.vector
            def _(dve):
                dve.memset(u_raw[:, :, 0:3], 0.0).then_inc(pads, 1)
                dve.wait_ge(x_in, 32)
                gn.vector(dve)
                for k in range(NCB):
                    dve.tensor_scalar(x[:, k, :], x[:, k, :], gn.scale[:, k:k + 1], gn.shift[:, k:k + 1],
                                      ALU.mult, ALU.add).then_inc(x_norm, 1)
                tap = Count(res)
                for m in range(DB):
                    dve.wait_ge(tile_read, NCH * (m + 1))
                    dve.wait_ge(res, tap.on(dve.tensor_scalar(
                        u_c[:, m, :], u_raw[:, m % 2, 0:L], conv_w[:, 0, m:m + 1], None, ALU.mult)))
                    for k in range(1, 4):
                        ins = dve.scalar_tensor_tensor(u_c[:, m, :], u_raw[:, m % 2, k:k + L],
                                                       conv_w[:, k, m:m + 1], u_c[:, m, :], ALU.mult, ALU.add)
                        if k < 3:
                            dve.wait_ge(res, tap.on(ins))
                    ins.then_inc(conv, 1)
                for c in range(NCH):
                    dve.wait_ge(xp_done, c + 1)
                    dve.tensor_copy(dbl[:, c * BANK:(c + 1) * BANK], ps[0:DTR + 2 * NST, c, :]).then_inc(dbl_ready, 1)

                def add_one(q):
                    buf = views[q % 2]
                    dve.wait_ge(e_ready, q + 1)
                    dve.tensor_scalar(buf[1], buf[0], 1.0, None, ALU.add).then_inc(w_ready, 1)

                def finish(q):
                    buf = views[q % 2]
                    dve.wait_ge(w_ready, q + 1)
                    dve.scalar_tensor_tensor(buf[0], buf[1], -1.0, buf[0], ALU.add, ALU.subtract).then_inc(res, 1)
                    tap.n += 1
                    dve.wait_ge(res, tap.n)
                    dve.wait_ge(ln_ready, q + 1)
                    dve.tensor_tensor(buf[2], buf[2], buf[0], ALU.subtract).then_inc(half_ready, 1)
                    dve.wait_ge(half_ready, q + 1)
                    dve.tensor_tensor(buf[2], buf[2], buf[3], ALU.add).then_inc(delta_ready, 1)

                for q in range(NQ + 1):
                    if q < NQ:
                        add_one(q)
                    if q >= 1:
                        finish(q - 1)


def scan_and_attend(nc, keep, dram, hc, scan, attend):
    with Phase(nc, "mix") as ph:
        s_in, s_out = ph.sem("scan_in"), ph.sem("y_stored")
        bc_in = [ph.sem(f"bc_in{i}") for i in range(3)]
        du_done, y_init, da_ready = ph.sem("du_done"), ph.sem("y_init"), ph.sem("da_ready")
        dbu_ready, h_ready, hc_ready = ph.sem("dbu_ready"), ph.sem("h_ready"), ph.sem("hc_ready")
        y_done, carried = ph.sem("y_done"), ph.sem("carried")
        a_in, t_ready = ph.sem("attn_in"), ph.sem("temp_ready")
        s_ready, p_ready, pv_done = ph.sem("s_ready"), ph.sem("p_ready"), ph.sem("pv_done")
        o_ready = ph.sem("o_ready")
        o_stored = [ph.sem("o_stored0"), ph.sem("o_stored1")]
        NS = NST * DB
        NG = NTC * KT
        if scan:
            delta = ph.sb("delta", [128, DB, TC])
            u = ph.sb("u", [128, DB, TC])
            du = ph.sb("du", [128, DB, TC])
            y = ph.sb("y", [128, DB, TC])
            bc = ph.sb("bc", [128, 3, 2, TC])
            da = ph.sb("da", [128, 3, TC])
            dbu = ph.sb("dbu", [128, 3, TC])
            hs = ph.sb("h", [128, 3, TC])
            hcs = ph.sb("h_c", [128, 3, TC])
        if attend:
            k_t = ph.sb("k", [2 * HD, L], F16)
            q_t = ph.sb("q", [2 * HD, 2, L], F16)
            v_t = ph.sb("v", [128, KT, VROW])
            p_t = ph.sb("p", [128, 4, TC])
            o_t = ph.sb("o", [VROW + HD + 1, 2, BANK])
            tcur = ph.sb("temp", [128, 2])
            s_ps = ph.ps("s", [128, 3, TC])
            o_ps = ph.ps("o", [128, 2, BANK])
        token = lambda t: t.rearrange("m p l -> p m l")[:, :, ds(hc * TC, TC)]

        def load_bc(sp, n):
            if n >= 3:
                sp.wait_ge(hc_ready, (n - 2) * DB)
            for i in range(2):
                src = dram["bc"][i * NST + n:i * NST + n + 1, ds(hc * TC, TC)]
                sp.dma_start(bc[:, n % 3, i, :], src.partition_broadcast(128).rearrange("p a l -> p (a l)")
                             ).then_inc(bc_in[n % 3], 16)

        def store_o(sp, c):
            sp.wait_ge(o_ready, c + 1)
            for i in range(2):
                col = c * TC + i * BANK
                sp.dma_start(dram["o"][ds(hc * HD, HD), col:col + BANK],
                             o_t[i * VROW:i * VROW + HD, c % 2, :]).then_inc(o_stored[c % 2], 16)
                sp.dma_start(dram["den"][ds(hc, 1), col:col + BANK],
                             o_t[i * VROW + HD:i * VROW + HD + 1, c % 2, :]).then_inc(o_stored[c % 2], 16)

        with nc.Block() as block:

            @block.sync
            def _(sp):
                if attend:
                    for half in range(2):
                        rows = slice(half * HD, (half + 1) * HD)
                        sp.dma_start(k_t[rows, :], dram["k"][half, ds(hc * HD, HD), :]).then_inc(a_in, 16)
                        for part in range(2):
                            sp.dma_start(q_t[rows, part, :], dram["q"][part, ds(hc * HD, HD), :]).then_inc(a_in, 16)
                    sp.dma_start(v_t[:, :, 0:HD],
                                 dram["v"][ds(hc, 1)].rearrange("a p t c -> p (a t) c")).then_inc(a_in, 16)
                if scan:
                    sp.dma_start(delta[:, :, :], token(dram["delta"])).then_inc(s_in, 16)
                    sp.dma_start(u[:, :, :], token(dram["u"])).then_inc(s_in, 16)
                    load_bc(sp, 0)
                    load_bc(sp, 1)
                for c in range(NTC):
                    if scan:
                        for n in range(2 + 4 * c, min(6 + 4 * c, NST)):
                            load_bc(sp, n)
                    if attend:
                        store_o(sp, c)
                if scan:
                    sp.wait_ge(y_done, NS)
                    sp.dma_start(token(dram["y"]), y[:, :, :]).then_inc(s_out, 16)
                    sp.wait_ge(s_out, 16)
                if attend:
                    for s in o_stored:
                        sp.wait_ge(s, 64 * NTC // 2)

            @block.tensor
            def _(pe):
                if not attend:
                    return
                pe.wait_ge(a_in, 16 * 7)
                pe.wait_ge(t_ready, 2)

                def scores(g):
                    c, t = divmod(g, KT)
                    if g >= 3:
                        pe.wait_ge(p_ready, g - 2)
                    for i in range(2):
                        for part in range(2):
                            col = c * TC + i * BANK
                            mm = pe.matmul(s_ps[:, g % 3, i * BANK:(i + 1) * BANK], k_t[:, t * 128:(t + 1) * 128],
                                           q_t[:, part, col:col + BANK], start=(part == 0), stop=(part == 1))
                    mm.then_inc(s_ready, 1)

                def weigh(g):
                    c, t = divmod(g, KT)
                    pe.wait_ge(p_ready, g + 1)
                    if t == 0 and c >= 2:
                        pe.wait_ge(o_ready, c - 1)
                    for i in range(2):
                        mm = pe.matmul(o_ps[i * VROW:(i + 1) * VROW, c % 2, :], v_t[:, t, :],
                                       p_t[:, g % 4, i * BANK:(i + 1) * BANK], start=(t == 0), stop=(t == KT - 1))
                    mm.then_inc(pv_done, 1)

                for g in range(NG + 2):
                    if g < NG:
                        scores(g)
                    if g >= 2:
                        weigh(g - 2)

            @block.scalar
            def _(act):
                def decay(s):
                    n, m = divmod(s, DB)
                    if s >= 3:
                        act.wait_ge(h_ready, s - 2)
                    act.activation(da[:, s % 3, :], delta[:, m, :], ACT.Exp,
                                   scale=keep["a"][:, m, n:n + 1]).then_inc(da_ready, 1)

                def probs(g):
                    act.wait_ge(s_ready, g + 1)
                    if g >= 4:
                        act.wait_ge(pv_done, g - 3)
                    act.activation(p_t[:, g % 4, :], s_ps[:, g % 3, :], ACT.Exp, bias=tcur[:, 1:2],
                                   scale=tcur[:, 0:1]).then_inc(p_ready, 1)

                if attend:
                    act.activation(tcur[:, :], keep["temp"][:, :, ds(hc, 1)].rearrange("p a b -> p (a b)"),
                                   ACT.Copy).then_inc(t_ready, 1)
                    act.wait_ge(t_ready, 2)
                if scan:
                    act.wait_ge(s_in, 32)
                if not attend:
                    for s in range(NS):
                        decay(s)
                else:
                    s = 0
                    for g in range(NG):
                        if scan and s * NG <= g * NS:
                            decay(s)
                            s += 1
                        probs(g)

            @block.gpsimd
            def _(pool):
                if attend:
                    pool.memset(v_t[:, :, HD + 1:], 0.0)
                    pool.memset(v_t[:, :, HD:HD + 1], 1.0).then_inc(t_ready, 1)
                if not scan:
                    return
                for s in range(NS):
                    n, m = divmod(s, DB)
                    pool.wait_ge(h_ready, s + 1)
                    pool.tensor_copy(keep["carry"][:, s:s + 1], hs[:, s % 3, TC - 1:TC]).then_inc(carried, 1)
                    pool.wait_ge(hc_ready, s + 1)
                    if s < DB:
                        pool.wait_ge(y_init, m + 1)
                    else:
                        pool.wait_ge(y_done, s - DB + 1)
                    pool.tensor_tensor(y[:, m, :], y[:, m, :], hcs[:, s % 3, :], ALU.add).then_inc(y_done, 1)

            @block.vector
            def _(dve):
                def read_o(c):
                    dve.wait_ge(pv_done, KT * (c + 1))
                    if c >= 2:
                        dve.wait_ge(o_stored[c % 2], 64 * (c // 2))
                    dve.tensor_copy(o_t[:, c % 2, :], o_ps[0:VROW + HD + 1, c % 2, :]).then_inc(o_ready, 1)

                if not scan:
                    for c in range(NTC):
                        read_o(c)
                    return
                dve.wait_ge(s_in, 32)
                for m in range(DB):
                    dve.tensor_tensor(du[:, m, :], delta[:, m, :], u[:, m, :], ALU.mult).then_inc(du_done, 1)
                    dve.tensor_scalar(y[:, m, :], u[:, m, :], keep["inner"][:, 2, m:m + 1], None,
                                      ALU.mult).then_inc(y_init, 1)

                def inflow(s):
                    n, m = divmod(s, DB)
                    dve.wait_ge(bc_in[n % 3], 32 * (n // 3 + 1))
                    if s < DB:
                        dve.wait_ge(du_done, m + 1)
                    if s >= 3:
                        dve.wait_ge(h_ready, s - 2)
                    dve.tensor_tensor(dbu[:, s % 3, :], du[:, m, :], bc[:, n % 3, 0, :], ALU.mult).then_inc(dbu_ready, 1)

                def recur(s):
                    dve.wait_ge(da_ready, s + 1)
                    dve.wait_ge(dbu_ready, s + 1)
                    if s >= 3:
                        dve.wait_ge(hc_ready, s - 2)
                        dve.wait_ge(carried, s - 2)
                    dve.tensor_tensor_scan(hs[:, s % 3, :], da[:, s % 3, :], dbu[:, s % 3, :],
                                           keep["carry"][:, s:s + 1], ALU.mult, ALU.add).then_inc(h_ready, 1)

                def outflow(s):
                    n = s // DB
                    dve.wait_ge(h_ready, s + 1)
                    if s >= 3:
                        dve.wait_ge(y_done, s - 2)
                    dve.tensor_tensor(hcs[:, s % 3, :], hs[:, s % 3, :], bc[:, n % 3, 1, :], ALU.mult).then_inc(hc_ready, 1)

                for s in range(-1, NS + 1):
                    if s + 1 < NS:
                        inflow(s + 1)
                    if 0 <= s < NS:
                        recur(s)
                    if s >= 1:
                        outflow(s - 1)
                        if attend and s % (NS // NTC) == 0:
                            read_o(s // (NS // NTC) - 1)


def clear_carry(nc, keep):
    with nc.Block() as block:

        @block.vector
        def _(dve):
            dve.memset(keep["carry"][:, :], 0.0)


def layer0_finish(nc, io, keep, dram, b):
    with Phase(nc, "l0post") as ph:
        x = ph.sb("x", [CB, NCB, L])
        y_in = ph.sb("y_in", [128, L])
        z_in = ph.sb("z_in", [128, L])
        pad = ph.sb("pad", [128, 2, PADW, PADW])
        acc = ph.sb("acc", [128, DB, H, W])
        ps = ph.ps("ps", [128, 8, BANK])
        x_in, yz_in, border = ph.sem("x_in"), ph.sem("yz_in"), ph.sem("border")
        gated, tap, conv = ph.sem("gated"), ph.sem("tap"), ph.sem("conv")
        tile_done, x1_ready, stored = ph.sem("tile_done"), ph.sem("x1_ready"), ph.sem("stored")

        with nc.Block() as block:

            @block.sync
            def _(sp):
                for m in range(DB):
                    if m >= 1:
                        sp.wait_ge(gated, 2 * m)
                    sp.dma_start(y_in[:, :], dram["y"][m]).then_inc(yz_in, 16)
                    sp.dma_start(z_in[:, :], dram["z"][m]).then_inc(yz_in, 16)
                    if m == 0:
                        sp.dma_start(x[:, :, :], io["x"][ds(b, 1)].rearrange("a (k p) l -> p (a k) l", p=CB)
                                     ).then_inc(x_in, 16)
                for k in range(NCB):
                    sp.wait_ge(x1_ready, NCH * (k + 1))
                    sp.dma_start(dram["x1"][k], x[:, k, :]).then_inc(stored, 16)
                sp.wait_ge(stored, 16 * NCB)

            @block.gpsimd
            def _(pool):
                for i in range(2):
                    pool.memset(pad[:, i, :, :], 0.0).then_inc(border, 1)

            @block.tensor
            def _(pe):
                pe.wait_ge(conv, DB)
                for t in range(NCB * NCH):
                    mo, c = divmod(t, NCH)
                    if t >= 8:
                        pe.wait_ge(x1_ready, t - 7)
                    for k in range(DB):
                        rhs = acc[:, k, c * ROWS:(c + 1) * ROWS, :].rearrange("p r w -> p (r w)")
                        mm = pe.matmul(ps[0:CB, t % 8, :], keep["w_out"][:, k, mo * CB:(mo + 1) * CB], rhs,
                                       start=(k == 0), stop=(k == DB - 1))
                    mm.then_inc(tile_done, 1)

            @block.vector
            def _(dve):
                taps = Count(tap)
                dve.wait_ge(border, 2)
                for m in range(DB):
                    inner = pad[:, m % 2, 1:H + 1, 1:W + 1].rearrange("p (r two) w -> p r two w", two=2)
                    yv = y_in[:, :].rearrange("p (r two w) -> p r two w", two=2, w=W)
                    zv = z_in[:, :].rearrange("p (r two w) -> p r two w", two=2, w=W)
                    dve.wait_ge(yz_in, 32 * (m + 1))
                    dve.tensor_tensor(inner[:, :, 0, :], yv[:, :, 0, :], zv[:, :, 0, :], ALU.mult).then_inc(gated, 1)
                    dve.tensor_tensor(inner[:, :, 1, :], yv[:, :, 1, ::-1], zv[:, :, 1, :], ALU.mult).then_inc(gated, 1)
                    dve.wait_ge(gated, 2 * (m + 1))
                    for k in range(9):
                        src = pad[:, m % 2, k // 3:k // 3 + H, k % 3:k % 3 + W]
                        w = keep["le"][:, m, k:k + 1]
                        if k == 0:
                            ins = dve.tensor_scalar(acc[:, m, :, :], src, w, None, ALU.mult)
                        else:
                            ins = dve.scalar_tensor_tensor(acc[:, m, :, :], src, w, acc[:, m, :, :], ALU.mult, ALU.add)
                        if k < 8:
                            dve.wait_ge(tap, taps.on(ins))
                    ins.then_inc(conv, 1)
                    if m == 0:
                        dve.wait_ge(conv, 1)
                dve.wait_ge(x_in, 16)
                for t in range(NCB * NCH):
                    mo, c = divmod(t, NCH)
                    dve.wait_ge(tile_done, t + 1)
                    xs = x[:, mo, c * BANK:(c + 1) * BANK]
                    dve.tensor_tensor(xs, ps[0:CB, t % 8, :], xs, ALU.add).then_inc(x1_ready, 1)


def layer1_project(nc, io, keep, dram):
    with Phase(nc, "l1pre") as ph:
        x = ph.sb("x", [CB, NCB, L])
        w_qkv = ph.sb("w_qkv", [CB, NCB, 3 * C])
        pad = ph.sb("pad", [CB, 2, PADW, PADW])
        qk = ph.sb("qk", [CB, 4, L])
        sq = ph.sb("sq", [CB, L])
        vt = ph.sb("vt", [128, 2, KT, HD])
        hi = ph.sb("hi", [CB, L], F16)
        lo = ph.sb("lo", [CB, L], F16)
        length = ph.sb("length", [128, 8 * KT])
        inv = ph.sb("inv", [128, 8 * KT])
        inv_t = ph.sb("inv_t", [128, 2, 128])
        ps = ph.ps("ps", [128, 6, BANK])
        ss_ps = ph.ps("ss", [128, BANK])
        it_ps = ph.ps("it", [128, BANK])
        gn = GroupNorm(ph, keep, x, it_ps, False)
        x_in, x_norm, border = ph.sem("x_in"), ph.sem("x_norm"), ph.sem("border")
        tile_done, tile_read = ph.sem("tile_done"), ph.sem("tile_read")
        tap, conv = ph.sem("tap"), ph.sem("conv")
        sq_ready, ss_done, root = ph.sem("sq_ready"), ph.sem("ss_done"), ph.sem("root")
        inv_ready, turned, inv_t_ready = ph.sem("inv_ready"), ph.sem("turned"), ph.sem("inv_t_ready")
        inv_stored = ph.sem("inv_stored")
        r_in = [ph.sem("r_in0"), ph.sem("r_in1")]
        unit, hi_ready, lo_ready, parts_stored = ph.sem("unit"), ph.sem("hi_ready"), ph.sem("lo_ready"), ph.sem("parts_stored")
        vt_stored = ph.sem("vt_stored")
        NB = 3 * NCB
        NQKV = NB * NCH
        RING = 6
        b_qkv, b_dw = keep["dw"][:, 9, :], keep["dw"][:, 10, :]
        r_buf = x

        with nc.Block() as block:

            @block.sync
            def _(sp):
                sp.dma_start(x[:, :, :], dram["x1"].rearrange("k p l -> p k l")).then_inc(x_in, 16)
                sp.dma_start(w_qkv[:, :, :], io["w_qkv_t"]).then_inc(x_in, 16)
                sp.wait_ge(inv_t_ready, 1)
                sp.dma_start(dram["inv"].rearrange("(a h) (t p) -> (h t) a p", a=2, p=128),
                             inv_t[:, :, :]).then_inc(inv_stored, 16)
                sp.wait_ge(inv_stored, 16)

                def load_r(j):
                    for jj in range(2):
                        src = dram["inv"][2 * j + jj:2 * j + jj + 1, :].partition_broadcast(HD)
                        sp.dma_start(r_buf[jj * HD:(jj + 1) * HD, j % 2, :],
                                     src.rearrange("p a l -> p (a l)")).then_inc(r_in[j % 2], 16)

                sp.wait_ge(tile_done, NQKV)
                load_r(0)
                load_r(1)
                for j in range(4):
                    dst = dram["q" if j < 2 else "k"]
                    rows = slice((j % 2) * CB, (j % 2 + 1) * CB)
                    sp.wait_ge(hi_ready, j + 1)
                    sp.dma_start(dst[0, rows, :], hi[:, :]).then_inc(parts_stored, 16)
                    sp.wait_ge(lo_ready, j + 1)
                    sp.dma_start(dst[1, rows, :], lo[:, :]).then_inc(parts_stored, 16)
                    if j < 2:
                        load_r(j + 2)
                sp.wait_ge(parts_stored, 16 * 8)
                sp.wait_ge(vt_stored, 32)

            @block.gpsimd
            def _(pool):
                for i in range(2):
                    pool.memset(pad[:, i, :, :], 0.0).then_inc(border, 1)

            @block.tensor
            def _(pe):
                pe.wait_ge(x_in, 32)
                gn.tensor(pe)
                pe.wait_ge(x_norm, NCB)

                def project(j):
                    for c in range(NCH):
                        t = j * NCH + c
                        if t >= RING:
                            pe.wait_ge(tile_read, t - RING + 1)
                        for k in range(NCB):
                            mm = pe.matmul(ps[0:CB, t % RING, :], w_qkv[:, k, j * CB:(j + 1) * CB],
                                           x[:, k, c * BANK:(c + 1) * BANK], start=(k == 0), stop=(k == NCB - 1))
                        mm.then_inc(tile_done, 1)

                def square_sums(j):
                    pe.wait_ge(sq_ready, j + 1)
                    out = ss_ps[:, 0:8 * KT].rearrange("p (j h t) -> p j h t", j=4, h=2)
                    for t in range(KT):
                        mm = pe.matmul(out[:, j, :, t], sq[:, t * 128:(t + 1) * 128], keep["head_sum"][:, :],
                                       start=True, stop=True)
                    mm.then_inc(ss_done, 1)

                def turn_v(j):
                    for g in range(KT // 4):
                        t = NQKV + j * (KT // 4) + g
                        pe.wait_ge(tile_read, t - RING + 1)
                        for i in range(4):
                            col = (4 * g + i) * 128
                            mm = pe.transpose(ps[:, t % RING, i * CB:(i + 1) * CB], sq[:, col:col + 128],
                                              keep["ident"][0:CB, 0:CB])
                        mm.then_inc(tile_done, 1)

                project(0)
                project(1)
                for j in range(2, NB):
                    project(j)
                    square_sums(j - 2)
                pe.wait_ge(inv_ready, 1)
                for i in range(2):
                    mm = pe.transpose(it_ps[:, i * 128:(i + 1) * 128], inv[:, i * 128:(i + 1) * 128], keep["ident"][:, :])
                mm.then_inc(turned, 1)
                for j in range(2):
                    pe.wait_ge(conv, 5 + j)
                    turn_v(j)

            @block.scalar
            def _(act):
                gn.scalar(act)

                def unload(j):
                    if j == 0:
                        act.wait_ge(border, 2)
                    if j >= 2:
                        act.wait_ge(conv, j - 1)
                    for c in range(NCH):
                        t = j * NCH + c
                        act.wait_ge(tile_done, t + 1)
                        act.activation(pad[:, j % 2, 1 + c * ROWS:1 + (c + 1) * ROWS, 1:W + 1],
                                       ps[0:CB, t % RING, :].rearrange("p (r w) -> p r w", w=W), ACT.Identity,
                                       bias=b_qkv[:, j:j + 1]).then_inc(tile_read, 1)

                def squares(j):
                    act.wait_ge(conv, j + 1)
                    if j >= 1:
                        act.wait_ge(ss_done, j)
                    act.activation(sq[:, :], qk[:, j, :], ACT.Square).then_inc(sq_ready, 1)

                unload(0)
                unload(1)
                for j in range(2, NB):
                    unload(j)
                    squares(j - 2)
                act.wait_ge(ss_done, 4)
                act.activation(length[:, :], ss_ps[:, 0:8 * KT], ACT.Sqrt).then_inc(root, 1)
                for j in range(2):
                    if j == 1:
                        act.wait_ge(vt_stored, 16)
                    for g in range(KT // 4):
                        t = NQKV + j * (KT // 4) + g
                        act.wait_ge(tile_done, t + 1)
                        act.activation(vt[:, :, 4 * g:4 * g + 4, :],
                                       ps[:, t % RING, 0:4 * CB].rearrange("p (i h c) -> p h i c", i=4, h=2),
                                       ACT.Copy).then_inc(tile_read, 1)
                    act.wait_ge(tile_read, NQKV + NCH * (j + 1))
                    act.dma_start(dram["v"][2 * j:2 * j + 2].rearrange("h p t c -> p h (t c)"),
                                  vt[:, :, :, :].rearrange("p h t c -> p h (t c)")).then_inc(vt_stored, 16)
                for j in range(4):
                    act.wait_ge(unit, j + 1)
                    if j >= 1:
                        act.wait_ge(lo_ready, j)
                        act.wait_ge(parts_stored, 32 * j)
                    act.activation(hi[:, :], qk[:, j, :], ACT.Copy).then_inc(hi_ready, 1)

            @block.vector
            def _(dve):
                dve.wait_ge(x_in, 32)
                gn.vector(dve)
                for k in range(NCB):
                    dve.tensor_scalar(x[:, k, :], x[:, k, :], gn.scale[:, k:k + 1], gn.shift[:, k:k + 1],
                                      ALU.mult, ALU.add).then_inc(x_norm, 1)
                taps = Count(tap)

                def convolve(j):
                    dve.wait_ge(tile_read, NCH * (j + 1))
                    if j == 4:
                        dve.wait_ge(ss_done, 4)
                    if j == 5:
                        dve.wait_ge(tile_done, NQKV + NCH)
                    dst = (qk[:, j, :] if j < 4 else sq[:, :]).rearrange("p (r w) -> p r w", w=W)
                    for k in range(9):
                        src = pad[:, j % 2, k // 3:k // 3 + H, k % 3:k % 3 + W]
                        w = keep["dw"][:, k, j:j + 1]
                        if k == 0:
                            ins = dve.tensor_scalar(dst, src, w, b_dw[:, j:j + 1], ALU.mult, ALU.add)
                        else:
                            ins = dve.scalar_tensor_tensor(dst, src, w, dst, ALU.mult, ALU.add)
                        if k < 8:
                            dve.wait_ge(tap, taps.on(ins))
                    ins.then_inc(conv, 1)

                for j in range(5):
                    convolve(j)
                dve.wait_ge(root, 1)
                dve.wait_ge(tap, taps.on(dve.tensor_scalar(length[:, :], length[:, :], 1e-12, 1.0 / QSCALE, ALU.max, ALU.mult)))
                dve.reciprocal(inv[:, :], length[:, :]).then_inc(inv_ready, 1)
                dve.wait_ge(turned, 1)
                dve.tensor_copy(inv_t[:, :, :], it_ps[:, 0:256].rearrange("p (a b) -> p a b", a=2)).then_inc(inv_t_ready, 1)
                convolve(5)
                for j in range(4):
                    dve.wait_ge(r_in[j % 2], 32 * (j // 2 + 1))
                    dve.tensor_tensor(qk[:, j, :], qk[:, j, :], r_buf[:, j % 2, :], ALU.mult).then_inc(unit, 1)
                    dve.wait_ge(hi_ready, j + 1)
                    if j >= 1:
                        dve.wait_ge(parts_stored, 32 * j)
                    dve.wait_ge(unit, j + 1)
                    dve.tensor_tensor(lo[:, :], qk[:, j, :], hi[:, :], ALU.subtract).then_inc(lo_ready, 1)


def layer1_finish(nc, io, keep, dram, b):
    with Phase(nc, "l1post") as ph:
        o = ph.sb("o", [CB, NCB, L])
        r = ph.sb("r", [CB, NCB, L])
        x = ph.sb("x", [CB, NCB, L])
        den = ph.sb("den", [128, HEADS * L // 128])
        ps = ph.ps("ps", [128, 8, BANK])
        den_in, den_inv, inv_stored, r_in = ph.sem("den_in"), ph.sem("den_inv"), ph.sem("inv_stored"), ph.sem("r_in")
        ox_in, scaled, tile_done, ready, stored = ph.sem("ox_in"), ph.sem("scaled"), ph.sem("tile_done"), ph.sem("ready"), ph.sem("stored")
        b_proj = keep["chan"][:, 2, :]
        flat = lambda t: t.rearrange("h (a l) -> (h a) l", l=128)

        with nc.Block() as block:

            @block.sync
            def _(sp):
                sp.dma_start(den[:, :], flat(dram["den"])).then_inc(den_in, 16)
                sp.dma_start(o[:, :, :], dram["o"].rearrange("(k p) l -> p k l", p=CB)).then_inc(ox_in, 16)
                sp.dma_start(x[:, :, :], dram["x1"].rearrange("k p l -> p k l")).then_inc(ox_in, 16)
                sp.wait_ge(den_inv, 1)
                sp.dma_start(flat(dram["rden"]), den[:, :]).then_inc(inv_stored, 16)
                sp.wait_ge(inv_stored, 16)
                for h in range(HEADS):
                    k, half = divmod(h, 2)
                    src = dram["rden"][h:h + 1, :].partition_broadcast(HD).rearrange("p a l -> p (a l)")
                    sp.dma_start(r[half * HD:(half + 1) * HD, k, :], src).then_inc(r_in, 16)
                for k in range(NCB):
                    sp.wait_ge(ready, NCH * (k + 1))
                    dst = io["out"][ds(b, 1)].rearrange("a (k p) l -> p (a k) l", p=CB)
                    sp.dma_start(dst[:, k, :], x[:, k, :]).then_inc(stored, 16)
                sp.wait_ge(stored, 16 * NCB)

            @block.tensor
            def _(pe):
                pe.wait_ge(scaled, NCB)
                for t in range(NCB * NCH):
                    mo, c = divmod(t, NCH)
                    if t >= 8:
                        pe.wait_ge(ready, t - 7)
                    for k in range(NCB):
                        mm = pe.matmul(ps[0:CB, t % 8, :], keep["w_proj"][:, k, mo * CB:(mo + 1) * CB],
                                       o[:, k, c * BANK:(c + 1) * BANK], start=(k == 0), stop=(k == NCB - 1))
                    mm.then_inc(tile_done, 1)

            @block.vector
            def _(dve):
                dve.wait_ge(den_in, 16)
                dve.reciprocal(den[:, :], den[:, :]).then_inc(den_inv, 1)
                dve.wait_ge(ox_in, 32)
                dve.wait_ge(r_in, 16 * HEADS)
                for k in range(NCB):
                    dve.tensor_tensor(o[:, k, :], o[:, k, :], r[:, k, :], ALU.mult).then_inc(scaled, 1)
                for t in range(NCB * NCH):
                    mo, c = divmod(t, NCH)
                    dve.wait_ge(tile_done, t + 1)
                    xs = x[:, mo, c * BANK:(c + 1) * BANK]
                    dve.scalar_tensor_tensor(xs, ps[0:CB, t % 8, :], b_proj[:, mo:mo + 1], xs,
                                             ALU.add, ALU.add).then_inc(ready, 1)


def build(nc, io):
    batches = io["x"].shape[0]
    scratch = {
        "u": ([DB, 128, L], F32), "z": ([DB, 128, L], F32), "delta": ([DB, 128, L], F32), "y": ([DB, 128, L], F32),
        "bc": ([2 * NST, L], F32), "x1": ([NCB, CB, L], F32), "inv": ([8, L], F32),
        "q": ([2, C, L], F16), "k": ([2, C, L], F16), "v": ([HEADS, 128, KT, HD], F32),
        "o": ([C, L], F32), "den": ([HEADS, L], F32), "rden": ([HEADS, L], F32),
    }
    dram = {k: nc.dram_tensor(f"scratch_{k}", shape, dt, kind="Internal").ap() for k, (shape, dt) in scratch.items()}
    kept = {
        "ident": [128, 128], "group_mean": [CB, CB], "all_mean": [CB, CB], "head_sum": [CB, 2],
        "x_proj": [128, DB, DTR + 2 * NST], "dt_proj": [DTR, DB, 128], "w_proj": [CB, NCB, C],
        "chan": [CB, 3, NCB], "inner": [128, 7, DB], "le": [128, DB, 9], "a": [128, DB, NST],
        "dw": [CB, 11, 6], "w_out": [128, DB, C], "temp": [128, 2, HEADS], "carry": [128, NST * DB],
    }
    with ExitStack() as ctx:
        keep = {k: ctx.enter_context(nc.sbuf_tensor(f"keep_{k}", shape, F32)) for k, shape in kept.items()}
        setup(nc, io, keep)

        def front(b):
            layer0_project(nc, io, keep, dram, b)
            clear_carry(nc, keep)

        def back(b):
            layer0_finish(nc, io, keep, dram, b)
            layer1_project(nc, io, keep, dram)

        front(0)
        with nc.Fori(0, NTC) as hc:
            scan_and_attend(nc, keep, dram, hc, True, False)
        back(0)
        if batches > 1:
            with nc.Fori(1, batches) as b:
                front(b)
                with nc.Fori(0, NTC) as hc:
                    scan_and_attend(nc, keep, dram, hc, True, True)
                layer1_finish(nc, io, keep, dram, b - 1)
                back(b)
        with nc.Fori(0, NTC) as hc:
            scan_and_attend(nc, keep, dram, hc, False, True)
        layer1_finish(nc, io, keep, dram, batches - 1)


def lay_out(inputs):
    a = {k.split("_conv_")[-1] if "_conv_" in k else k: np.asarray(v) for k, v in inputs.items()}
    w_dw = a["w_dw"].reshape(3 * C, 9)
    rows = lambda v, p: v.reshape(-1, p).T
    eye = np.eye(128, dtype=np.float32)
    group = np.kron(np.eye(CB // GROUP, dtype=np.float32), np.full((GROUP, GROUP), 1.0 / GROUP, np.float32))
    heads = np.kron(np.eye(2, dtype=np.float32), np.ones((HD, 1), np.float32))
    blocks = lambda w, p: w.reshape(-1, p, w.shape[1]).transpose(1, 0, 2)
    inner = np.stack([rows(a["conv1d_b"], 128), rows(a["dt_proj_b"], 128), rows(a["Dskip"], 128)]
                     + [rows(a["conv1d_w"][:, k], 128) for k in range(4)], axis=1)
    dw = np.stack([rows(w_dw[:, k], CB) for k in range(9)] + [rows(a["b_qkv"], CB), rows(a["b_dw"], CB)], axis=1)
    return {
        "x": a["x"].reshape(-1, C, L),
        "ident": eye,
        "group_mean": group,
        "all_mean": np.full((CB, CB), 1.0 / C, np.float32),
        "head_sum": heads,
        "in_proj_t": blocks(a["in_proj_w"].T, CB),
        "x_proj_t": blocks(a["x_proj_w"].T, 128),
        "dt_proj_t": a["dt_proj_w"].T.reshape(DTR, DB, 128),
        "out_proj": blocks(a["out_proj_w"], CB),
        "proj_out_t": blocks(a["proj_out_w"].T, CB),
        "w_qkv_t": blocks(a["w_qkv"].T, CB),
        "w_proj_t": blocks(a["w_proj"].T, CB),
        "chan": np.stack([rows(a["gn_gamma"], CB), rows(a["gn_beta"], CB), rows(a["b_proj"], CB)], axis=1),
        "inner": inner,
        "le": blocks(a["le_w"].reshape(DIN, 9), 128),
        "a_log": blocks(a["A_log"], 128),
        "dw": dw,
        "temperature": a["temperature"].reshape(HEADS),
    }


def kernel(**inputs):
    import concourse.bacc as bacc
    from concourse.bass_utils import run_bass_kernel_spmd

    nc = bacc.Bacc("TRN2", target_bir_lowering=False, num_devices=1)
    arrays, io = {}, {}
    for name, a in lay_out(inputs).items():
        a = np.ascontiguousarray(a)
        arrays[f"in_{name}"] = a
        io[name] = nc.dram_tensor(f"in_{name}", a.shape, mybir.dt.from_np(a.dtype), kind="ExternalInput").ap()
    batches = io["x"].shape[0]
    io["out"] = nc.dram_tensor("out", (batches, C, L), F32, kind="ExternalOutput").ap()
    build(nc, io)
    r = run_bass_kernel_spmd(nc, [arrays], core_ids=[0])
    return r.results[0]["out"].reshape(batches, C, H, W)
```

```python
from contextlib import ExitStack

import concourse.bass as bass
import numpy as np
from concourse import mybir

F32 = mybir.dt.float32
F16 = mybir.dt.float16
ALU = mybir.AluOpType
ACT = mybir.ActivationFunctionType
ds = bass.ds

C = 192
H = W = 64
L = H * W
CB = 96
NCB = C // CB
DIN = 2 * C
DB = DIN // 128
NST = 16
DTR = 12
GROUP = C // 32
HEADS = 4
HD = C // HEADS
BANK = 512
NCH = L // BANK
ROWS = BANK // W
TC = 1024
NTC = L // TC
KT = L // 128
PADW = W + 2
QSCALE = 64.0
VROW = 64
SHIFT_FREE = 60.0


class Count:

    def __init__(self, sem):
        self.sem, self.n = sem, 0

    def on(self, ins, by=1):
        ins.then_inc(self.sem, by)
        self.n += by
        return self.n


def end_phase(nc, sems):
    for s in sems:
        nc.sync.sem_clear(s)
    nc.all_engine_barrier()


class Phase:

    def __init__(self, nc, name):
        self.nc, self.name, self.ctx, self.sems = nc, f"{name}{nc.next_id()}", ExitStack(), []

    def __enter__(self):
        self.ctx.__enter__()
        return self

    def __exit__(self, *e):
        if e[0] is None:
            end_phase(self.nc, self.sems)
        return self.ctx.__exit__(*e)

    def sb(self, name, shape, dt=F32):
        return self.ctx.enter_context(self.nc.sbuf_tensor(f"{self.name}_{name}", shape, dt))

    def ps(self, name, shape):
        return self.ctx.enter_context(self.nc.psum_tensor(f"{self.name}_ps_{name}", shape, F32))

    def sem(self, name):
        s = self.ctx.enter_context(self.nc.semaphore(f"{self.name}_{name}"))
        self.sems.append(s)
        return s


def setup(nc, io, keep):
    with Phase(nc, "setup") as ph:
        op_w = ph.sb("out_proj", [CB, NCB, DIN])
        po_w = ph.sb("proj_out", [CB, NCB, C])
        temp = ph.sb("temp", [128, HEADS])
        tabs = ph.sb("tabs", [128, HEADS])
        comb_ps = ph.ps("comb", [128, DB, BANK])
        loaded, combined, a_exp, tmp = ph.sem("loaded"), ph.sem("combined"), ph.sem("a_exp"), ph.sem("tmp")
        loads = [
            (keep["ident"][:, :], io["ident"]),
            (keep["group_mean"][:, :], io["group_mean"]),
            (keep["all_mean"][:, :], io["all_mean"]),
            (keep["head_sum"][:, :], io["head_sum"]),
            (keep["x_proj"][:, :, :], io["x_proj_t"]),
            (keep["dt_proj"][:, :, :], io["dt_proj_t"]),
            (keep["w_proj"][:, :, :], io["w_proj_t"]),
            (keep["chan"][:, :, :], io["chan"]),
            (keep["inner"][:, :, :], io["inner"]),
            (keep["le"][:, :, :], io["le"]),
            (keep["a"][:, :, :], io["a_log"]),
            (keep["dw"][:, :, :], io["dw"]),
            (op_w[:, :, :], io["out_proj"]),
            (po_w[:, :, :], io["proj_out_t"]),
            (temp[:, :], io["temperature"].partition_broadcast(128)),
        ]
        with nc.Block() as block:

            @block.sync
            def _(sp):
                for dst, src in loads:
                    sp.dma_start(dst, src).then_inc(loaded, 16)

            @block.tensor
            def _(pe):
                pe.wait_ge(loaded, 16 * len(loads))
                for m in range(DB):
                    for k in range(NCB):
                        mm = pe.matmul(comb_ps[:, m, 0:C], op_w[:, k, m * 128:(m + 1) * 128], po_w[:, k, :],
                                       start=(k == 0), stop=(k == NCB - 1))
                mm.then_inc(combined, 1)

            @block.scalar
            def _(act):
                act.wait_ge(loaded, 16 * len(loads))
                act.activation(keep["a"][:, :, :], keep["a"][:, :, :], ACT.Exp).then_inc(a_exp, 1)

            @block.vector
            def _(dve):
                dve.wait_ge(loaded, 16 * len(loads))
                dve.tensor_scalar(keep["le"][:, :, 4:5], keep["le"][:, :, 4:5], 1.0, None, ALU.add)
                dve.tensor_scalar(keep["temp"][:, 0, :], temp[:, :], 1.0 / QSCALE ** 2, None, ALU.mult)
                dve.tensor_scalar(tabs[:, :], temp[:, :], -1.0, None, ALU.mult).then_inc(tmp, 1)
                dve.wait_ge(tmp, 1)
                dve.tensor_tensor(tabs[:, :], tabs[:, :], temp[:, :], ALU.max).then_inc(tmp, 1)
                dve.wait_ge(tmp, 2)
                dve.tensor_scalar(tabs[:, :], tabs[:, :], -1.0, SHIFT_FREE, ALU.mult, ALU.add).then_inc(tmp, 1)
                dve.wait_ge(tmp, 3)
                dve.tensor_scalar(keep["temp"][:, 1, :], tabs[:, :], 0.0, None, ALU.min)
                dve.wait_ge(a_exp, 1)
                dve.tensor_scalar(keep["a"][:, :, :], keep["a"][:, :, :], -1.0, None, ALU.mult)
                dve.wait_ge(combined, 1)
                dve.tensor_copy(keep["w_out"][:, :, :], comb_ps[:, :, 0:C])


def share(i, n, total):
    return range(total * i // n, total * (i + 1) // n)


def load_image(q, dst, src, sem):
    for k in range(NCB):
        for half in range(2):
            cols = slice(half * L // 2, (half + 1) * L // 2)
            q.dma_start(dst[:, k, cols], src[:, k, cols]).then_inc(sem[2 * k + half], 16)


class GroupNorm:

    EPS = 1e-5

    def __init__(self, ph, keep, x, ps, whole):
        self.keep, self.x, self.ps, self.whole = keep, x, ps, whole
        self.x_in = [ph.sem(f"x_in{i}") for i in range(2 * NCB)] if whole else []
        self.chunk_stats = ph.sb("chunk_stats", [CB, NCB, NCH, 6])
        self.mv = ph.sb("mean_var", [CB, NCB, 2])
        self.chan = ph.sb("chan_stats", [CB, 2, NCB])
        self.grp = ph.sb("group_stats", [CB, 2, NCB])
        self.tmp = ph.sb("stats_tmp", [CB, NCB])
        self.std = ph.sb("std", [CB, NCB])
        self.scale = ph.sb("gn_scale", [CB, NCB])
        self.shift = ph.sb("gn_shift", [CB, NCB])
        self.tot = ph.sb("total", [CB, 2])
        self.rows = ph.sem("chan_stats_ready")
        self.means = ph.sem("means_ready")
        self.var = ph.sem("var_ready")
        self.root = ph.sem("root_ready")
        self.step = ph.sem("stats_step")

    def tensor(self, pe):
        pe.wait_ge(self.rows, 1)
        pe.matmul(self.ps[0:CB, 0:2 * NCB], self.keep["group_mean"][:, :],
                  self.chan[:, :, :].rearrange("p a b -> p (a b)"), start=True, stop=True).then_inc(self.means, 1)
        if self.whole:
            pe.wait_ge(self.rows, 2)
            for k in range(NCB):
                mm = pe.matmul(self.ps[0:CB, 0:2], self.keep["all_mean"][:, :], self.chan[:, :, k],
                               start=(k == 0), stop=(k == NCB - 1))
            mm.then_inc(self.means, 1)

    def scalar(self, act):
        act.wait_ge(self.var, 1)
        act.activation(self.std[:, :], self.tmp[:, :], ACT.Sqrt).then_inc(self.root, 1)
        if self.whole:
            act.wait_ge(self.var, 2)
            act.activation(self.std[:, 0:1], self.tmp[:, 0:1], ACT.Sqrt).then_inc(self.root, 1)

    def vector(self, dve):
        step = Count(self.step)

        def then(ins):
            dve.wait_ge(self.step, step.on(ins))

        for k in range(NCB):
            for c in range(NCH):
                if self.x_in and c % (NCH // 2) == 0:
                    dve.wait_ge(self.x_in[2 * k + c // (NCH // 2)], 16)
                ins = dve.bn_stats(self.chunk_stats[:, k, c, :], self.x[:, k, c * BANK:(c + 1) * BANK])
        then(ins)
        for k in range(NCB):
            ins = dve.bn_aggr(self.mv[:, k, :], self.chunk_stats[:, k, :, :].rearrange("p c s -> p (c s)"))
        then(ins)
        mean, var = self.mv[:, :, 0], self.mv[:, :, 1]
        step.on(dve.tensor_copy(self.chan[:, 0, :], mean))
        then(dve.tensor_tensor(self.tmp[:, :], mean, mean, ALU.mult))
        dve.tensor_tensor(self.chan[:, 1, :], self.tmp[:, :], var, ALU.add).then_inc(self.rows, 1)
        dve.wait_ge(self.rows, 1)
        dve.wait_ge(self.means, 1)
        then(dve.tensor_copy(self.grp[:, :, :], self.ps[0:CB, 0:2 * NCB].rearrange("p (a b) -> p a b", a=2)))
        gm, gsq = self.grp[:, 0, :], self.grp[:, 1, :]
        then(dve.tensor_tensor(self.std[:, :], gm, gm, ALU.mult))
        dve.scalar_tensor_tensor(self.tmp[:, :], gsq, self.EPS, self.std[:, :], ALU.add, ALU.subtract).then_inc(self.var, 1)
        dve.wait_ge(self.var, 1)
        dve.wait_ge(self.root, 1)
        then(dve.reciprocal(self.scale[:, :], self.std[:, :]))
        then(dve.scalar_tensor_tensor(self.shift[:, :], gm, -1.0, self.scale[:, :], ALU.mult, ALU.mult))
        if not self.whole:
            return
        then(dve.tensor_tensor(self.tmp[:, :], mean, self.scale[:, :], ALU.mult))
        then(dve.tensor_tensor(self.chan[:, 0, :], self.tmp[:, :], self.shift[:, :], ALU.add))
        then(dve.tensor_tensor(self.tmp[:, :], self.chan[:, 0, :], self.chan[:, 0, :], ALU.mult))
        then(dve.tensor_tensor(self.chan[:, 1, :], self.scale[:, :], self.scale[:, :], ALU.mult))
        then(dve.tensor_tensor(self.chan[:, 1, :], self.chan[:, 1, :], var, ALU.mult))
        dve.tensor_tensor(self.chan[:, 1, :], self.chan[:, 1, :], self.tmp[:, :], ALU.add).then_inc(self.rows, 1)
        dve.wait_ge(self.rows, 2)
        dve.wait_ge(self.means, 2)
        then(dve.tensor_copy(self.tot[:, :], self.ps[0:CB, 0:2]))
        then(dve.tensor_tensor(self.std[:, 0:1], self.tot[:, 0:1], self.tot[:, 0:1], ALU.mult))
        dve.scalar_tensor_tensor(self.tmp[:, 0:1], self.tot[:, 1:2], self.EPS, self.std[:, 0:1],
                                 ALU.add, ALU.subtract).then_inc(self.var, 1)
        dve.wait_ge(self.var, 2)
        dve.wait_ge(self.root, 2)
        then(dve.reciprocal(self.std[:, 1:2], self.std[:, 0:1]))
        gamma, beta = self.keep["chan"][:, 0, :], self.keep["chan"][:, 1, :]
        r = self.std[:, 1:2]
        then(dve.scalar_tensor_tensor(self.scale[:, :], self.scale[:, :], r, gamma, ALU.mult, ALU.mult))
        then(dve.tensor_scalar(self.shift[:, :], self.shift[:, :], self.tot[:, 0:1], r, ALU.subtract, ALU.mult))
        then(dve.tensor_tensor(self.shift[:, :], self.shift[:, :], gamma, ALU.mult))
        then(dve.tensor_tensor(self.shift[:, :], self.shift[:, :], beta, ALU.add))


def layer0_project(nc, io, keep, dram, b):
    with Phase(nc, "l0pre") as ph:
        x = ph.sb("x", [CB, NCB, L])
        w_in = ph.sb("in_proj", [CB, NCB, 2 * DIN])
        u_raw = ph.sb("u_raw", [128, 2, L + 3])
        u_c = ph.sb("u_conv", [128, DB, L])
        z_s = ph.sb("z_silu", [128, 2, L])
        dbl = ph.sb("dbl", [DTR + 2 * NST, L])
        ps = ph.ps("ps", [128, 8, BANK])
        gn = GroupNorm(ph, keep, x, ps[:, 0, :], True)
        w_in_in, x_norm = ph.sem("w_in_loaded"), ph.sem("x_norm")
        tile_done, tile_read = ph.sem("tile_done"), ph.sem("tile_read")
        pads, conv, u_ready = ph.sem("pads"), ph.sem("conv"), ph.sem("u_ready")
        z_stored = [ph.sem("z_stored0"), ph.sem("z_stored1")]
        xp_done, dbl_ready = ph.sem("x_proj_done"), ph.sem("dbl_ready")
        dt_done, dt_read, dt_abs = ph.sem("dt_done"), ph.sem("dt_read"), ph.sem("dt_abs")
        e_ready, w_ready, ln_ready = ph.sem("e_ready"), ph.sem("w_ready"), ph.sem("ln_ready")
        tap_done, half_ready, rest_ready = ph.sem("tap_done"), ph.sem("half_ready"), ph.sem("rest_ready")
        delta_ready = ph.sem("delta_ready")
        delta_stored = [ph.sem(f"delta_stored{i}") for i in range(4)]
        u_stored, bc_stored = ph.sem("u_stored"), ph.sem("bc_stored")
        NT = 2 * DB * NCH
        NEARLY = (DB + 1) * NCH
        NQ = DB * NTC
        NSETS = 4
        views = [[t[:, r, i * TC:(i + 1) * TC] for i in range(4)] for t in (u_raw, u_c) for r in range(2)]
        conv_b, dt_b = keep["inner"][:, 0, :], keep["inner"][:, 1, :]
        conv_w = keep["inner"][:, 3:7, :]

        with nc.Block() as block:

            @block.sync
            def _(sp):
                load_image(sp, x, io["x"][ds(b, 1)].rearrange("a (k p) l -> p (a k) l", p=CB), gn.x_in)
                sp.dma_start(w_in[:, :, :], io["in_proj_t"]).then_inc(w_in_in, 16)
                for m in range(DB):
                    sp.wait_ge(u_ready, m + 1)
                    sp.dma_start(dram["u"][m], u_c[:, m, :]).then_inc(u_stored, 16)
                sp.wait_ge(dbl_ready, NCH)
                sp.dma_start(dram["bc"], dbl[DTR:, :]).then_inc(bc_stored, 16)
                for q in range(NQ):
                    m, c = divmod(q, NTC)
                    sp.wait_ge(delta_ready, q + 1)
                    sp.dma_start(dram["delta"][m][:, c * TC:(c + 1) * TC], views[q % NSETS][2]
                                 ).then_inc(delta_stored[q % NSETS], 16)
                sp.wait_ge(u_stored, 16 * DB)
                sp.wait_ge(bc_stored, 16)
                sp.wait_ge(z_stored[0], 32)
                sp.wait_ge(z_stored[1], 16)
                for s in delta_stored:
                    sp.wait_ge(s, 16 * NQ // NSETS)

            @block.tensor
            def _(pe):
                gn.tensor(pe)
                pe.wait_ge(w_in_in, 16)
                pe.wait_ge(x_norm, NCB)

                def project(t):
                    m, c = divmod(t, NCH)
                    if t >= 4:
                        pe.wait_ge(tile_read, t - 3)
                    if t == NEARLY:
                        pe.wait_ge(dbl_ready, NCH)
                    for k in range(NCB):
                        mm = pe.matmul(ps[:, t % 4, :], w_in[:, k, m * 128:(m + 1) * 128],
                                       x[:, k, c * BANK:(c + 1) * BANK], start=(k == 0), stop=(k == NCB - 1))
                    mm.then_inc(tile_done, 1)

                for t in range(NEARLY):
                    project(t)
                pe.wait_ge(u_ready, DB)
                for c in range(NCH):
                    if c >= 4:
                        pe.wait_ge(dbl_ready, c - 3)
                    for k in range(DB):
                        mm = pe.matmul(ps[0:DTR + 2 * NST, 4 + c % 4, :], keep["x_proj"][:, k, :],
                                       u_c[:, k, c * BANK:(c + 1) * BANK], start=(k == 0), stop=(k == DB - 1))
                    mm.then_inc(xp_done, 1)
                pe.wait_ge(dbl_ready, NCH)
                for q in range(NQ):
                    m, chunk = divmod(q, NTC)
                    if q >= 2:
                        pe.wait_ge(dt_read, q - 1)
                    for c in range(2):
                        col = chunk * TC + c * BANK
                        mm = pe.matmul(ps[:, 4 + 2 * (q % 2) + c, :], keep["dt_proj"][:, m, :],
                                       dbl[0:DTR, col:col + BANK], start=True, stop=True)
                    mm.then_inc(dt_done, 1)
                    for t in share(q, NQ, NT - NEARLY):
                        project(NEARLY + t)

            @block.scalar
            def _(act):
                gn.scalar(act)

                def unload_u(m):
                    if m == 0:
                        act.wait_ge(pads, 1)
                    if m >= 2:
                        act.wait_ge(conv, 2 * (m - 1))
                    for c in range(NCH):
                        t = m * NCH + c
                        act.wait_ge(tile_done, t + 1)
                        src = ps[:, t % 4, :].rearrange("p (r two w) -> p r two w", two=2, w=W)
                        dst = u_raw[:, m % 2, 3 + c * BANK:3 + (c + 1) * BANK].rearrange(
                            "p (r two w) -> p r two w", two=2, w=W)
                        act.activation(dst[:, :, 0, :], src[:, :, 0, :], ACT.Copy)
                        act.activation(dst[:, :, 1, :], src[:, :, 1, ::-1], ACT.Copy).then_inc(tile_read, 1)

                def silu_u(m):
                    act.wait_ge(conv, 2 * (m + 1))
                    act.activation(u_c[:, m, :], u_c[:, m, :], ACT.Silu, bias=conv_b[:, m:m + 1]).then_inc(u_ready, 1)

                def silu_z(t):
                    m, c = t // NCH - DB, t % NCH
                    if m >= 2 and c == 0:
                        act.wait_ge(z_stored[m % 2], 16)
                    act.wait_ge(tile_done, t + 1)
                    act.activation(z_s[:, m % 2, c * BANK:(c + 1) * BANK], ps[:, t % 4, :], ACT.Silu).then_inc(tile_read, 1)
                    if c == NCH - 1:
                        act.wait_ge(tile_read, t + 1)
                        act.dma_start(dram["z"][m], z_s[:, m % 2, :]).then_inc(z_stored[m % 2], 16)

                unload_u(0)
                unload_u(1)
                silu_u(0)
                unload_u(2)
                silu_u(1)
                for t in range(DB * NCH, NEARLY):
                    silu_z(t)
                silu_u(2)

                def softplus_front(q):
                    m, buf = q // NTC, views[q % NSETS]
                    v = ps[:, 4 + 2 * (q % 2):6 + 2 * (q % 2), :].rearrange("p a b -> p (a b)")
                    act.wait_ge(dt_done, q + 1)
                    if q >= NSETS:
                        act.wait_ge(delta_ready, q - NSETS + 1)
                        act.wait_ge(delta_stored[q % NSETS], 16 * (q // NSETS))
                    elif q == 2:
                        act.wait_ge(u_stored, 16 * DB)
                    act.activation(buf[0], v, ACT.Abs, bias=dt_b[:, m:m + 1]).then_inc(dt_abs, 1)
                    act.activation(buf[3], v, ACT.Relu, bias=dt_b[:, m:m + 1]).then_inc(dt_read, 1)
                    act.wait_ge(dt_abs, q + 1)
                    act.activation(buf[0], buf[0], ACT.Exp, scale=-1.0).then_inc(e_ready, 1)

                def softplus_ln(q):
                    buf = views[q % NSETS]
                    act.wait_ge(w_ready, q + 1)
                    act.activation(buf[2], buf[1], ACT.Ln).then_inc(ln_ready, 1)

                for q in range(NQ + 1):
                    if q < NQ:
                        softplus_front(q)
                    if q >= 1:
                        softplus_ln(q - 1)
                    if q < NQ:
                        for t in share(q, NQ, NT - NEARLY):
                            silu_z(NEARLY + t)

            @block.vector
            def _(dve):
                dve.memset(u_raw[:, :, 0:3], 0.0).then_inc(pads, 1)
                gn.vector(dve)
                for k in range(NCB):
                    dve.tensor_scalar(x[:, k, :], x[:, k, :], gn.scale[:, k:k + 1], gn.shift[:, k:k + 1],
                                      ALU.mult, ALU.add).then_inc(x_norm, 1)
                tap = Count(tap_done)
                for m in range(DB):
                    for half in range(2):
                        lo = half * L // 2
                        dst = u_c[:, m, lo:lo + L // 2]
                        dve.wait_ge(tile_read, NCH * m + NCH // 2 * (half + 1))
                        for k in range(4):
                            src = u_raw[:, m % 2, lo + k:lo + k + L // 2]
                            w = conv_w[:, k, m:m + 1]
                            if k == 0:
                                ins = dve.tensor_scalar(dst, src, w, None, ALU.mult)
                            else:
                                ins = dve.scalar_tensor_tensor(dst, src, w, dst, ALU.mult, ALU.add)
                            if k < 3:
                                dve.wait_ge(tap_done, tap.on(ins))
                        ins.then_inc(conv, 1)
                for c in range(NCH):
                    dve.wait_ge(xp_done, c + 1)
                    dve.tensor_copy(dbl[:, c * BANK:(c + 1) * BANK], ps[0:DTR + 2 * NST, 4 + c % 4, :]).then_inc(dbl_ready, 1)

                def add_one(q):
                    buf = views[q % NSETS]
                    dve.wait_ge(e_ready, q + 1)
                    dve.tensor_scalar(buf[1], buf[0], 1.0, None, ALU.add).then_inc(w_ready, 1)

                def correct(q):
                    buf = views[q % NSETS]
                    dve.wait_ge(w_ready, q + 1)
                    dve.scalar_tensor_tensor(buf[0], buf[1], -1.0, buf[0], ALU.add, ALU.subtract).then_inc(half_ready, 1)
                    dve.wait_ge(half_ready, q + 1)
                    dve.wait_ge(dt_read, q + 1)
                    dve.tensor_tensor(buf[3], buf[3], buf[0], ALU.subtract).then_inc(rest_ready, 1)

                def finish(q):
                    buf = views[q % NSETS]
                    dve.wait_ge(rest_ready, q + 1)
                    dve.wait_ge(ln_ready, q + 1)
                    dve.tensor_tensor(buf[2], buf[2], buf[3], ALU.add).then_inc(delta_ready, 1)

                for q in range(NQ + 1):
                    if q < NQ:
                        add_one(q)
                    if q >= 1:
                        finish(q - 1)
                    if q < NQ:
                        correct(q)


class Attention:

    def __init__(self, ph, keep, dram, b, units, s_bufs, o_bufs):
        self.keep, self.units, self.steps = keep, units, len(units) * KT
        self.s_bufs, self.o_bufs = s_bufs, o_bufs
        self.order = list(dict.fromkeys(h for h, _ in units))
        self.kv_bufs, self.q_bufs = min(2, len(self.order)), min(2, len(units))
        if not units:
            return
        pick = lambda name: dram[name][ds(b, 1)]
        self.dq = pick("q").rearrange("a s c l -> (a s) c l")
        self.dk = pick("k").rearrange("a s c l -> (a s) c l")
        self.dv = pick("v").rearrange("a h p t c -> (a h) p t c")
        self.do = pick("o").rearrange("a c l -> (a c) l")
        self.dden = pick("den").rearrange("a h l -> (a h) l")
        self.k = ph.sb("k", [2 * HD, self.kv_bufs, L], F16)
        self.v = ph.sb("v", [128, self.kv_bufs, KT, VROW])
        self.q = ph.sb("q", [2 * HD, self.q_bufs, 2, TC], F16)
        self.p = ph.sb("p", [128, 3, TC])
        self.o = ph.sb("o", [VROW + HD + 1, o_bufs, BANK])
        self.s_ps = ph.ps("s", [128, s_bufs, TC])
        self.o_ps = ph.ps("o", [128, o_bufs, BANK])
        self.loaded = [ph.sem(f"attn_in{i}") for i in range(2)]
        self.loads = [0, 0]
        self.ones, self.s_ready, self.p_ready = ph.sem("v_ones"), ph.sem("s_ready"), ph.sem("p_ready")
        self.pv_done, self.o_ready = ph.sem("pv_done"), ph.sem("o_ready")
        self.stored = [ph.sem(f"o_stored{i}") for i in range(o_bufs)]

    def unit(self, i):
        h, chunk = self.units[i]
        return slice(h * HD, (h + 1) * HD), chunk * TC, self.order.index(h) % self.kv_bufs, i % self.q_bufs

    def new_head(self, i):
        return i == 0 or self.units[i][0] != self.units[i - 1][0]

    def need(self, i):
        return sum(16 * (7 if self.new_head(j) else 4) for j in range(i % 2, i + 1, 2))

    def load(self, sp, i):
        rows, col, kv, qb = self.unit(i)
        sem = self.loaded[i % 2]
        if i >= 2:
            sp.wait_ge(self.pv_done, KT * (i - 1))
        for half in range(2):
            dst = slice(half * HD, (half + 1) * HD)
            if self.new_head(i):
                sp.dma_start(self.k[dst, kv, :], self.dk[half, rows, :]).then_inc(sem, 16)
            for part in range(2):
                sp.dma_start(self.q[dst, qb, part, :], self.dq[part, rows, ds(col, TC)]).then_inc(sem, 16)
        if self.new_head(i):
            sp.dma_start(self.v[:, kv, :, 0:HD], self.dv[self.units[i][0]]).then_inc(sem, 16)

    def store(self, sp, i):
        rows, col, _, _ = self.unit(i)
        h, buf = self.units[i][0], i % self.o_bufs
        sp.wait_ge(self.o_ready, i + 1)
        for half in range(2):
            sp.dma_start(self.do[rows, ds(col + half * BANK, BANK)],
                         self.o[half * VROW:half * VROW + HD, buf, :]).then_inc(self.stored[buf], 16)
            sp.dma_start(self.dden[h:h + 1, ds(col + half * BANK, BANK)],
                         self.o[half * VROW + HD:half * VROW + HD + 1, buf, :]).then_inc(self.stored[buf], 16)

    def end(self, sp):
        for buf in range(self.o_bufs if self.units else 0):
            sp.wait_ge(self.stored[buf], 64 * len(range(buf, len(self.units), self.o_bufs)))

    def ones_beside_v(self, pool):
        if self.units:
            pool.memset(self.v[:, :, :, HD + 1:], 0.0)
            pool.memset(self.v[:, :, :, HD:HD + 1], 1.0).then_inc(self.ones, 1)

    def scores(self, pe, g):
        i, t = divmod(g, KT)
        _, _, kv, qb = self.unit(i)
        if t == 0:
            pe.wait_ge(self.loaded[i % 2], self.need(i))
        if g >= self.s_bufs:
            pe.wait_ge(self.p_ready, g - self.s_bufs + 1)
        for half in range(2):
            cols = slice(half * BANK, (half + 1) * BANK)
            for part in range(2):
                mm = pe.matmul(self.s_ps[:, g % self.s_bufs, cols], self.k[:, kv, t * 128:(t + 1) * 128],
                               self.q[:, qb, part, cols], start=(part == 0), stop=(part == 1))
        mm.then_inc(self.s_ready, 1)

    def weigh(self, pe, g):
        i, t = divmod(g, KT)
        kv = self.unit(i)[2]
        if g == 0:
            pe.wait_ge(self.ones, 1)
        pe.wait_ge(self.p_ready, g + 1)
        if t == 0 and i >= self.o_bufs:
            pe.wait_ge(self.o_ready, i - self.o_bufs + 1)
        for half in range(2):
            mm = pe.matmul(self.o_ps[half * VROW:(half + 1) * VROW, i % self.o_bufs, :], self.v[:, kv, t, :],
                           self.p[:, g % 3, half * BANK:(half + 1) * BANK], start=(t == 0), stop=(t == KT - 1))
        mm.then_inc(self.pv_done, 1)

    def tensor(self, pe, g):
        self.scores(pe, g)
        if g >= 2:
            self.weigh(pe, g - 2)
        if g == self.steps - 1:
            self.weigh(pe, g - 1)
            self.weigh(pe, g)

    def scalar(self, act, g):
        h = self.units[g // KT][0]
        act.wait_ge(self.s_ready, g + 1)
        if g >= 3:
            act.wait_ge(self.pv_done, g - 2)
        act.activation(self.p[:, g % 3, :], self.s_ps[:, g % self.s_bufs, :], ACT.Exp,
                       bias=self.keep["temp"][:, 1, h:h + 1], scale=self.keep["temp"][:, 0, h:h + 1]
                       ).then_inc(self.p_ready, 1)

    def finished(self, g):
        if g == self.steps - 1:
            return g // KT
        return g // KT - 1 if g % KT == 1 and g > KT else None

    def wait_sums(self, eng, i):
        eng.wait_ge(self.pv_done, KT * (i + 1))
        if i >= self.o_bufs:
            eng.wait_ge(self.stored[i % self.o_bufs], 64 * (i // self.o_bufs))

    def sums(self, i):
        return self.o[:, i % self.o_bufs, :], self.o_ps[0:VROW + HD + 1, i % self.o_bufs, :]

    def read_by_vector(self, dve, i):
        self.wait_sums(dve, i)
        dve.tensor_copy(*self.sums(i)).then_inc(self.o_ready, 1)

    def read_by_scalar(self, act, i):
        self.wait_sums(act, i)
        act.activation(*self.sums(i), ACT.Copy).then_inc(self.o_ready, 1)


def scan_and_attend(nc, keep, dram, b, scan, heads):
    with Phase(nc, "mix") as ph:
        units = [(h, j) for h in heads for j in range(NTC)]
        att = Attention(ph, keep, dram, b, units, 3, 2)
        NS = NST * DB
        ALL = NS * NTC
        NG, NU = att.steps, len(units)
        chunk_in = [[ph.sem(f"chunk_in{i}_{m}") for m in range(DB)] for i in range(2)]
        y_stored = [ph.sem(f"y_stored{i}") for i in range(2)]
        BCS = 3
        bc_in = [ph.sem(f"bc_in{i}") for i in range(BCS)]
        du_done, y_init, da_ready = ph.sem("du_done"), ph.sem("y_init"), ph.sem("da_ready")
        dbu_ready, h_ready, hc_ready = ph.sem("dbu_ready"), ph.sem("h_ready"), ph.sem("hc_ready")
        y_done, carried, cleared = ph.sem("y_done"), ph.sem("carried"), ph.sem("cleared")
        if scan:
            delta = ph.sb("delta", [128, 2, DB, TC])
            du = ph.sb("du", [128, 2, DB, TC])
            y = ph.sb("y", [128, 2, DB, TC])
            bc = ph.sb("bc", [128, BCS, 2, TC])
            da = ph.sb("da", [128, 3, TC])
            xs = ph.sb("in_out", [128, 4, TC])
            hs = ph.sb("h", [128, 3, TC])
            carry = ph.sb("carry", [128, NS])
        read_at = [min(ALL * (i + 1) // NU + DB, ALL) for i in range(NU)]
        swap_at = [min(NST * NTC * (2 * i + 1) // (2 * NU) + BCS, NST * NTC - 1) for i in range(NU)]

        def split(s):
            j, r = divmod(s, NS)
            return j, r // DB, r % DB, s // DB

        def token(name, j):
            return dram[name].rearrange("m p l -> p m l")[:, :, j * TC:(j + 1) * TC]

        def load_chunk(sp, j, m):
            if j >= 2:
                sp.wait_ge(h_ready, (j - 1) * NS)
            sp.dma_start(delta[:, j % 2, m, :], token("delta", j)[:, m, :]).then_inc(chunk_in[j % 2][m], 16)
            sp.dma_start(du[:, j % 2, m, :], token("u", j)[:, m, :]).then_inc(chunk_in[j % 2][m], 16)

        def load_bc(sp, a):
            if a >= BCS:
                sp.wait_ge(hc_ready, (a - BCS + 1) * DB)
            j, n = divmod(a, NST)
            for i in range(2):
                src = dram["bc"][i * NST + n:i * NST + n + 1, j * TC:(j + 1) * TC]
                sp.dma_start(bc[:, a % BCS, i, :], src.partition_broadcast(128).rearrange("p a l -> p (a l)")
                             ).then_inc(bc_in[a % BCS], 16)

        def store_y(sp, j):
            sp.wait_ge(y_done, NS * (j + 1))
            sp.dma_start(token("y", j), y[:, j % 2, :, :]).then_inc(y_stored[j % 2], 16)

        with nc.Block(no_gpsimd_drain=True) as block:

            @block.sync
            def _(sp):
                def swap_units(i):
                    if i >= 1:
                        att.store(sp, i - 1)
                        if i + 1 < NU:
                            att.load(sp, i + 1)

                if scan:
                    load_chunk(sp, 0, 0)
                    load_bc(sp, 0)
                    for m in range(1, DB):
                        load_chunk(sp, 0, m)
                    for a in range(1, NST * NTC):
                        load_bc(sp, a)
                        if a in swap_at:
                            swap_units(swap_at.index(a))
                        if a % NST == 4 and a // NST + 1 < NTC:
                            for m in range(DB):
                                load_chunk(sp, a // NST + 1, m)
                        if a % NST == 2 and a >= NST:
                            store_y(sp, a // NST - 1)
                    store_y(sp, NTC - 1)
                    for i in range(2):
                        sp.wait_ge(y_stored[i], 16 * len(range(i, NTC, 2)))
                else:
                    for i in range(NU):
                        swap_units(i)
                if NU:
                    att.store(sp, NU - 1)
                    att.end(sp)

            @block.tensor
            def _(pe):
                for g in range(NG):
                    att.tensor(pe, g)

            @block.scalar
            def _(act):
                def decay(s):
                    j, n, m, _ = split(s)
                    if n == 0:
                        act.wait_ge(chunk_in[j % 2][m], 32 * (j // 2 + 1))
                    if s >= 3:
                        act.wait_ge(h_ready, s - 2)
                    act.activation(da[:, s % 3, :], delta[:, j % 2, m, :], ACT.Exp,
                                   scale=keep["a"][:, m, n:n + 1]).then_inc(da_ready, 1)

                ahead = min(3, ALL) if NU else ALL
                for i in range(min(2, NU)):
                    att.load(act, i)
                if scan:
                    for s in range(ahead):
                        decay(s)
                for g in range(NG):
                    if scan:
                        for s in share(g, NG, ALL - ahead):
                            decay(s + ahead)
                    att.scalar(act, g)

            @block.gpsimd
            def _(pool):
                att.ones_beside_v(pool)
                if not scan:
                    return
                for s in range(ALL):
                    j, _, m, _ = split(s)
                    col = s % NS
                    pool.wait_ge(h_ready, s + 1)
                    pool.tensor_copy(carry[:, col:col + 1], hs[:, s % 3, TC - 1:TC]).then_inc(carried, 1)
                    pool.wait_ge(hc_ready, s + 1)
                    if col < DB:
                        pool.wait_ge(y_init, DB * j + m + 1)
                    else:
                        pool.wait_ge(y_done, s - DB + 1)
                    pool.tensor_tensor(y[:, j % 2, m, :], y[:, j % 2, m, :], xs[:, s % 4, :], ALU.add).then_inc(y_done, 1)

            @block.vector
            def _(dve):
                if not scan:
                    for i in range(NU):
                        att.read_by_vector(dve, i)
                    return

                def start_block(j, m):
                    i = DB * j + m
                    dve.wait_ge(chunk_in[j % 2][m], 32 * (j // 2 + 1))
                    if j >= 2:
                        dve.wait_ge(y_stored[j % 2], 16 * (j // 2))
                    dve.tensor_scalar(y[:, j % 2, m, :], du[:, j % 2, m, :], keep["inner"][:, 2, m:m + 1], None,
                                      ALU.mult).then_inc(y_init, 1)
                    dve.wait_ge(y_init, i + 1)
                    dve.tensor_tensor(du[:, j % 2, m, :], delta[:, j % 2, m, :], du[:, j % 2, m, :],
                                      ALU.mult).then_inc(du_done, 1)
                    dve.wait_ge(du_done, i + 1)

                def inflow(s):
                    j, n, m, a = split(s)
                    if n == 0:
                        start_block(j, m)
                    dve.wait_ge(bc_in[a % BCS], 32 * (a // BCS + 1))
                    if s >= 4:
                        dve.wait_ge(y_done, s - 3)
                    dve.tensor_tensor(xs[:, s % 4, :], du[:, j % 2, m, :], bc[:, a % BCS, 0, :], ALU.mult).then_inc(dbu_ready, 1)

                def recur(s):
                    col = s % NS
                    dve.wait_ge(da_ready, s + 1)
                    dve.wait_ge(dbu_ready, s + 1)
                    if s >= 3:
                        dve.wait_ge(hc_ready, s - 2)
                        dve.wait_ge(carried, s - 2)
                    dve.tensor_tensor_scan(hs[:, s % 3, :], da[:, s % 3, :], xs[:, s % 4, :],
                                           carry[:, col:col + 1], ALU.mult, ALU.add).then_inc(h_ready, 1)

                def outflow(s):
                    a = split(s)[3]
                    dve.wait_ge(h_ready, s + 1)
                    dve.tensor_tensor(xs[:, s % 4, :], hs[:, s % 3, :], bc[:, a % BCS, 1, :], ALU.mult).then_inc(hc_ready, 1)

                dve.memset(carry[:, :], 0.0).then_inc(cleared, 1)
                dve.wait_ge(cleared, 1)
                for s in range(-1, ALL + 1):
                    if s + 1 < ALL:
                        inflow(s + 1)
                    if 0 <= s < ALL:
                        recur(s)
                    if s >= 1:
                        outflow(s - 1)
                        if s in read_at:
                            att.read_by_vector(dve, read_at.index(s))


def layer0_finish(nc, io, keep, dram, x, b, units):
    with Phase(nc, "l0post") as ph:
        y_in = ph.sb("y_in", [128, L])
        z_in = ph.sb("z_in", [128, L])
        pad = ph.sb("pad", [128, DB, PADW, PADW])
        acc = ph.sb("acc", [128, 2, DB, TC])
        ps = ph.ps("ps", [128, 3, BANK])
        att = Attention(ph, keep, dram, b - 1, units, 2, 1)
        x_in, border = ph.sem("x_in"), ph.sem("border")
        yz_in = [ph.sem("yz_in0"), ph.sem("yz_in1")]
        gated, tap, conv = ph.sem("gated"), ph.sem("tap"), ph.sem("conv")
        tile_done, x1_ready, stored = ph.sem("tile_done"), ph.sem("x1_ready"), ph.sem("stored")
        QROWS = TC // W
        PER = TC // BANK
        NT = NTC * NCB * PER

        def place(t):
            quarter, rest = divmod(t, NCB * PER)
            mo, c = divmod(rest, PER)
            col = quarter * TC + c * BANK
            return quarter, mo, slice(col, col + BANK), slice(c * BANK, (c + 1) * BANK)

        with nc.Block(no_gpsimd_drain=True) as block:

            @block.sync
            def _(sp):
                for m in range(DB):
                    for half in range(2):
                        cols = slice(half * L // 2, (half + 1) * L // 2)
                        if m >= 1:
                            sp.wait_ge(gated, 2 * (2 * (m - 1) + half + 1))
                        sp.dma_start(y_in[:, cols], dram["y"][m][:, cols]).then_inc(yz_in[half], 16)
                        sp.dma_start(z_in[:, cols], dram["z"][m][:, cols]).then_inc(yz_in[half], 16)
                    if m == 0:
                        for i in range(min(2, len(units))):
                            att.load(sp, i)
                sp.dma_start(x[:, :, :], io["x"][ds(b, 1)].rearrange("a (k p) l -> p (a k) l", p=CB)).then_inc(x_in, 16)
                for i in range(len(units)):
                    att.store(sp, i)
                dst = dram["x1"][ds(b, 1)].rearrange("a k p l -> p (a k) l")
                for quarter in range(NTC):
                    sp.wait_ge(x1_ready, NCB * PER * (quarter + 1))
                    cols = slice(quarter * TC, (quarter + 1) * TC)
                    sp.dma_start(dst[:, :, cols], x[:, :, cols]).then_inc(stored, 16)
                sp.wait_ge(stored, 16 * NTC)
                att.end(sp)

            @block.gpsimd
            def _(pool):
                for m in range(DB):
                    pool.memset(pad[:, m, 0::PADW - 1, :], 0.0)
                    pool.memset(pad[:, m, 1:H + 1, 0::PADW - 1], 0.0).then_inc(border, 1)
                att.ones_beside_v(pool)

            @block.tensor
            def _(pe):
                for g in range(att.steps):
                    att.tensor(pe, g)
                for t in range(NT):
                    quarter, mo, _, cols = place(t)
                    pe.wait_ge(conv, max(DB * (quarter + 1), 2 * DB - 1))
                    if t >= 3:
                        pe.wait_ge(x1_ready, t - 2)
                    for k in range(DB):
                        mm = pe.matmul(ps[0:CB, t % 3, :], keep["w_out"][:, k, mo * CB:(mo + 1) * CB],
                                       acc[:, quarter % 2, k, cols], start=(k == 0), stop=(k == DB - 1))
                    mm.then_inc(tile_done, 1)

            @block.scalar
            def _(act):
                for g in range(att.steps):
                    att.scalar(act, g)
                    if (i := att.finished(g)) is not None:
                        att.read_by_scalar(act, i)

            @block.vector
            def _(dve):
                taps = Count(tap)
                def gate(m, half):
                    rows = slice(half * H // 4, (half + 1) * H // 4)
                    inner = pad[:, m, 1:H + 1, 1:W + 1].rearrange("p (r two) w -> p r two w", two=2)[:, rows]
                    yv = y_in[:, :].rearrange("p (r two w) -> p r two w", two=2, w=W)[:, rows]
                    zv = z_in[:, :].rearrange("p (r two w) -> p r two w", two=2, w=W)[:, rows]
                    dve.wait_ge(yz_in[half], 32 * (m + 1))
                    dve.tensor_tensor(inner[:, :, 0, :], yv[:, :, 0, :], zv[:, :, 0, :], ALU.mult).then_inc(gated, 1)
                    dve.tensor_tensor(inner[:, :, 1, :], yv[:, :, 1, ::-1], zv[:, :, 1, :], ALU.mult).then_inc(gated, 1)

                def convolve(quarter, m):
                    dve.wait_ge(gated, 4 * m + (2 if quarter == 0 else 4))
                    dve.wait_ge(border, m + 1)
                    if quarter >= 2:
                        dve.wait_ge(tile_done, NCB * PER * (quarter - 1))
                    dst = acc[:, quarter % 2, m, :].rearrange("p (r w) -> p r w", w=W)
                    for k in range(9):
                        r = quarter * QROWS + k // 3
                        src = pad[:, m, r:r + QROWS, k % 3:k % 3 + W]
                        w = keep["le"][:, m, k:k + 1]
                        if k == 0:
                            ins = dve.tensor_scalar(dst, src, w, None, ALU.mult)
                        else:
                            ins = dve.scalar_tensor_tensor(dst, src, w, dst, ALU.mult, ALU.add)
                        if k < 8:
                            dve.wait_ge(tap, taps.on(ins))
                    ins.then_inc(conv, 1)

                def residual(t):
                    _, mo, cols, _ = place(t)
                    dve.wait_ge(tile_done, t + 1)
                    dve.tensor_tensor(x[:, mo, cols], ps[0:CB, t % 3, :], x[:, mo, cols], ALU.add).then_inc(x1_ready, 1)

                for m in range(DB):
                    gate(m, 0)
                    convolve(0, m)
                    gate(m, 1)
                    convolve(1, m)
                dve.wait_ge(x_in, 16)
                for quarter in range(2, NTC + 2):
                    for m in range(DB):
                        for t in share(m, DB, NCB * PER):
                            residual((quarter - 2) * NCB * PER + t)
                        if quarter < NTC:
                            convolve(quarter, m)


def layer1_project(nc, io, keep, dram, x, b, units):
    with Phase(nc, "l1pre") as ph:
        NB = 3 * NCB
        NQK = 2 * NCB
        NQKV = NB * NCH
        w_qkv = ph.sb("w_qkv", [CB, NCB, 3 * C])
        pad = ph.sb("pad", [CB, 2, PADW, PADW])
        qkv = ph.sb("qkv", [CB, 2, L])
        sq = ph.sb("sq", [CB, 2, TC])
        vt = ph.sb("vt", [128, 2, KT, HD])
        hi = ph.sb("hi", [CB, L], F16)
        lo = ph.sb("lo", [CB, L], F16)
        inv_b = ph.sb("inv_b", [CB, L])
        length = ph.sb("length", [128, 2 * KT])
        inv = ph.sb("inv", [128, 2 * KT])
        inv_t = ph.sb("inv_t", [2 * KT, 128])
        ps = ph.ps("ps", [128, 2, BANK])
        ss_ps = ph.ps("ss", [128, BANK])
        gn = GroupNorm(ph, keep, x, ps[:, 0, :], False)
        att = Attention(ph, keep, dram, b - 1, units, 2, 1)
        w_loaded, x_norm, border = ph.sem("w_loaded"), ph.sem("x_norm"), ph.sem("border")
        tile_done, tile_read = ph.sem("tile_done"), ph.sem("tile_read")
        tap, conv, conv_half = ph.sem("tap"), ph.sem("conv"), ph.sem("conv_half")
        sq_ready, ss_done, root = ph.sem("sq_ready"), ph.sem("ss_done"), ph.sem("root")
        clipped, inv_ready, turned, inv_t_ready = ph.sem("clipped"), ph.sem("inv_ready"), ph.sem("turned"), ph.sem("inv_t_ready")
        inv_stored, inv_b_in = ph.sem("inv_stored"), ph.sem("inv_b_in")
        unit, hi_ready, lo_ready, parts_stored = ph.sem("unit"), ph.sem("hi_ready"), ph.sem("lo_ready"), ph.sem("parts_stored")
        vt_stored = ph.sem("vt_stored")
        b_qkv, b_dw = keep["dw"][:, 9, :], keep["dw"][:, 10, :]
        HALF = L // 2
        AHEAD = att.steps // 8
        BESIDE = att.steps // 12
        BEHIND = (att.steps - AHEAD - (NB - 1) * BESIDE) // (NB - 1)

        def plan():
            yield "attend", range(AHEAD)
            yield "norm", None
            g = AHEAD
            for j in range(NB):
                beside = BESIDE if j else 0
                behind = (att.steps - g - beside if j == NB - 1 else BEHIND) if j >= 1 else 0
                if j >= 2:
                    yield "square", j - 2
                    yield "attend", range(g, g + behind // 2)
                    yield "turn", j - 2
                    g += behind // 2
                    behind -= behind // 2
                yield "project", (j, range(g, g + beside))
                g += beside
                yield "attend", range(g, g + behind)
                g += behind

        with nc.Block(no_gpsimd_drain=True) as block:

            @block.sync
            def _(sp):
                sp.dma_start(w_qkv[:, :, :], io["w_qkv_t"]).then_inc(w_loaded, 16)
                for i in range(min(2, len(units))):
                    att.load(sp, i)
                for j in range(NQK):
                    sp.wait_ge(inv_t_ready, j + 1)
                    sp.dma_start(dram["inv"].rearrange("h (t p) -> (h t) p", p=128)[2 * j * KT:2 * (j + 1) * KT, :],
                                 inv_t[:, :]).then_inc(inv_stored, 16)
                    sp.wait_ge(inv_stored, 16 * (j + 1))
                    if j >= 1:
                        sp.wait_ge(unit, 2 * j)
                    for i in range(2):
                        src = dram["inv"][2 * j + i:2 * j + i + 1, :].partition_broadcast(HD)
                        sp.dma_start(inv_b[i * HD:(i + 1) * HD, :], src.rearrange("p a l -> p (a l)")
                                     ).then_inc(inv_b_in, 16)
                    dst = dram["q" if j < NCB else "k"][ds(b, 1)].rearrange("a s c l -> (a s) c l")
                    for part, (src, ready) in enumerate(((hi, hi_ready), (lo, lo_ready))):
                        sp.wait_ge(ready, 2 * (j + 1))
                        sp.dma_start(dst[part, (j % NCB) * CB:(j % NCB + 1) * CB, :], src[:, :]).then_inc(parts_stored, 16)
                sp.wait_ge(parts_stored, 16 * 2 * NQK)

            @block.gpsimd
            def _(pool):
                for i in range(2):
                    pool.memset(pad[:, i, 0::PADW - 1, :], 0.0)
                    pool.memset(pad[:, i, 1:H + 1, 0::PADW - 1], 0.0).then_inc(border, 1)
                att.ones_beside_v(pool)

            @block.tensor
            def _(pe):
                def project(j, steps):
                    if j == 0:
                        pe.wait_ge(w_loaded, 16)
                        pe.wait_ge(x_norm, NCB)
                    for c in range(NCH):
                        t = j * NCH + c
                        if t >= 2:
                            pe.wait_ge(tile_read, t - 1)
                        for k in range(NCB):
                            mm = pe.matmul(ps[0:CB, t % 2, :], w_qkv[:, k, j * CB:(j + 1) * CB],
                                           x[:, k, c * BANK:(c + 1) * BANK], start=(k == 0), stop=(k == NCB - 1))
                        mm.then_inc(tile_done, 1)
                        for s in share(c, NCH, len(steps)):
                            att.tensor(pe, steps[s])

                def lengths(j):
                    if j >= 1:
                        pe.wait_ge(root, j)
                    out = ss_ps[:, 0:2 * KT].rearrange("p (h t) -> p h t", h=2)
                    for c in range(NTC):
                        pe.wait_ge(sq_ready, j * NTC + c + 1)
                        for i in range(TC // 128):
                            mm = pe.matmul(out[:, :, c * TC // 128 + i], sq[:, c % 2, i * 128:(i + 1) * 128],
                                           keep["head_sum"][:, :], start=True, stop=True)
                        mm.then_inc(ss_done, 1)

                def turn_inverse(j):
                    pe.wait_ge(inv_ready, j + 1)
                    if j >= 1:
                        pe.wait_ge(inv_t_ready, j)
                    pe.transpose(ss_ps[0:2 * KT, 128:256], inv[:, :], keep["ident"][:, :]).then_inc(turned, 1)

                def turn_v(j):
                    for g in range(KT // 4):
                        t = NQKV + j * (KT // 4) + g
                        if j == 1 and g < KT // 8:
                            pe.wait_ge(conv_half, 2)
                        else:
                            pe.wait_ge(conv, NQK + 1 + j)
                        pe.wait_ge(tile_read, t - 1)
                        for i in range(4):
                            col = (4 * g + i) * 128
                            mm = pe.transpose(ps[:, t % 2, i * CB:(i + 1) * CB], qkv[:, j % 2, col:col + 128],
                                              keep["ident"][0:CB, 0:CB])
                        mm.then_inc(tile_done, 1)

                for what, arg in plan():
                    if what == "attend":
                        for g in arg:
                            att.tensor(pe, g)
                    elif what == "norm":
                        gn.tensor(pe)
                    elif what == "project":
                        project(*arg)
                    elif what == "square":
                        lengths(arg)
                    else:
                        turn_inverse(arg)
                for j in range(2):
                    turn_v(j)

            @block.scalar
            def _(act):
                def unload(j, steps):
                    if j == 0:
                        act.wait_ge(border, 2)
                    if j >= 2:
                        act.wait_ge(conv, j - 1)
                    for c in range(NCH):
                        t = j * NCH + c
                        act.wait_ge(tile_done, t + 1)
                        act.activation(pad[:, j % 2, 1 + c * ROWS:1 + (c + 1) * ROWS, 1:W + 1],
                                       ps[0:CB, t % 2, :].rearrange("p (r w) -> p r w", w=W), ACT.Identity,
                                       bias=b_qkv[:, j:j + 1]).then_inc(tile_read, 1)
                        for s in share(c, NCH, len(steps)):
                            attend(steps[s])

                def attend(g):
                    att.scalar(act, g)
                    if (i := att.finished(g)) is not None:
                        att.read_by_scalar(act, i)
                        att.store(act, i)
                        if i + 2 < len(units):
                            att.load(act, i + 2)

                def lengths(j):
                    act.wait_ge(conv, j + 1)
                    for c in range(NTC):
                        i = j * NTC + c
                        if i >= 2:
                            act.wait_ge(ss_done, i - 1)
                        act.activation(sq[:, c % 2, :], qkv[:, j % 2, c * TC:(c + 1) * TC], ACT.Square).then_inc(sq_ready, 1)
                    act.wait_ge(ss_done, NTC * (j + 1))
                    if j >= 1:
                        act.wait_ge(inv_ready, j)
                    act.activation(length[:, :], ss_ps[:, 0:2 * KT], ACT.Sqrt).then_inc(root, 1)

                def unload_inverse(j):
                    act.wait_ge(turned, j + 1)
                    if j >= 1:
                        act.wait_ge(inv_stored, 16 * j)
                    act.activation(inv_t[:, :], ss_ps[0:2 * KT, 128:256], ACT.Copy).then_inc(inv_t_ready, 1)

                for what, arg in plan():
                    if what == "attend":
                        for g in arg:
                            attend(g)
                    elif what == "norm":
                        gn.scalar(act)
                    elif what == "project":
                        unload(*arg)
                    elif what == "square":
                        lengths(arg)
                    else:
                        unload_inverse(arg)
                for j in range(2):
                    if j == 1:
                        act.wait_ge(vt_stored, 16)
                    for g in range(KT // 4):
                        t = NQKV + j * (KT // 4) + g
                        act.wait_ge(tile_done, t + 1)
                        act.activation(vt[:, :, 4 * g:4 * g + 4, :],
                                       ps[:, t % 2, 0:4 * CB].rearrange("p (i h c) -> p h i c", i=4, h=2),
                                       ACT.Copy).then_inc(tile_read, 1)
                    act.wait_ge(tile_read, NQKV + NCH * (j + 1))
                    dst = dram["v"][ds(b, 1)].rearrange("a h p t c -> p (a h) (t c)")
                    act.dma_start(dst[:, 2 * j:2 * j + 2, :], vt[:, :, :, :].rearrange("p h t c -> p h (t c)")
                                  ).then_inc(vt_stored, 16)
                act.wait_ge(vt_stored, 32)
                att.end(act)

            @block.vector
            def _(dve):
                gn.vector(dve)
                for k in range(NCB):
                    dve.tensor_scalar(x[:, k, :], x[:, k, :], gn.scale[:, k:k + 1], gn.shift[:, k:k + 1],
                                      ALU.mult, ALU.add).then_inc(x_norm, 1)
                taps = Count(tap)

                def convolve(j):
                    halves = 2 if j in (0, NB - 1) else 1
                    for half in range(halves):
                        n = H // halves
                        r0 = half * n
                        dve.wait_ge(tile_read, NCH * j + min(NCH, NCH // halves * (half + 1) + 1))
                        dst = qkv[:, j % 2, r0 * W:(r0 + n) * W].rearrange("p (r w) -> p r w", w=W)
                        for k in range(9):
                            src = pad[:, j % 2, r0 + k // 3:r0 + k // 3 + n, k % 3:k % 3 + W]
                            w = keep["dw"][:, k, j:j + 1]
                            if k == 0:
                                ins = dve.tensor_scalar(dst, src, w, b_dw[:, j:j + 1], ALU.mult, ALU.add)
                            else:
                                ins = dve.scalar_tensor_tensor(dst, src, w, dst, ALU.mult, ALU.add)
                            if k < 8:
                                dve.wait_ge(tap, taps.on(ins))
                            if k == 3 and 1 <= j <= NQK:
                                invert(j - 1)
                        if half < halves - 1:
                            ins.then_inc(conv_half, 1)
                    ins.then_inc(conv, 1)

                def invert(j):
                    dve.wait_ge(root, j + 1)
                    dve.tensor_scalar(length[:, :], length[:, :], 1e-12, 1.0 / QSCALE, ALU.max, ALU.mult).then_inc(clipped, 1)
                    dve.wait_ge(clipped, j + 1)
                    dve.reciprocal(inv[:, :], length[:, :]).then_inc(inv_ready, 1)

                def normalize(j):
                    dve.wait_ge(inv_b_in, 32 * (j + 1))
                    for i in range(2):
                        cols = slice(i * HALF, (i + 1) * HALF)
                        dve.tensor_tensor(qkv[:, j % 2, cols], qkv[:, j % 2, cols], inv_b[:, cols], ALU.mult).then_inc(unit, 1)
                    if j >= 1:
                        dve.wait_ge(parts_stored, 32 * j)
                    for i in range(2):
                        cols = slice(i * HALF, (i + 1) * HALF)
                        dve.wait_ge(unit, 2 * j + i + 1)
                        dve.tensor_copy(hi[:, cols], qkv[:, j % 2, cols]).then_inc(hi_ready, 1)
                    for i in range(2):
                        cols = slice(i * HALF, (i + 1) * HALF)
                        dve.wait_ge(hi_ready, 2 * j + i + 1)
                        dve.tensor_tensor(lo[:, cols], qkv[:, j % 2, cols], hi[:, cols], ALU.subtract).then_inc(lo_ready, 1)

                for j in range(NB):
                    if j >= 2:
                        dve.wait_ge(lo_ready, 2 * (j - 1))
                    convolve(j)
                    if 1 <= j <= NQK:
                        normalize(j - 1)


def layer1_finish(nc, io, keep, dram, b):
    with Phase(nc, "l1post") as ph:
        o = ph.sb("o", [CB, NCB, L])
        r = ph.sb("r", [CB, NCB, L])
        x = ph.sb("x", [CB, NCB, L])
        den = ph.sb("den", [128, HEADS * L // 128])
        ps = ph.ps("ps", [128, 8, BANK])
        den_in, den_inv, inv_stored = ph.sem("den_in"), ph.sem("den_inv"), ph.sem("inv_stored")
        o_in = [ph.sem(f"o_in{i}") for i in range(NTC)]
        r_in = [ph.sem(f"r_in{i}") for i in range(NTC)]
        scaled, tile_done, ready, stored = ph.sem("scaled"), ph.sem("tile_done"), ph.sem("ready"), ph.sem("stored")
        b_proj = keep["chan"][:, 2, :]
        PER = TC // BANK
        NT = NTC * NCB * PER

        def place(t):
            chunk, rest = divmod(t, NCB * PER)
            mo, c = divmod(rest, PER)
            return mo, slice(chunk * TC + c * BANK, chunk * TC + (c + 1) * BANK)

        with nc.Block(no_gpsimd_drain=True) as block:

            @block.sync
            def _(sp):
                d = dram["den"][ds(b, 1)].rearrange("a h (t l) -> (a h t) l", l=128)
                sp.dma_start(den[:, :], d).then_inc(den_in, 16)
                for i in range(NTC):
                    cols = slice(i * TC, (i + 1) * TC)
                    sp.dma_start(o[:, :, cols], dram["o"][ds(b, 1)].rearrange("a (k p) l -> p (a k) l", p=CB)[:, :, cols]
                                 ).then_inc(o_in[i], 16)
                    sp.dma_start(x[:, :, cols], dram["x1"][ds(b, 1)].rearrange("a k p l -> p (a k) l")[:, :, cols]
                                 ).then_inc(o_in[i], 16)
                dst = io["out"][ds(b, 1)].rearrange("a (k p) l -> p (a k) l", p=CB)
                for i in range(NTC):
                    cols = slice(i * TC, (i + 1) * TC)
                    sp.wait_ge(ready, NCB * PER * (i + 1))
                    sp.dma_start(dst[:, :, cols], x[:, :, cols]).then_inc(stored, 16)
                sp.wait_ge(stored, 16 * NTC)

            @block.scalar
            def _(act):
                act.wait_ge(den_inv, 1)
                act.dma_start(dram["rden"].rearrange("h (t l) -> (h t) l", l=128), den[:, :]).then_inc(inv_stored, 16)
                act.wait_ge(inv_stored, 16)
                for i in range(NTC):
                    cols = slice(i * TC, (i + 1) * TC)
                    for h in range(HEADS):
                        k, half = divmod(h, 2)
                        src = dram["rden"][h:h + 1, cols].partition_broadcast(HD).rearrange("p a l -> p (a l)")
                        act.dma_start(r[half * HD:(half + 1) * HD, k, cols], src).then_inc(r_in[i], 16)

            @block.tensor
            def _(pe):
                for t in range(NT):
                    mo, cols = place(t)
                    pe.wait_ge(scaled, t // (NCB * PER) + 1)
                    if t >= 8:
                        pe.wait_ge(ready, t - 7)
                    for k in range(NCB):
                        mm = pe.matmul(ps[0:CB, t % 8, :], keep["w_proj"][:, k, mo * CB:(mo + 1) * CB],
                                       o[:, k, cols], start=(k == 0), stop=(k == NCB - 1))
                    mm.then_inc(tile_done, 1)

            @block.vector
            def _(dve):
                dve.wait_ge(den_in, 16)
                dve.reciprocal(den[:, :], den[:, :]).then_inc(den_inv, 1)

                def scale(i):
                    cols = slice(i * TC, (i + 1) * TC)
                    dve.wait_ge(o_in[i], 32)
                    dve.wait_ge(r_in[i], 16 * HEADS)
                    dve.tensor_tensor(o[:, :, cols], o[:, :, cols], r[:, :, cols], ALU.mult).then_inc(scaled, 1)

                scale(0)
                for i in range(NTC):
                    if i + 1 < NTC:
                        scale(i + 1)
                    for t in range(NCB * PER * i, NCB * PER * (i + 1)):
                        mo, cols = place(t)
                        dve.wait_ge(tile_done, t + 1)
                        dve.scalar_tensor_tensor(x[:, mo, cols], ps[0:CB, t % 8, :], b_proj[:, mo:mo + 1], x[:, mo, cols],
                                                 ALU.add, ALU.add).then_inc(ready, 1)


def build(nc, io):
    batches = io["x"].shape[0]
    scratch = {
        "u": ([DB, 128, L], F32), "z": ([DB, 128, L], F32), "delta": ([DB, 128, L], F32), "y": ([DB, 128, L], F32),
        "bc": ([2 * NST, L], F32), "inv": ([8, L], F32), "rden": ([HEADS, L], F32),
        "x1": ([batches, NCB, CB, L], F32), "q": ([batches, 2, C, L], F16), "k": ([batches, 2, C, L], F16),
        "v": ([batches, HEADS, 128, KT, HD], F32), "o": ([batches, C, L], F32), "den": ([batches, HEADS, L], F32),
    }
    dram = {k: nc.dram_tensor(f"scratch_{k}", shape, dt, kind="Internal").ap() for k, (shape, dt) in scratch.items()}
    kept = {
        "ident": [128, 128], "group_mean": [CB, CB], "all_mean": [CB, CB], "head_sum": [CB, 2],
        "x_proj": [128, DB, DTR + 2 * NST], "dt_proj": [DTR, DB, 128], "w_proj": [CB, NCB, C],
        "chan": [CB, 3, NCB], "inner": [128, 7, DB], "le": [128, DB, 9], "a": [128, DB, NST],
        "dw": [CB, 11, 6], "w_out": [128, DB, C], "temp": [128, 2, HEADS],
    }
    with ExitStack() as ctx:
        keep = {k: ctx.enter_context(nc.sbuf_tensor(f"keep_{k}", shape, F32)) for k, shape in kept.items()}
        setup(nc, io, keep)

        heads, last = range(HEADS), HEADS - 1
        beside_finish = [(last, 0)]
        beside_project = [(last, i) for i in range(1, NTC)]

        def between(b, units0, units1):
            with nc.sbuf_tensor(f"x_between{nc.next_id()}", [CB, NCB, L], F32) as x:
                layer0_finish(nc, io, keep, dram, x, b, units0)
                layer1_project(nc, io, keep, dram, x, b, units1)

        layer0_project(nc, io, keep, dram, 0)
        scan_and_attend(nc, keep, dram, 0, True, [])
        between(0, [], [])
        if batches > 1:
            with nc.Fori(1, batches) as b:
                layer0_project(nc, io, keep, dram, b)
                scan_and_attend(nc, keep, dram, b - 1, True, heads[:last])
                between(b, beside_finish, beside_project)
                layer1_finish(nc, io, keep, dram, b - 1)
        scan_and_attend(nc, keep, dram, batches - 1, False, heads)
        layer1_finish(nc, io, keep, dram, batches - 1)


def lay_out(inputs):
    a = {k.split("_conv_")[-1] if "_conv_" in k else k: np.asarray(v) for k, v in inputs.items()}
    w_dw = a["w_dw"].reshape(3 * C, 9)
    rows = lambda v, p: v.reshape(-1, p).T
    eye = np.eye(128, dtype=np.float32)
    group = np.kron(np.eye(CB // GROUP, dtype=np.float32), np.full((GROUP, GROUP), 1.0 / GROUP, np.float32))
    heads = np.kron(np.eye(2, dtype=np.float32), np.ones((HD, 1), np.float32))
    blocks = lambda w, p: w.reshape(-1, p, w.shape[1]).transpose(1, 0, 2)
    inner = np.stack([rows(a["conv1d_b"], 128), rows(a["dt_proj_b"], 128), rows(a["Dskip"], 128)]
                     + [rows(a["conv1d_w"][:, k], 128) for k in range(4)], axis=1)
    dw = np.stack([rows(w_dw[:, k], CB) for k in range(9)] + [rows(a["b_qkv"], CB), rows(a["b_dw"], CB)], axis=1)
    return {
        "x": a["x"].reshape(-1, C, L),
        "ident": eye,
        "group_mean": group,
        "all_mean": np.full((CB, CB), 1.0 / C, np.float32),
        "head_sum": heads,
        "in_proj_t": blocks(a["in_proj_w"].T, CB),
        "x_proj_t": blocks(a["x_proj_w"].T, 128),
        "dt_proj_t": a["dt_proj_w"].T.reshape(DTR, DB, 128),
        "out_proj": blocks(a["out_proj_w"], CB),
        "proj_out_t": blocks(a["proj_out_w"].T, CB),
        "w_qkv_t": blocks(a["w_qkv"].T, CB),
        "w_proj_t": blocks(a["w_proj"].T, CB),
        "chan": np.stack([rows(a["gn_gamma"], CB), rows(a["gn_beta"], CB), rows(a["b_proj"], CB)], axis=1),
        "inner": inner,
        "le": blocks(a["le_w"].reshape(DIN, 9), 128),
        "a_log": blocks(a["A_log"], 128),
        "dw": dw,
        "temperature": a["temperature"].reshape(HEADS),
    }


def kernel(**inputs):
    import concourse.bacc as bacc
    from concourse.bass_utils import run_bass_kernel_spmd

    nc = bacc.Bacc("TRN2", target_bir_lowering=False, num_devices=1)
    arrays, io = {}, {}
    for name, a in lay_out(inputs).items():
        a = np.ascontiguousarray(a)
        arrays[f"in_{name}"] = a
        io[name] = nc.dram_tensor(f"in_{name}", a.shape, mybir.dt.from_np(a.dtype), kind="ExternalInput").ap()
    batches = io["x"].shape[0]
    io["out"] = nc.dram_tensor("out", (batches, C, L), F32, kind="ExternalOutput").ap()
    build(nc, io)
    r = run_bass_kernel_spmd(nc, [arrays], core_ids=[0])
    return r.results[0]["out"].reshape(batches, C, H, W)
```

```python
from contextlib import ExitStack

import concourse.bass as bass
import numpy as np
from concourse import mybir

F32 = mybir.dt.float32
F16 = mybir.dt.float16
ALU = mybir.AluOpType
ACT = mybir.ActivationFunctionType
ds = bass.ds

C = 192
H = W = 64
L = H * W
CB = 96
NCB = C // CB
DIN = 2 * C
DB = DIN // 128
NST = 16
DTR = 12
GROUP = C // 32
HEADS = 4
HD = C // HEADS
BANK = 512
NCH = L // BANK
ROWS = BANK // W
TC = 1024
NTC = L // TC
KT = L // 128
PADW = W + 2
QSCALE = 64.0
VROW = 64
SHIFT_FREE = 60.0


class Count:

    def __init__(self, sem):
        self.sem, self.n = sem, 0

    def on(self, ins, by=1):
        ins.then_inc(self.sem, by)
        self.n += by
        return self.n


def end_phase(nc, sems):
    for s in sems:
        nc.sync.sem_clear(s)
    nc.all_engine_barrier()


class Phase:

    def __init__(self, nc, name):
        self.nc, self.name, self.ctx, self.sems = nc, f"{name}{nc.next_id()}", ExitStack(), []

    def __enter__(self):
        self.ctx.__enter__()
        return self

    def __exit__(self, *e):
        if e[0] is None:
            end_phase(self.nc, self.sems)
        return self.ctx.__exit__(*e)

    def sb(self, name, shape, dt=F32):
        return self.ctx.enter_context(self.nc.sbuf_tensor(f"{self.name}_{name}", shape, dt))

    def ps(self, name, shape):
        return self.ctx.enter_context(self.nc.psum_tensor(f"{self.name}_ps_{name}", shape, F32))

    def sem(self, name):
        s = self.ctx.enter_context(self.nc.semaphore(f"{self.name}_{name}"))
        self.sems.append(s)
        return s


def setup(nc, io, keep):
    with Phase(nc, "setup") as ph:
        op_w = ph.sb("out_proj", [CB, NCB, DIN])
        po_w = ph.sb("proj_out", [CB, NCB, C])
        temp = ph.sb("temp", [128, HEADS])
        tabs = ph.sb("tabs", [128, HEADS])
        comb_ps = ph.ps("comb", [128, DB, BANK])
        loaded, combined, a_exp, tmp = ph.sem("loaded"), ph.sem("combined"), ph.sem("a_exp"), ph.sem("tmp")
        loads = [
            (keep["ident"][:, :], io["ident"]),
            (keep["group_mean"][:, :], io["group_mean"]),
            (keep["all_mean"][:, :], io["all_mean"]),
            (keep["head_sum"][:, :], io["head_sum"]),
            (keep["x_proj"][:, :, :], io["x_proj_t"]),
            (keep["dt_proj"][:, :, :], io["dt_proj_t"]),
            (keep["w_proj"][:, :, :], io["w_proj_t"]),
            (keep["chan"][:, :, :], io["chan"]),
            (keep["inner"][:, :, :], io["inner"]),
            (keep["le"][:, :, :], io["le"]),
            (keep["a"][:, :, :], io["a_log"]),
            (keep["dw"][:, :, :], io["dw"]),
            (op_w[:, :, :], io["out_proj"]),
            (po_w[:, :, :], io["proj_out_t"]),
            (temp[:, :], io["temperature"].partition_broadcast(128)),
        ]
        with nc.Block() as block:

            @block.sync
            def _(sp):
                for dst, src in loads:
                    sp.dma_start(dst, src).then_inc(loaded, 16)

            @block.tensor
            def _(pe):
                pe.wait_ge(loaded, 16 * len(loads))
                for m in range(DB):
                    for k in range(NCB):
                        mm = pe.matmul(comb_ps[:, m, 0:C], op_w[:, k, m * 128:(m + 1) * 128], po_w[:, k, :],
                                       start=(k == 0), stop=(k == NCB - 1))
                mm.then_inc(combined, 1)

            @block.scalar
            def _(act):
                act.wait_ge(loaded, 16 * len(loads))
                act.activation(keep["a"][:, :, :], keep["a"][:, :, :], ACT.Exp).then_inc(a_exp, 1)

            @block.vector
            def _(dve):
                dve.wait_ge(loaded, 16 * len(loads))
                dve.tensor_scalar(keep["le"][:, :, 4:5], keep["le"][:, :, 4:5], 1.0, None, ALU.add)
                dve.tensor_scalar(keep["temp"][:, 0, :], temp[:, :], 1.0 / QSCALE ** 2, None, ALU.mult)
                dve.tensor_scalar(tabs[:, :], temp[:, :], -1.0, None, ALU.mult).then_inc(tmp, 1)
                dve.wait_ge(tmp, 1)
                dve.tensor_tensor(tabs[:, :], tabs[:, :], temp[:, :], ALU.max).then_inc(tmp, 1)
                dve.wait_ge(tmp, 2)
                dve.tensor_scalar(tabs[:, :], tabs[:, :], -1.0, SHIFT_FREE, ALU.mult, ALU.add).then_inc(tmp, 1)
                dve.wait_ge(tmp, 3)
                dve.tensor_scalar(keep["temp"][:, 1, :], tabs[:, :], 0.0, None, ALU.min)
                dve.wait_ge(a_exp, 1)
                dve.tensor_scalar(keep["a"][:, :, :], keep["a"][:, :, :], -1.0, None, ALU.mult)
                dve.wait_ge(combined, 1)
                dve.tensor_copy(keep["w_out"][:, :, :], comb_ps[:, :, 0:C])


def share(i, n, total):
    return range(total * i // n, total * (i + 1) // n)


def load_image(q, dst, src, sem):
    for k in range(NCB):
        for half in range(2):
            cols = slice(half * L // 2, (half + 1) * L // 2)
            q.dma_start(dst[:, k, cols], src[:, k, cols]).then_inc(sem[2 * k + half], 16)


class GroupNorm:

    EPS = 1e-5

    def __init__(self, ph, keep, x, ps, whole, chunk_stats=None):
        self.keep, self.x, self.ps, self.whole = keep, x, ps, whole
        self.x_in = [ph.sem(f"x_in{i}") for i in range(2 * NCB)] if whole else []
        self.chunk_stats = ph.sb("chunk_stats", [CB, NCB, NCH, 6]) if whole else chunk_stats
        self.mv = ph.sb("mean_var", [CB, NCB, 2])
        self.chan = ph.sb("chan_stats", [CB, 2, NCB])
        self.grp = ph.sb("group_stats", [CB, 2, NCB])
        self.tmp = ph.sb("stats_tmp", [CB, NCB])
        self.std = ph.sb("std", [CB, NCB])
        self.scale = ph.sb("gn_scale", [CB, NCB])
        self.shift = ph.sb("gn_shift", [CB, NCB])
        self.tot = ph.sb("total", [CB, 2])
        self.rows = ph.sem("chan_stats_ready")
        self.means = ph.sem("means_ready")
        self.var = ph.sem("var_ready")
        self.root = ph.sem("root_ready")
        self.step = ph.sem("stats_step")

    def tensor(self, pe):
        pe.wait_ge(self.rows, 1)
        pe.matmul(self.ps[0:CB, 0:2 * NCB], self.keep["group_mean"][:, :],
                  self.chan[:, :, :].rearrange("p a b -> p (a b)"), start=True, stop=True).then_inc(self.means, 1)
        if self.whole:
            pe.wait_ge(self.rows, 2)
            for k in range(NCB):
                mm = pe.matmul(self.ps[0:CB, 0:2], self.keep["all_mean"][:, :], self.chan[:, :, k],
                               start=(k == 0), stop=(k == NCB - 1))
            mm.then_inc(self.means, 1)

    def scalar(self, act):
        act.wait_ge(self.var, 1)
        act.activation(self.std[:, :], self.tmp[:, :], ACT.Sqrt).then_inc(self.root, 1)
        if self.whole:
            act.wait_ge(self.var, 2)
            act.activation(self.std[:, 0:1], self.tmp[:, 0:1], ACT.Sqrt).then_inc(self.root, 1)

    def vector(self, dve):
        step = Count(self.step)

        def then(ins):
            dve.wait_ge(self.step, step.on(ins))

        if self.whole:
            for k in range(NCB):
                for c in range(NCH):
                    if c % (NCH // 2) == 0:
                        dve.wait_ge(self.x_in[2 * k + c // (NCH // 2)], 16)
                    ins = dve.bn_stats(self.chunk_stats[:, k, c, :], self.x[:, k, c * BANK:(c + 1) * BANK])
            then(ins)
        for k in range(NCB):
            ins = dve.bn_aggr(self.mv[:, k, :], self.chunk_stats[:, k, :, :].rearrange("p c s -> p (c s)"))
        then(ins)
        mean, var = self.mv[:, :, 0], self.mv[:, :, 1]
        step.on(dve.tensor_copy(self.chan[:, 0, :], mean))
        then(dve.tensor_tensor(self.tmp[:, :], mean, mean, ALU.mult))
        dve.tensor_tensor(self.chan[:, 1, :], self.tmp[:, :], var, ALU.add).then_inc(self.rows, 1)
        dve.wait_ge(self.rows, 1)
        dve.wait_ge(self.means, 1)
        then(dve.tensor_copy(self.grp[:, :, :], self.ps[0:CB, 0:2 * NCB].rearrange("p (a b) -> p a b", a=2)))
        gm, gsq = self.grp[:, 0, :], self.grp[:, 1, :]
        then(dve.tensor_tensor(self.std[:, :], gm, gm, ALU.mult))
        dve.scalar_tensor_tensor(self.tmp[:, :], gsq, self.EPS, self.std[:, :], ALU.add, ALU.subtract).then_inc(self.var, 1)
        dve.wait_ge(self.var, 1)
        dve.wait_ge(self.root, 1)
        then(dve.reciprocal(self.scale[:, :], self.std[:, :]))
        then(dve.scalar_tensor_tensor(self.shift[:, :], gm, -1.0, self.scale[:, :], ALU.mult, ALU.mult))
        if not self.whole:
            return
        then(dve.tensor_tensor(self.tmp[:, :], mean, self.scale[:, :], ALU.mult))
        then(dve.tensor_tensor(self.chan[:, 0, :], self.tmp[:, :], self.shift[:, :], ALU.add))
        then(dve.tensor_tensor(self.tmp[:, :], self.chan[:, 0, :], self.chan[:, 0, :], ALU.mult))
        then(dve.tensor_tensor(self.chan[:, 1, :], self.scale[:, :], self.scale[:, :], ALU.mult))
        then(dve.tensor_tensor(self.chan[:, 1, :], self.chan[:, 1, :], var, ALU.mult))
        dve.tensor_tensor(self.chan[:, 1, :], self.chan[:, 1, :], self.tmp[:, :], ALU.add).then_inc(self.rows, 1)
        dve.wait_ge(self.rows, 2)
        dve.wait_ge(self.means, 2)
        then(dve.tensor_copy(self.tot[:, :], self.ps[0:CB, 0:2]))
        then(dve.tensor_tensor(self.std[:, 0:1], self.tot[:, 0:1], self.tot[:, 0:1], ALU.mult))
        dve.scalar_tensor_tensor(self.tmp[:, 0:1], self.tot[:, 1:2], self.EPS, self.std[:, 0:1],
                                 ALU.add, ALU.subtract).then_inc(self.var, 1)
        dve.wait_ge(self.var, 2)
        dve.wait_ge(self.root, 2)
        then(dve.reciprocal(self.std[:, 1:2], self.std[:, 0:1]))
        gamma, beta = self.keep["chan"][:, 0, :], self.keep["chan"][:, 1, :]
        r = self.std[:, 1:2]
        then(dve.scalar_tensor_tensor(self.scale[:, :], self.scale[:, :], r, gamma, ALU.mult, ALU.mult))
        then(dve.tensor_scalar(self.shift[:, :], self.shift[:, :], self.tot[:, 0:1], r, ALU.subtract, ALU.mult))
        then(dve.tensor_tensor(self.shift[:, :], self.shift[:, :], gamma, ALU.mult))
        then(dve.tensor_tensor(self.shift[:, :], self.shift[:, :], beta, ALU.add))


def layer0_project(nc, io, keep, dram, b):
    with Phase(nc, "l0pre") as ph:
        x = ph.sb("x", [CB, NCB, L])
        w_in = ph.sb("in_proj", [CB, NCB, 2 * DIN])
        u_raw = ph.sb("u_raw", [128, 2, L + 3])
        u_c = ph.sb("u_conv", [128, DB, L])
        z_s = ph.sb("z_silu", [128, 2, L])
        dbl = ph.sb("dbl", [DTR + 2 * NST, L])
        ps = ph.ps("ps", [128, 8, BANK])
        gn = GroupNorm(ph, keep, x, ps[:, 0, :], True)
        w_in_in, x_norm = ph.sem("w_in_loaded"), ph.sem("x_norm")
        tile_done, tile_read = ph.sem("tile_done"), ph.sem("tile_read")
        pads, conv, u_ready = ph.sem("pads"), ph.sem("conv"), ph.sem("u_ready")
        z_stored = [ph.sem("z_stored0"), ph.sem("z_stored1")]
        xp_done, dbl_ready = ph.sem("x_proj_done"), ph.sem("dbl_ready")
        dt_done, dt_read, dt_abs = ph.sem("dt_done"), ph.sem("dt_read"), ph.sem("dt_abs")
        e_ready, w_ready, ln_ready = ph.sem("e_ready"), ph.sem("w_ready"), ph.sem("ln_ready")
        tap_done, half_ready, rest_ready = ph.sem("tap_done"), ph.sem("half_ready"), ph.sem("rest_ready")
        delta_ready = ph.sem("delta_ready")
        delta_stored = [ph.sem(f"delta_stored{i}") for i in range(4)]
        u_stored, bc_stored = ph.sem("u_stored"), ph.sem("bc_stored")
        NT = 2 * DB * NCH
        NEARLY = (DB + 1) * NCH
        NQ = DB * NTC
        NSETS = 4
        views = [[t[:, r, i * TC:(i + 1) * TC] for i in range(4)] for t in (u_raw, u_c) for r in range(2)]
        conv_b, dt_b = keep["inner"][:, 0, :], keep["inner"][:, 1, :]
        conv_w = keep["inner"][:, 3:7, :]

        def dt_result(q):
            return ps[:, 4 + 2 * (q % 2):6 + 2 * (q % 2), :].rearrange("p a b -> p (a b)")

        with nc.Block() as block:

            @block.sync
            def _(sp):
                load_image(sp, x, io["x"][ds(b, 1)].rearrange("a (k p) l -> p (a k) l", p=CB), gn.x_in)
                sp.dma_start(w_in[:, :, :], io["in_proj_t"]).then_inc(w_in_in, 16)
                for m in range(DB):
                    sp.wait_ge(u_ready, 2 * (m + 1))
                    sp.dma_start(dram["u"][m], u_c[:, m, :]).then_inc(u_stored, 16)
                sp.wait_ge(dbl_ready, NCH)
                sp.dma_start(dram["bc"], dbl[DTR:, :]).then_inc(bc_stored, 16)
                for q in range(NQ):
                    m, c = divmod(q, NTC)
                    sp.wait_ge(delta_ready, q + 1)
                    sp.dma_start(dram["delta"][m][:, c * TC:(c + 1) * TC], views[q % NSETS][2]
                                 ).then_inc(delta_stored[q % NSETS], 16)
                sp.wait_ge(u_stored, 16 * DB)
                sp.wait_ge(bc_stored, 16)
                sp.wait_ge(z_stored[0], 32)
                sp.wait_ge(z_stored[1], 16)
                for s in delta_stored:
                    sp.wait_ge(s, 16 * NQ // NSETS)

            @block.tensor
            def _(pe):
                gn.tensor(pe)
                pe.wait_ge(w_in_in, 16)
                pe.wait_ge(x_norm, NCB)

                def project(t):
                    m, c = divmod(t, NCH)
                    if t >= 4:
                        pe.wait_ge(tile_read, t - 3)
                    if t == NEARLY:
                        pe.wait_ge(dbl_ready, NCH)
                    for k in range(NCB):
                        mm = pe.matmul(ps[:, t % 4, :], w_in[:, k, m * 128:(m + 1) * 128],
                                       x[:, k, c * BANK:(c + 1) * BANK], start=(k == 0), stop=(k == NCB - 1))
                    mm.then_inc(tile_done, 1)

                for t in range(NEARLY):
                    project(t)
                for c in range(0, NCH, 2):
                    pe.wait_ge(u_ready, 2 * DB - 1 if c < NCH // 2 else 2 * DB)
                    for k in range(DB):
                        for i in range(2):
                            mm = pe.matmul(ps[64 * i:64 * i + DTR + 2 * NST, 4 + c // 2, :], keep["x_proj"][:, k, :],
                                           u_c[:, k, (c + i) * BANK:(c + i + 1) * BANK], start=(k == 0), stop=(k == DB - 1))
                    mm.then_inc(xp_done, 2)
                pe.wait_ge(dbl_ready, NCH)
                for q in range(NQ):
                    m, chunk = divmod(q, NTC)
                    if q >= 2:
                        pe.wait_ge(dt_read, q - 1)
                    for c in range(2):
                        col = chunk * TC + c * BANK
                        mm = pe.matmul(ps[:, 4 + 2 * (q % 2) + c, :], keep["dt_proj"][:, m, :],
                                       dbl[0:DTR, col:col + BANK], start=True, stop=True)
                    mm.then_inc(dt_done, 1)
                    if q % 4 == 3:
                        for t in share(q // 4, NQ // 4, NT - NEARLY):
                            project(NEARLY + t)

            @block.scalar
            def _(act):
                gn.scalar(act)

                def unload_u(m):
                    if m == 0:
                        act.wait_ge(pads, 1)
                    if m >= 2:
                        act.wait_ge(conv, 2 * (m - 1))
                    for c in range(NCH):
                        t = m * NCH + c
                        act.wait_ge(tile_done, t + 1)
                        src = ps[:, t % 4, :].rearrange("p (r two w) -> p r two w", two=2, w=W)
                        dst = u_raw[:, m % 2, 3 + c * BANK:3 + (c + 1) * BANK].rearrange(
                            "p (r two w) -> p r two w", two=2, w=W)
                        act.activation(dst[:, :, 0, :], src[:, :, 0, :], ACT.Copy)
                        act.activation(dst[:, :, 1, :], src[:, :, 1, ::-1], ACT.Copy).then_inc(tile_read, 1)

                def silu_u(m):
                    for half in range(2):
                        cols = slice(half * L // 2, (half + 1) * L // 2)
                        act.wait_ge(conv, 2 * m + half + 1)
                        act.activation(u_c[:, m, cols], u_c[:, m, cols], ACT.Silu, bias=conv_b[:, m:m + 1]).then_inc(u_ready, 1)

                def silu_z(t):
                    m, c = t // NCH - DB, t % NCH
                    if m >= 2 and c == 0:
                        act.wait_ge(z_stored[m % 2], 16)
                    act.wait_ge(tile_done, t + 1)
                    act.activation(z_s[:, m % 2, c * BANK:(c + 1) * BANK], ps[:, t % 4, :], ACT.Silu).then_inc(tile_read, 1)
                    if c == NCH - 1:
                        act.wait_ge(tile_read, t + 1)
                        act.dma_start(dram["z"][m], z_s[:, m % 2, :]).then_inc(z_stored[m % 2], 16)

                unload_u(0)
                unload_u(1)
                silu_u(0)
                unload_u(2)
                silu_u(1)
                for t in range(DB * NCH, NEARLY):
                    silu_z(t)
                silu_u(2)

                def magnitude(q):
                    m, buf = q // NTC, views[q % NSETS]
                    v = dt_result(q)
                    act.wait_ge(dt_done, q + 1)
                    if q >= NSETS:
                        act.wait_ge(delta_ready, q - NSETS + 1)
                        act.wait_ge(delta_stored[q % NSETS], 16 * (q // NSETS))
                    elif q == 2:
                        act.wait_ge(u_stored, 16 * DB)
                    act.activation(buf[0], v, ACT.Abs, bias=dt_b[:, m:m + 1]).then_inc(dt_abs, 1)

                def decay(q):
                    buf = views[q % NSETS]
                    act.wait_ge(dt_abs, q + 1)
                    act.activation(buf[0], buf[0], ACT.Exp, scale=-1.0).then_inc(e_ready, 1)

                def softplus_ln(q):
                    buf = views[q % NSETS]
                    act.wait_ge(w_ready, q + 1)
                    act.activation(buf[2], buf[1], ACT.Ln).then_inc(ln_ready, 1)

                for q in range(0, NQ + 2, 2):
                    if q < NQ:
                        magnitude(q)
                        magnitude(q + 1)
                        decay(q)
                        decay(q + 1)
                    if q >= 2:
                        softplus_ln(q - 2)
                        softplus_ln(q - 1)
                    if q % 4 == 2 and q < NQ:
                        for t in share(q // 4, NQ // 4, NT - NEARLY):
                            silu_z(NEARLY + t)

            @block.vector
            def _(dve):
                dve.memset(u_raw[:, :, 0:3], 0.0).then_inc(pads, 1)
                gn.vector(dve)
                for k in range(NCB):
                    dve.tensor_scalar(x[:, k, :], x[:, k, :], gn.scale[:, k:k + 1], gn.shift[:, k:k + 1],
                                      ALU.mult, ALU.add).then_inc(x_norm, 1)
                tap = Count(tap_done)
                for m in range(DB):
                    order = [(k, half) for half in range(2) for k in range(4)]
                    last = {}
                    for k, half in order if m in (0, DB - 1) else sorted(order):
                        lo = half * L // 2
                        dst = u_c[:, m, lo:lo + L // 2]
                        src = u_raw[:, m % 2, lo + k:lo + k + L // 2]
                        w = conv_w[:, k, m:m + 1]
                        if k == 0:
                            dve.wait_ge(tile_read, NCH * m + NCH // 2 * (half + 1))
                            ins = dve.tensor_scalar(dst, src, w, None, ALU.mult)
                        else:
                            dve.wait_ge(tap_done, last[half])
                            ins = dve.scalar_tensor_tensor(dst, src, w, dst, ALU.mult, ALU.add)
                        if k < 3:
                            last[half] = tap.on(ins)
                        else:
                            ins.then_inc(conv, 1)
                for c in range(NCH):
                    dve.wait_ge(xp_done, c + 1)
                    rows = slice(64 * (c % 2), 64 * (c % 2) + DTR + 2 * NST)
                    dve.tensor_copy(dbl[:, c * BANK:(c + 1) * BANK], ps[rows, 4 + c // 2, :]).then_inc(dbl_ready, 1)

                def positive(q):
                    m = q // NTC
                    dve.wait_ge(dt_abs, q + 1)
                    if q >= NSETS:
                        dve.wait_ge(delta_ready, q - NSETS + 1)
                    elif q == 2:
                        dve.wait_ge(u_stored, 16 * DB)
                    dve.tensor_scalar(views[q % NSETS][3], dt_result(q), dt_b[:, m:m + 1], 0.0, ALU.add, ALU.max
                                      ).then_inc(dt_read, 1)

                def add_one(q):
                    buf = views[q % NSETS]
                    dve.wait_ge(e_ready, q + 1)
                    dve.tensor_scalar(buf[1], buf[0], 1.0, None, ALU.add).then_inc(w_ready, 1)

                def correct(q):
                    buf = views[q % NSETS]
                    dve.wait_ge(w_ready, q + 1)
                    dve.scalar_tensor_tensor(buf[0], buf[1], -1.0, buf[0], ALU.add, ALU.subtract).then_inc(half_ready, 1)
                    dve.wait_ge(half_ready, q + 1)
                    dve.wait_ge(dt_read, q + 1)
                    dve.tensor_tensor(buf[3], buf[3], buf[0], ALU.subtract).then_inc(rest_ready, 1)

                def finish(q):
                    buf = views[q % NSETS]
                    dve.wait_ge(rest_ready, q + 1)
                    dve.wait_ge(ln_ready, q + 1)
                    dve.tensor_tensor(buf[2], buf[2], buf[3], ALU.add).then_inc(delta_ready, 1)

                for q in range(0, NQ + 2, 2):
                    for i in (q, q + 1) if q < NQ else ():
                        positive(i)
                    for i in (q, q + 1) if q < NQ else ():
                        add_one(i)
                    for i in (q - 2, q - 1) if q >= 2 else ():
                        finish(i)
                    for i in (q, q + 1) if q < NQ else ():
                        correct(i)


class Attention:

    def __init__(self, ph, keep, dram, b, units, s_bufs, o_bufs):
        self.keep, self.units, self.steps = keep, units, len(units) * KT
        self.s_bufs, self.o_bufs = s_bufs, o_bufs
        self.order = list(dict.fromkeys(h for h, _ in units))
        self.kv_bufs, self.q_bufs = min(2, len(self.order)), min(2, len(units))
        if not units:
            return
        pick = lambda name: dram[name][ds(b, 1)]
        self.dq = pick("q").rearrange("a s c l -> (a s) c l")
        self.dk = pick("k").rearrange("a s c l -> (a s) c l")
        self.dv = pick("v").rearrange("a h p t c -> (a h) p t c")
        self.do = pick("o").rearrange("a c l -> (a c) l")
        self.dden = pick("den").rearrange("a h l -> (a h) l")
        self.k = ph.sb("k", [2 * HD, self.kv_bufs, L], F16)
        self.v = ph.sb("v", [128, self.kv_bufs, KT, VROW])
        self.q = ph.sb("q", [2 * HD, self.q_bufs, 2, TC], F16)
        self.p = ph.sb("p", [128, 3, TC])
        self.o = ph.sb("o", [VROW + HD + 1, o_bufs, BANK])
        self.s_ps = ph.ps("s", [128, s_bufs, TC])
        self.o_ps = ph.ps("o", [128, o_bufs, BANK])
        self.loaded = [ph.sem(f"attn_in{i}") for i in range(2)]
        self.ones, self.s_ready, self.p_ready = ph.sem("v_ones"), ph.sem("s_ready"), ph.sem("p_ready")
        self.pv_done, self.o_ready = ph.sem("pv_done"), ph.sem("o_ready")
        self.stored = [ph.sem(f"o_stored{i}") for i in range(o_bufs)]

    def unit(self, i):
        h, chunk = self.units[i]
        return slice(h * HD, (h + 1) * HD), chunk * TC, self.order.index(h) % self.kv_bufs, i % self.q_bufs

    def new_head(self, i):
        return i == 0 or self.units[i][0] != self.units[i - 1][0]

    def need(self, i):
        return sum(16 * (7 if self.new_head(j) else 4) for j in range(i % 2, i + 1, 2))

    def load(self, sp, i):
        rows, col, kv, qb = self.unit(i)
        sem = self.loaded[i % 2]
        if i >= 2:
            sp.wait_ge(self.pv_done, KT * (i - 1))
        for half in range(2):
            dst = slice(half * HD, (half + 1) * HD)
            if self.new_head(i):
                sp.dma_start(self.k[dst, kv, :], self.dk[half, rows, :]).then_inc(sem, 16)
            for part in range(2):
                sp.dma_start(self.q[dst, qb, part, :], self.dq[part, rows, ds(col, TC)]).then_inc(sem, 16)
        if self.new_head(i):
            sp.dma_start(self.v[:, kv, :, 0:HD], self.dv[self.units[i][0]]).then_inc(sem, 16)

    def store(self, sp, i):
        rows, col, _, _ = self.unit(i)
        h, buf = self.units[i][0], i % self.o_bufs
        sp.wait_ge(self.o_ready, i + 1)
        for half in range(2):
            sp.dma_start(self.do[rows, ds(col + half * BANK, BANK)],
                         self.o[half * VROW:half * VROW + HD, buf, :]).then_inc(self.stored[buf], 16)
            sp.dma_start(self.dden[h:h + 1, ds(col + half * BANK, BANK)],
                         self.o[half * VROW + HD:half * VROW + HD + 1, buf, :]).then_inc(self.stored[buf], 16)

    def end(self, sp):
        for buf in range(self.o_bufs if self.units else 0):
            sp.wait_ge(self.stored[buf], 64 * len(range(buf, len(self.units), self.o_bufs)))

    def ones_beside_v(self, pool):
        if self.units:
            pool.memset(self.v[:, :, :, HD + 1:], 0.0)
            pool.memset(self.v[:, :, :, HD:HD + 1], 1.0).then_inc(self.ones, 1)

    def scores(self, pe, g):
        i, t = divmod(g, KT)
        _, _, kv, qb = self.unit(i)
        if t == 0:
            pe.wait_ge(self.loaded[i % 2], self.need(i))
        if g >= self.s_bufs:
            pe.wait_ge(self.p_ready, g - self.s_bufs + 1)
        for half in range(2):
            cols = slice(half * BANK, (half + 1) * BANK)
            for part in range(2):
                mm = pe.matmul(self.s_ps[:, g % self.s_bufs, cols], self.k[:, kv, t * 128:(t + 1) * 128],
                               self.q[:, qb, part, cols], start=(part == 0), stop=(part == 1))
        mm.then_inc(self.s_ready, 1)

    def weigh(self, pe, g):
        i, t = divmod(g, KT)
        kv = self.unit(i)[2]
        if g == 0:
            pe.wait_ge(self.ones, 1)
        pe.wait_ge(self.p_ready, g + 1)
        if t == 0 and i >= self.o_bufs:
            pe.wait_ge(self.o_ready, i - self.o_bufs + 1)
        for half in range(2):
            mm = pe.matmul(self.o_ps[half * VROW:(half + 1) * VROW, i % self.o_bufs, :], self.v[:, kv, t, :],
                           self.p[:, g % 3, half * BANK:(half + 1) * BANK], start=(t == 0), stop=(t == KT - 1))
        mm.then_inc(self.pv_done, 1)

    def tensor(self, pe, g):
        self.scores(pe, g)
        if g >= 2:
            self.weigh(pe, g - 2)
        if g == self.steps - 1:
            self.weigh(pe, g - 1)
            self.weigh(pe, g)

    def scalar(self, act, g):
        h = self.units[g // KT][0]
        act.wait_ge(self.s_ready, g + 1)
        if g >= 3:
            act.wait_ge(self.pv_done, g - 2)
        act.activation(self.p[:, g % 3, :], self.s_ps[:, g % self.s_bufs, :], ACT.Exp,
                       bias=self.keep["temp"][:, 1, h:h + 1], scale=self.keep["temp"][:, 0, h:h + 1]
                       ).then_inc(self.p_ready, 1)

    def finished(self, g):
        if g == self.steps - 1:
            return g // KT
        return g // KT - 1 if g % KT == 1 and g > KT else None

    def wait_sums(self, eng, i):
        eng.wait_ge(self.pv_done, KT * (i + 1))
        if i >= self.o_bufs:
            eng.wait_ge(self.stored[i % self.o_bufs], 64 * (i // self.o_bufs))

    def sums(self, i):
        return self.o[:, i % self.o_bufs, :], self.o_ps[0:VROW + HD + 1, i % self.o_bufs, :]

    def read_by_vector(self, dve, i):
        self.wait_sums(dve, i)
        dve.tensor_copy(*self.sums(i)).then_inc(self.o_ready, 1)

    def read_by_scalar(self, act, i):
        self.wait_sums(act, i)
        act.activation(*self.sums(i), ACT.Copy).then_inc(self.o_ready, 1)


def scan_alone(nc, keep, dram):
    with Phase(nc, "scan") as ph:
        NS = NST * DB
        ALL = NS * NTC
        R = 3
        delta = ph.sb("delta", [128, 2, DB, TC])
        u = ph.sb("u", [128, 2, DB, TC])
        du = ph.sb("du", [128, 2, DB, TC])
        y = ph.sb("y", [128, DB, TC])
        bc = ph.sb("bc", [128, R, 2, TC])
        da = ph.sb("da", [128, R, TC])
        dbu = ph.sb("dbu", [128, R, TC])
        h = ph.sb("h", [128, R, TC])
        hc = ph.sb("hc", [128, R, TC])
        carry = ph.sb("carry", [128, NS])
        skip = ph.sb("skip", [128, DB, 128])
        YS = 4
        sums = ph.ps("y", [128, YS, TC])
        chunk_in = [[ph.sem(f"chunk_in{i}_{m}") for m in range(DB)] for i in range(2)]
        bc_in = [ph.sem(f"bc_in{i}") for i in range(R)]
        y_stored = [ph.sem(f"y_stored{m}") for m in range(DB)]
        prepared, du_ready, da_ready = ph.sem("prepared"), ph.sem("du_ready"), ph.sem("da_ready")
        dbu_ready, h_ready, hc_ready = ph.sem("dbu_ready"), ph.sem("h_ready"), ph.sem("hc_ready")
        summed, y_ready, carried = ph.sem("summed"), ph.sem("y_ready"), ph.sem("carried")

        def split(s):
            j, r = divmod(s, NS)
            return j, r // DB, r % DB, s // DB

        def load_chunk(sp, j, m):
            if j >= 2:
                sp.wait_ge(summed, (j - 1) * NS)
            for dst, name in ((delta, "delta"), (u, "u")):
                sp.dma_start(dst[:, j % 2, m, :], dram[name][m, :, j * TC:(j + 1) * TC]).then_inc(chunk_in[j % 2][m], 16)

        def load_bc(sp, a):
            if a >= R:
                sp.wait_ge(hc_ready, (a - R + 1) * DB)
            j, n = divmod(a, NST)
            for i in range(2):
                src = dram["bc"][i * NST + n:i * NST + n + 1, j * TC:(j + 1) * TC]
                sp.dma_start(bc[:, a % R, i, :], src.partition_broadcast(128).rearrange("p a l -> p (a l)")
                             ).then_inc(bc_in[a % R], 16)

        def store_y(sp, i):
            j, m = divmod(i, DB)
            sp.wait_ge(y_ready, i + 1)
            sp.dma_start(dram["y"][m, :, j * TC:(j + 1) * TC], y[:, m, :]).then_inc(y_stored[m], 16)

        with nc.Block(no_gpsimd_drain=True) as block:

            @block.sync
            def _(sp):
                load_chunk(sp, 0, 0)
                load_bc(sp, 0)
                for m in range(1, DB):
                    load_chunk(sp, 0, m)
                for a in range(1, NST * NTC):
                    load_bc(sp, a)
                    j, n = divmod(a, NST)
                    if n == R + 1 and j >= 1:
                        for m in range(DB):
                            store_y(sp, (j - 1) * DB + m)
                    if n == R + 2 and j + 1 < NTC:
                        for m in range(DB):
                            load_chunk(sp, j + 1, m)
                for m in range(DB):
                    store_y(sp, (NTC - 1) * DB + m)
                for m in range(DB):
                    sp.wait_ge(y_stored[m], 16 * NTC)

            @block.tensor
            def _(pe):
                pe.wait_ge(prepared, 1)
                for s in range(ALL):
                    j, n, m, _ = split(s)
                    i = j * DB + m
                    if n == 0:
                        pe.wait_ge(chunk_in[j % 2][m], 32 * (j // 2 + 1))
                        if i >= YS:
                            pe.wait_ge(y_ready, i - YS + 1)
                        for c in range(0, TC, BANK):
                            pe.matmul(sums[:, i % YS, c:c + BANK], skip[:, m, :], u[:, j % 2, m, c:c + BANK],
                                      start=True, stop=False)
                    pe.wait_ge(hc_ready, s + 1)
                    for c in range(0, TC, BANK):
                        mm = pe.matmul(sums[:, i % YS, c:c + BANK], keep["ident"][:, :], hc[:, s % R, c:c + BANK],
                                       start=False, stop=(n == NST - 1))
                    mm.then_inc(summed, 1)

            @block.scalar
            def _(act):
                def decay(s):
                    j, n, m, _ = split(s)
                    if n == 0:
                        act.wait_ge(chunk_in[j % 2][m], 32 * (j // 2 + 1))
                    act.activation(da[:, s % R, :], delta[:, j % 2, m, :], ACT.Exp,
                                   scale=keep["a"][:, m, n:n + 1]).then_inc(da_ready, 1)

                for s in range(R):
                    decay(s)
                act.wait_ge(prepared, 1)
                for s in range(ALL):
                    j, n, m, _ = split(s)
                    col, i = s % NS, j * DB + m
                    act.wait_ge(h_ready, s + 1)
                    act.activation(carry[:, col:col + 1], h[:, s % R, TC - 1:TC], ACT.Copy).then_inc(carried, 1)
                    if s + R < ALL:
                        decay(s + R)
                    if n == NST - 1:
                        act.wait_ge(summed, s + 1)
                        if j >= 1:
                            act.wait_ge(y_stored[m], 16 * j)
                        act.activation(y[:, m, :], sums[:, i % YS, :], ACT.Copy).then_inc(y_ready, 1)

            @block.vector
            def _(dve):
                def inflow(s):
                    j, n, m, a = split(s)
                    if n == 0:
                        i = DB * j + m
                        dve.wait_ge(chunk_in[j % 2][m], 32 * (j // 2 + 1))
                        if j >= 2:
                            dve.wait_ge(dbu_ready, (j - 1) * NS)
                        dve.tensor_tensor(du[:, j % 2, m, :], delta[:, j % 2, m, :], u[:, j % 2, m, :],
                                          ALU.mult).then_inc(du_ready, 1)
                        dve.wait_ge(du_ready, i + 1)
                    dve.wait_ge(bc_in[a % R], 32 * (a // R + 1))
                    if s >= R:
                        dve.wait_ge(h_ready, s - R + 1)
                    dve.tensor_tensor(dbu[:, s % R, :], du[:, j % 2, m, :], bc[:, a % R, 0, :], ALU.mult).then_inc(dbu_ready, 1)

                def recur(s):
                    col = s % NS
                    dve.wait_ge(da_ready, s + 1)
                    dve.wait_ge(dbu_ready, s + 1)
                    if s >= R:
                        dve.wait_ge(hc_ready, s - R + 1)
                        dve.wait_ge(carried, s - R + 1)
                    dve.tensor_tensor_scan(h[:, s % R, :], da[:, s % R, :], dbu[:, s % R, :], carry[:, col:col + 1],
                                           ALU.mult, ALU.add).then_inc(h_ready, 1)

                def outflow(s):
                    a = split(s)[3]
                    dve.wait_ge(h_ready, s + 1)
                    if s >= R:
                        dve.wait_ge(summed, s - R + 1)
                    dve.tensor_tensor(hc[:, s % R, :], h[:, s % R, :], bc[:, a % R, 1, :], ALU.mult).then_inc(hc_ready, 1)

                dve.memset(carry[:, :], 0.0)
                for m in range(DB):
                    ins = dve.tensor_scalar(skip[:, m, :], keep["ident"][:, :], keep["inner"][:, 2, m:m + 1], None, ALU.mult)
                ins.then_inc(prepared, 1)
                dve.wait_ge(prepared, 1)
                for s in range(-1, ALL + 1):
                    if s + 1 < ALL:
                        inflow(s + 1)
                    if 0 <= s < ALL:
                        recur(s)
                    if s >= 1:
                        outflow(s - 1)


def scan_and_attend(nc, keep, dram, b, scan, units):
    with Phase(nc, "mix") as ph:
        att = Attention(ph, keep, dram, b, units, *((2, 1) if scan else (3, 2)))
        NS = NST * DB
        ALL = NS * NTC
        PIECES = TC // BANK
        NG, NU = att.steps, len(units)
        chunk_in = [[ph.sem(f"chunk_in{i}_{m}") for m in range(DB)] for i in range(2)]
        y_stored = [ph.sem(f"y_stored{i}") for i in range(2)]
        BCS = 3
        bc_in = [ph.sem(f"bc_in{i}") for i in range(BCS)]
        du_done, y_init, da_ready = ph.sem("du_done"), ph.sem("y_init"), ph.sem("da_ready")
        dbu_ready, h_ready, hc_ready = ph.sem("dbu_ready"), ph.sem("h_ready"), ph.sem("hc_ready")
        y_done, carried, cleared = ph.sem("y_done"), ph.sem("carried"), ph.sem("cleared")
        if scan:
            delta = ph.sb("delta", [128, 2, DB, TC])
            du = ph.sb("du", [128, 2, DB, TC])
            y = ph.sb("y", [128, 2, DB, TC])
            bc = ph.sb("bc", [128, BCS, 2, TC])
            da = ph.sb("da", [128, 3, TC])
            hc = ph.sb("hc", [128, 3, TC])
            h = ph.ps("h", [128, 3, BANK])
            carry = ph.sb("carry", [128, NS])
        swap_at = [min(NST * NTC * (2 * i + 1) // (2 * NU) + BCS, NST * NTC - 1) for i in range(NU)]

        def split(s):
            j, r = divmod(s, NS)
            return j, r // DB, r % DB, s // DB

        def place(q):
            s, i = divmod(q, PIECES)
            return s, slice(i * BANK, (i + 1) * BANK)

        def token(name, j):
            return dram[name].rearrange("m p l -> p m l")[:, :, j * TC:(j + 1) * TC]

        def load_chunk(sp, j, m):
            if j >= 2:
                sp.wait_ge(h_ready, (j - 1) * NS * PIECES)
            sp.dma_start(delta[:, j % 2, m, :], token("delta", j)[:, m, :]).then_inc(chunk_in[j % 2][m], 16)
            sp.dma_start(du[:, j % 2, m, :], token("u", j)[:, m, :]).then_inc(chunk_in[j % 2][m], 16)

        def load_bc(sp, a):
            if a >= BCS:
                sp.wait_ge(hc_ready, (a - BCS + 1) * DB * PIECES)
            j, n = divmod(a, NST)
            for i in range(2):
                src = dram["bc"][i * NST + n:i * NST + n + 1, j * TC:(j + 1) * TC]
                sp.dma_start(bc[:, a % BCS, i, :], src.partition_broadcast(128).rearrange("p a l -> p (a l)")
                             ).then_inc(bc_in[a % BCS], 16)

        def store_y(sp, j):
            for m in range(DB):
                sp.wait_ge(y_done, (NS * (j + 1) - DB + m + 1) * PIECES)
                sp.dma_start(token("y", j)[:, m, :], y[:, j % 2, m, :]).then_inc(y_stored[j % 2], 16)

        with nc.Block(no_gpsimd_drain=True) as block:

            @block.sync
            def _(sp):
                def swap_units(i):
                    if i >= 1:
                        att.store(sp, i - 1)
                        if i + 1 < NU:
                            att.load(sp, i + 1)

                if scan:
                    load_chunk(sp, 0, 0)
                    load_bc(sp, 0)
                    for m in range(1, DB):
                        load_chunk(sp, 0, m)
                    for a in range(1, NST * NTC):
                        load_bc(sp, a)
                        if a in swap_at:
                            swap_units(swap_at.index(a))
                        if a % NST == 4 and a // NST + 1 < NTC:
                            for m in range(DB):
                                load_chunk(sp, a // NST + 1, m)
                        if a % NST == 2 and a >= NST:
                            store_y(sp, a // NST - 1)
                    store_y(sp, NTC - 1)
                else:
                    for i in range(NU):
                        swap_units(i)
                if NU:
                    att.store(sp, NU - 1)
                if scan:
                    for i in range(2):
                        sp.wait_ge(y_stored[i], 16 * DB * len(range(i, NTC, 2)))
                att.end(sp)

            @block.tensor
            def _(pe):
                for g in range(NG):
                    att.tensor(pe, g)

            @block.scalar
            def _(act):
                def decay(s):
                    j, n, m, _ = split(s)
                    if n == 0:
                        act.wait_ge(chunk_in[j % 2][m], 32 * (j // 2 + 1))
                        if j >= 2:
                            act.wait_ge(y_stored[j % 2], 16 * DB * (j // 2))
                        act.activation(y[:, j % 2, m, :], du[:, j % 2, m, :], ACT.Copy,
                                       scale=keep["inner"][:, 2, m:m + 1]).then_inc(y_init, 1)
                    if s >= 3:
                        act.wait_ge(h_ready, (s - 2) * PIECES)
                    act.activation(da[:, s % 3, :], delta[:, j % 2, m, :], ACT.Exp,
                                   scale=keep["a"][:, m, n:n + 1]).then_inc(da_ready, 1)

                ahead = min(3, ALL) if NU else ALL
                for i in range(min(2, NU)):
                    att.load(act, i)
                if scan:
                    for s in range(ahead):
                        decay(s)
                for g in range(NG):
                    if scan:
                        for s in share(g, NG, ALL - ahead):
                            decay(s + ahead)
                    att.scalar(act, g)
                    if scan and att.finished(g) is not None:
                        att.read_by_scalar(act, att.finished(g))

            @block.gpsimd
            def _(pool):
                att.ones_beside_v(pool)
                if not scan:
                    return
                for q in range(ALL * PIECES):
                    s, cols = place(q)
                    j, n, m, _ = split(s)
                    pool.wait_ge(hc_ready, q + 1)
                    if n == 0:
                        pool.wait_ge(y_init, DB * j + m + 1)
                    else:
                        pool.wait_ge(y_done, q + 1 - DB * PIECES)
                    pool.tensor_tensor(y[:, j % 2, m, cols], y[:, j % 2, m, cols], hc[:, s % 3, cols],
                                       ALU.add).then_inc(y_done, 1)

            @block.vector
            def _(dve):
                if not scan:
                    for i in range(NU):
                        att.read_by_vector(dve, i)
                    return

                def start_block(j, m):
                    i = DB * j + m
                    dve.wait_ge(chunk_in[j % 2][m], 32 * (j // 2 + 1))
                    dve.wait_ge(y_init, i + 1)
                    dve.tensor_tensor(du[:, j % 2, m, :], delta[:, j % 2, m, :], du[:, j % 2, m, :],
                                      ALU.mult).then_inc(du_done, 1)
                    dve.wait_ge(du_done, i + 1)

                def inflow(q):
                    s, cols = place(q)
                    j, n, m, a = split(s)
                    if cols.start == 0:
                        if n == 0:
                            start_block(j, m)
                        dve.wait_ge(bc_in[a % BCS], 32 * (a // BCS + 1))
                    if q >= 3:
                        dve.wait_ge(hc_ready, q - 2)
                        dve.wait_ge(carried, q - 2)
                    dve.tensor_tensor(h[:, q % 3, :], du[:, j % 2, m, cols], bc[:, a % BCS, 0, cols],
                                      ALU.mult).then_inc(dbu_ready, 1)

                def recur(q):
                    s, cols = place(q)
                    col = s % NS
                    dve.wait_ge(da_ready, s + 1)
                    dve.wait_ge(dbu_ready, q + 1)
                    if cols.start > 0:
                        dve.wait_ge(carried, q)
                    elif s >= NS:
                        dve.wait_ge(carried, q - NS * PIECES + PIECES)
                    dve.tensor_tensor_scan(h[:, q % 3, :], da[:, s % 3, cols], h[:, q % 3, :], carry[:, col:col + 1],
                                           ALU.mult, ALU.add).then_inc(h_ready, 1)

                def keep_last(q):
                    col = place(q)[0] % NS
                    dve.wait_ge(h_ready, q + 1)
                    dve.tensor_copy(carry[:, col:col + 1], h[:, q % 3, BANK - 1:BANK]).then_inc(carried, 1)

                def outflow(q):
                    s, cols = place(q)
                    a = split(s)[3]
                    dve.wait_ge(h_ready, q + 1)
                    if s >= 3:
                        dve.wait_ge(y_done, q + 1 - 3 * PIECES)
                    dve.tensor_tensor(hc[:, s % 3, cols], h[:, q % 3, :], bc[:, a % BCS, 1, cols],
                                      ALU.mult).then_inc(hc_ready, 1)

                dve.memset(carry[:, :], 0.0).then_inc(cleared, 1)
                dve.wait_ge(cleared, 1)
                inflow(0)
                for q in range(ALL * PIECES):
                    recur(q)
                    if q + 1 < ALL * PIECES:
                        inflow(q + 1)
                    keep_last(q)
                    if q >= 1:
                        outflow(q - 1)
                outflow(ALL * PIECES - 1)


def layer0_finish(nc, io, keep, dram, x, x_stats, b, units):
    with Phase(nc, "l0post") as ph:
        y_in = ph.sb("y_in", [128, L])
        z_in = ph.sb("z_in", [128, L])
        pad = ph.sb("pad", [128, DB, PADW, PADW])
        acc = ph.sb("acc", [128, 2, DB, TC])
        ps = ph.ps("ps", [128, 3, BANK])
        att = Attention(ph, keep, dram, b - 1, units, 2, 1)
        x_in, border = ph.sem("x_in"), ph.sem("border")
        yz_in = [ph.sem("yz_in0"), ph.sem("yz_in1")]
        gated, tap, conv = ph.sem("gated"), ph.sem("tap"), ph.sem("conv")
        tile_done, x1_ready, stored = ph.sem("tile_done"), ph.sem("x1_ready"), ph.sem("stored")
        QROWS = TC // W
        PER = TC // BANK
        NT = NTC * NCB * PER

        def place(t):
            quarter, rest = divmod(t, NCB * PER)
            c, mo = divmod(rest, NCB)
            col = quarter * TC + c * BANK
            return quarter, mo, slice(col, col + BANK), slice(c * BANK, (c + 1) * BANK)

        both = range(PER)
        rest = [(quarter, m, both) for quarter in range(2, NTC) for m in range(DB)]
        passes = [[(0, 0, both)]] + [[(0, m, both), (1, m - 1, both)] for m in range(1, DB)] + [[(1, DB - 1, both)]]
        passes += [rest[i:i + 2] for i in range(0, len(rest) - 2, 2)]
        passes += [[(quarter, m, range(c, c + 1)) for quarter, m, _ in rest[-2:]] for c in both]

        def filtered(t):
            quarter, c = t // (NCB * PER), t % (NCB * PER) // NCB
            order = [place for step in passes for place in step]
            return 1 + max(i for i, (q, _, cs) in enumerate(order) if q == quarter and c in cs)

        with nc.Block(no_gpsimd_drain=True) as block:

            @block.sync
            def _(sp):
                for m in range(DB):
                    for half in range(2):
                        cols = slice(half * L // 2, (half + 1) * L // 2)
                        if m >= 1:
                            sp.wait_ge(gated, 2 * (2 * (m - 1) + half + 1))
                        sp.dma_start(y_in[:, cols], dram["y"][m][:, cols]).then_inc(yz_in[half], 16)
                        sp.dma_start(z_in[:, cols], dram["z"][m][:, cols]).then_inc(yz_in[half], 16)
                    if m == 0:
                        for i in range(min(2, len(units))):
                            att.load(sp, i)
                sp.dma_start(x[:, :, :], io["x"][ds(b, 1)].rearrange("a (k p) l -> p (a k) l", p=CB)).then_inc(x_in, 16)
                for i in range(len(units)):
                    att.store(sp, i)
                dst = dram["x1"][ds(b, 1)].rearrange("a k p l -> p (a k) l")
                for quarter in range(NTC):
                    sp.wait_ge(x1_ready, NCB * PER * (quarter + 1))
                    cols = slice(quarter * TC, (quarter + 1) * TC)
                    sp.dma_start(dst[:, :, cols], x[:, :, cols]).then_inc(stored, 16)
                sp.wait_ge(stored, 16 * NTC)
                att.end(sp)

            @block.gpsimd
            def _(pool):
                for m in range(DB):
                    pool.memset(pad[:, m, 0::PADW - 1, :], 0.0)
                    pool.memset(pad[:, m, 1:H + 1, 0::PADW - 1], 0.0).then_inc(border, 1)
                att.ones_beside_v(pool)

            @block.tensor
            def _(pe):
                for g in range(att.steps):
                    att.tensor(pe, g)
                pe.wait_ge(x_in, 16)
                for t in range(NT):
                    quarter, mo, xcols, cols = place(t)
                    pe.wait_ge(conv, filtered(t))
                    if t >= 3:
                        pe.wait_ge(x1_ready, t - 2)
                    for k in range(DB):
                        pe.matmul(ps[0:CB, t % 3, :], keep["w_out"][:, k, mo * CB:(mo + 1) * CB],
                                  acc[:, quarter % 2, k, cols], start=(k == 0), stop=False)
                    pe.matmul(ps[0:CB, t % 3, :], keep["ident"][0:CB, 0:CB], x[:, mo, xcols], start=False, stop=True
                              ).then_inc(tile_done, 1)

            @block.scalar
            def _(act):
                for g in range(att.steps):
                    att.scalar(act, g)
                    if (i := att.finished(g)) is not None:
                        att.read_by_scalar(act, i)
                for t in range(NT):
                    _, mo, cols, _ = place(t)
                    act.wait_ge(tile_done, t + 1)
                    act.activation(x[:, mo, cols], ps[0:CB, t % 3, :], ACT.Copy).then_inc(x1_ready, 1)

            @block.vector
            def _(dve):
                taps = Count(tap)
                def gate(m, half):
                    rows = slice(half * H // 4, (half + 1) * H // 4)
                    inner = pad[:, m, 1:H + 1, 1:W + 1].rearrange("p (r two) w -> p r two w", two=2)[:, rows]
                    yv = y_in[:, :].rearrange("p (r two w) -> p r two w", two=2, w=W)[:, rows]
                    zv = z_in[:, :].rearrange("p (r two w) -> p r two w", two=2, w=W)[:, rows]
                    dve.wait_ge(yz_in[half], 32 * (m + 1))
                    dve.tensor_tensor(inner[:, :, 0, :], yv[:, :, 0, :], zv[:, :, 0, :], ALU.mult).then_inc(gated, 1)
                    dve.tensor_tensor(inner[:, :, 1, :], yv[:, :, 1, ::-1], zv[:, :, 1, :], ALU.mult).then_inc(gated, 1)

                def convolve(places, between={}):
                    for quarter, m, _ in places:
                        dve.wait_ge(gated, 4 * m + (2 if quarter == 0 else 4))
                        dve.wait_ge(border, m + 1)
                        if quarter >= 2:
                            dve.wait_ge(tile_done, NCB * PER * (quarter - 1))
                    last = {}
                    for k in range(9):
                        for quarter, m, cs in places:
                            lo, n = cs.start * ROWS, len(cs) * ROWS
                            dst = acc[:, quarter % 2, m, lo * W:(lo + n) * W].rearrange("p (r w) -> p r w", w=W)
                            r = quarter * QROWS + lo + k // 3
                            src = pad[:, m, r:r + n, k % 3:k % 3 + W]
                            w = keep["le"][:, m, k:k + 1]
                            if k == 0:
                                ins = dve.tensor_scalar(dst, src, w, None, ALU.mult)
                            else:
                                dve.wait_ge(tap, last[quarter, m])
                                ins = dve.scalar_tensor_tensor(dst, src, w, dst, ALU.mult, ALU.add)
                            if k < 8:
                                last[quarter, m] = taps.on(ins)
                            else:
                                ins.then_inc(conv, 1)
                        for t in between.get(k, ()):
                            statistics(t)

                def statistics(t):
                    _, mo, cols, _ = place(t)
                    dve.wait_ge(x1_ready, t + 1)
                    dve.bn_stats(x_stats[:, mo, cols.start // BANK, :], x[:, mo, cols])

                read = 0
                for i, places in enumerate(passes):
                    if i < DB:
                        gate(i, 0)
                        if i == 0:
                            convolve(places)
                        gate(i, 1)
                    done = [t for t in range(NT) if all(t // (NCB * PER) < quarter for quarter, _, _ in places)]
                    extra = done[read:read + 4] if i > DB else []
                    if i > 0:
                        convolve(places, {4: extra[:2], 7: extra[2:]})
                    read += len(extra)
                for t in range(read, NT):
                    statistics(t)


def layer1_project(nc, io, keep, dram, x, x_stats, b, units):
    with Phase(nc, "l1pre") as ph:
        NB = 3 * NCB
        NQK = 2 * NCB
        NQKV = NB * NCH
        w_qkv = ph.sb("w_qkv", [CB, NCB, 3 * C])
        pad = ph.sb("pad", [CB, 2, PADW, PADW])
        qkv = ph.sb("qkv", [CB, 2, L])
        sq = ph.sb("sq", [CB, 2, TC])
        vt = ph.sb("vt", [128, 2, KT, HD])
        hi = ph.sb("hi", [CB, L], F16)
        lo = ph.sb("lo", [CB, L], F16)
        inv_b = ph.sb("inv_b", [CB, L])
        length = ph.sb("length", [128, 2 * KT])
        inv = ph.sb("inv", [128, 2 * KT])
        inv_t = ph.sb("inv_t", [2 * KT, 128])
        ps = ph.ps("ps", [128, 2, BANK])
        ss_ps = ph.ps("ss", [128, BANK])
        gn = GroupNorm(ph, keep, x, ps[:, 0, :], False, x_stats)
        att = Attention(ph, keep, dram, b - 1, units, 2, 1)
        w_loaded, x_norm, border = ph.sem("w_loaded"), ph.sem("x_norm"), ph.sem("border")
        tile_done, tile_read = ph.sem("tile_done"), ph.sem("tile_read")
        tap, conv, conv_half = ph.sem("tap"), ph.sem("conv"), ph.sem("conv_half")
        sq_ready, ss_done, root = ph.sem("sq_ready"), ph.sem("ss_done"), ph.sem("root")
        clipped, inv_ready, turned, inv_t_ready = ph.sem("clipped"), ph.sem("inv_ready"), ph.sem("turned"), ph.sem("inv_t_ready")
        inv_stored, inv_b_in = ph.sem("inv_stored"), ph.sem("inv_b_in")
        unit, hi_ready, lo_ready, parts_stored = ph.sem("unit"), ph.sem("hi_ready"), ph.sem("lo_ready"), ph.sem("parts_stored")
        vt_stored = ph.sem("vt_stored")
        b_qkv, b_dw, b_proj = keep["dw"][:, 9, :], keep["dw"][:, 10, :], keep["chan"][:, 2, :]
        HALF = L // 2
        PIECES = NCH if units else 0
        if units:
            fin_x = ph.sb("fin_x", [CB, NCB * BANK])
            fin_out = sq[:, :, :].rearrange("p i (k l) -> p i k l", k=NCB)
            den = ph.sb("den", [128, HEADS * L // 128])
            v_flat = att.v[0:CB, 0, :, :].rearrange("p t c -> p (t c)")
            views = [[att.p[0:CB, i, :] for i in range(3)],
                     [v_flat[:, 0:NCB * BANK], v_flat[:, NCB * BANK:2 * NCB * BANK], fin_x[:, :]]]
            fin_o, fin_r, fin_x1 = ([views[i][k].rearrange("p (k l) -> p k l", k=NCB) for i in range(2)] for k in range(3))
        den_in, den_inv, den_stored, scaled = ph.sem("den_in"), ph.sem("den_inv"), ph.sem("den_stored"), ph.sem("scaled")
        fin_in = [ph.sem("fin_in0"), ph.sem("fin_in1")]
        out_stored = [ph.sem("out_stored0"), ph.sem("out_stored1")]
        turns = [[("turn", j, g) for g in range(KT // 4)] for j in range(2)]
        ends = [("finish", i, mo) for i in range(PIECES) for mo in range(NCB)]
        tail = turns[0] + ends[:len(ends) // 2] + turns[1][:KT // 8] + ends[len(ends) // 2:] + turns[1][KT // 8:]
        tail_tile = {what: NQKV + i for i, what in enumerate(tail)}
        BESIDE = att.steps // 12
        BEHIND = (att.steps - (NB - 2) * BESIDE) // (NB - 2)

        def plan():
            yield "norm", None
            g = 0
            for j in range(NB):
                beside = BESIDE if 1 <= j < NB - 1 else 0
                behind = (att.steps - g - beside if j == NB - 2 else BEHIND) if 1 <= j < NB - 1 else 0
                if j >= 2:
                    yield "square", j - 2
                    yield "attend", range(g, g + behind // 2)
                    yield "turn", j - 2
                    g += behind // 2
                    behind -= behind // 2
                yield "project", (j, range(g, g + beside))
                g += beside
                yield "attend", range(g, g + behind)
                g += behind

        def load_piece(sp, i):
            cols, sem = slice(i * BANK, (i + 1) * BANK), fin_in[i % 2]
            sp.dma_start(fin_o[i % 2], dram["o"][ds(b - 1, 1)].rearrange("a (k p) l -> p (a k) l", p=CB)[:, :, cols]
                         ).then_inc(sem, 16)
            sp.dma_start(fin_x1[i % 2], dram["x1"][ds(b - 1, 1)].rearrange("a k p l -> p (a k) l")[:, :, cols]
                         ).then_inc(sem, 16)
            for h in range(HEADS):
                k, half = divmod(h, 2)
                src = dram["rden"][h:h + 1, cols].partition_broadcast(HD).rearrange("p a l -> p (a l)")
                sp.dma_start(fin_r[i % 2][half * HD:(half + 1) * HD, k, :], src).then_inc(sem, 16)

        with nc.Block(no_gpsimd_drain=True) as block:

            @block.sync
            def _(sp):
                sp.dma_start(w_qkv[:, :, :], io["w_qkv_t"]).then_inc(w_loaded, 16)
                for i in range(min(2, len(units))):
                    att.load(sp, i)
                for j in range(NQK):
                    sp.wait_ge(inv_t_ready, j + 1)
                    sp.dma_start(dram["inv"].rearrange("h (t p) -> (h t) p", p=128)[2 * j * KT:2 * (j + 1) * KT, :],
                                 inv_t[:, :]).then_inc(inv_stored, 16)
                    sp.wait_ge(inv_stored, 16 * (j + 1))
                    if j >= 1:
                        sp.wait_ge(unit, 2 * j)
                    for i in range(2):
                        src = dram["inv"][2 * j + i:2 * j + i + 1, :].partition_broadcast(HD)
                        sp.dma_start(inv_b[i * HD:(i + 1) * HD, :], src.rearrange("p a l -> p (a l)")
                                     ).then_inc(inv_b_in, 16)
                    dst = dram["q" if j < NCB else "k"][ds(b, 1)].rearrange("a s c l -> (a s) c l")
                    for part, (src, ready) in enumerate(((hi, hi_ready), (lo, lo_ready))):
                        sp.wait_ge(ready, 2 * (j + 1))
                        sp.dma_start(dst[part, (j % NCB) * CB:(j % NCB + 1) * CB, :], src[:, :]).then_inc(parts_stored, 16)
                    if j == NQK - 2 and units:
                        att.end(sp)
                        sp.dma_start(den[:, :], dram["den"][ds(b - 1, 1)].rearrange("a h (t l) -> (a h t) l", l=128)
                                     ).then_inc(den_in, 16)
                        sp.wait_ge(den_inv, 1)
                        sp.dma_start(dram["rden"].rearrange("h (t l) -> (h t) l", l=128), den[:, :]).then_inc(den_stored, 16)
                        sp.wait_ge(den_stored, 16)
                        for i in range(2):
                            load_piece(sp, i)
                for i in range(PIECES):
                    sp.wait_ge(tile_read, tail_tile["finish", i, NCB - 1] + 1)
                    dst = io["out"][ds(b - 1, 1)].rearrange("a (k p) l -> p (a k) l", p=CB)
                    sp.dma_start(dst[:, :, i * BANK:(i + 1) * BANK], fin_out[:, i % 2, :, :]).then_inc(out_stored[i % 2], 16)
                    if i + 2 < PIECES:
                        load_piece(sp, i + 2)
                sp.wait_ge(parts_stored, 16 * 2 * NQK)
                for i in range(2 if units else 0):
                    sp.wait_ge(out_stored[i], 16 * PIECES // 2)

            @block.gpsimd
            def _(pool):
                for i in range(2):
                    pool.memset(pad[:, i, 0::PADW - 1, :], 0.0)
                    pool.memset(pad[:, i, 1:H + 1, 0::PADW - 1], 0.0).then_inc(border, 1)
                att.ones_beside_v(pool)

            @block.tensor
            def _(pe):
                def project(j, steps):
                    if j == 0:
                        pe.wait_ge(w_loaded, 16)
                        pe.wait_ge(x_norm, NCB)
                    for c in range(NCH):
                        t = j * NCH + c
                        if t >= 2:
                            pe.wait_ge(tile_read, t - 1)
                        for k in range(NCB):
                            mm = pe.matmul(ps[0:CB, t % 2, :], w_qkv[:, k, j * CB:(j + 1) * CB],
                                           x[:, k, c * BANK:(c + 1) * BANK], start=(k == 0), stop=(k == NCB - 1))
                        mm.then_inc(tile_done, 1)
                        for s in share(c, NCH, len(steps)):
                            att.tensor(pe, steps[s])

                def lengths(j):
                    if j >= 1:
                        pe.wait_ge(root, j)
                    out = ss_ps[:, 0:2 * KT].rearrange("p (h t) -> p h t", h=2)
                    for c in range(NTC):
                        pe.wait_ge(sq_ready, j * NTC + c + 1)
                        for i in range(TC // 128):
                            mm = pe.matmul(out[:, :, c * TC // 128 + i], sq[:, c % 2, i * 128:(i + 1) * 128],
                                           keep["head_sum"][:, :], start=True, stop=True)
                        mm.then_inc(ss_done, 1)

                def turn_inverse(j):
                    pe.wait_ge(inv_ready, j + 1)
                    if j >= 1:
                        pe.wait_ge(inv_t_ready, j)
                    pe.transpose(ss_ps[0:2 * KT, 128:256], inv[:, :], keep["ident"][:, :]).then_inc(turned, 1)

                def turn_v(j, g):
                    if j == 1 and g < KT // 8:
                        pe.wait_ge(conv_half, NB)
                    else:
                        pe.wait_ge(conv, NQK + 1 + j)
                    t = tail_tile["turn", j, g]
                    pe.wait_ge(tile_read, t - 1)
                    for i in range(4):
                        col = (4 * g + i) * 128
                        mm = pe.transpose(ps[:, t % 2, i * CB:(i + 1) * CB], qkv[:, j % 2, col:col + 128],
                                          keep["ident"][0:CB, 0:CB])
                    mm.then_inc(tile_done, 1)

                def finish(i, mo):
                    t = tail_tile["finish", i, mo]
                    pe.wait_ge(scaled, i + 1)
                    pe.wait_ge(tile_read, t - 1)
                    for k in range(NCB):
                        pe.matmul(ps[0:CB, t % 2, :], keep["w_proj"][:, k, mo * CB:(mo + 1) * CB], fin_o[i % 2][:, k, :],
                                  start=(k == 0), stop=False)
                    pe.matmul(ps[0:CB, t % 2, :], keep["ident"][0:CB, 0:CB], fin_x1[i % 2][:, mo, :],
                              start=False, stop=True).then_inc(tile_done, 1)

                for what, arg in plan():
                    if what == "attend":
                        for g in arg:
                            att.tensor(pe, g)
                    elif what == "norm":
                        gn.tensor(pe)
                    elif what == "project":
                        project(*arg)
                    elif what == "square":
                        lengths(arg)
                    else:
                        turn_inverse(arg)
                for what, i, k in tail:
                    (turn_v if what == "turn" else finish)(i, k)

            @block.scalar
            def _(act):
                def unload(j, steps):
                    if j == 0:
                        act.wait_ge(border, 2)
                    if j >= 2:
                        act.wait_ge(conv, j - 1)
                    for c in range(NCH):
                        t = j * NCH + c
                        act.wait_ge(tile_done, t + 1)
                        act.activation(pad[:, j % 2, 1 + c * ROWS:1 + (c + 1) * ROWS, 1:W + 1],
                                       ps[0:CB, t % 2, :].rearrange("p (r w) -> p r w", w=W), ACT.Identity,
                                       bias=b_qkv[:, j:j + 1]).then_inc(tile_read, 1)
                        for s in share(c, NCH, len(steps)):
                            attend(steps[s])

                def attend(g):
                    att.scalar(act, g)
                    if (i := att.finished(g)) is not None:
                        att.read_by_scalar(act, i)
                        att.store(act, i)
                        if i + 2 < len(units):
                            att.load(act, i + 2)

                def lengths(j):
                    act.wait_ge(conv, j + 1)
                    for c in range(NTC):
                        i = j * NTC + c
                        if i >= 2:
                            act.wait_ge(ss_done, i - 1)
                        act.activation(sq[:, c % 2, :], qkv[:, j % 2, c * TC:(c + 1) * TC], ACT.Square).then_inc(sq_ready, 1)
                    act.wait_ge(ss_done, NTC * (j + 1))
                    if j >= 1:
                        act.wait_ge(inv_ready, j)
                    act.activation(length[:, :], ss_ps[:, 0:2 * KT], ACT.Sqrt).then_inc(root, 1)

                def unload_inverse(j):
                    act.wait_ge(turned, j + 1)
                    if j >= 1:
                        act.wait_ge(inv_stored, 16 * j)
                    act.activation(inv_t[:, :], ss_ps[0:2 * KT, 128:256], ACT.Copy).then_inc(inv_t_ready, 1)

                for what, arg in plan():
                    if what == "attend":
                        for g in arg:
                            attend(g)
                    elif what == "norm":
                        gn.scalar(act)
                    elif what == "project":
                        unload(*arg)
                    elif what == "square":
                        lengths(arg)
                    else:
                        unload_inverse(arg)
                def unload_v(j, g):
                    t = tail_tile["turn", j, g]
                    if j == 1 and g == 0:
                        act.wait_ge(vt_stored, 16)
                    act.wait_ge(tile_done, t + 1)
                    act.activation(vt[:, :, 4 * g:4 * g + 4, :],
                                   ps[:, t % 2, 0:4 * CB].rearrange("p (i h c) -> p h i c", i=4, h=2),
                                   ACT.Copy).then_inc(tile_read, 1)
                    if g == KT // 4 - 1:
                        act.wait_ge(tile_read, t + 1)
                        dst = dram["v"][ds(b, 1)].rearrange("a h p t c -> p (a h) (t c)")
                        act.dma_start(dst[:, 2 * j:2 * j + 2, :], vt[:, :, :, :].rearrange("p h t c -> p h (t c)")
                                      ).then_inc(vt_stored, 16)

                def unload_piece(i, mo):
                    t = tail_tile["finish", i, mo]
                    act.wait_ge(tile_done, t + 1)
                    if i >= 2:
                        act.wait_ge(out_stored[i % 2], 16 * (i // 2))
                    act.activation(fin_out[:, i % 2, mo, :], ps[0:CB, t % 2, :], ACT.Identity,
                                   bias=b_proj[:, mo:mo + 1]).then_inc(tile_read, 1)

                for what, i, k in tail:
                    (unload_v if what == "turn" else unload_piece)(i, k)
                act.wait_ge(vt_stored, 32)
                att.end(act)

            @block.vector
            def _(dve):
                gn.vector(dve)
                for k in range(NCB):
                    dve.tensor_scalar(x[:, k, :], x[:, k, :], gn.scale[:, k:k + 1], gn.shift[:, k:k + 1],
                                      ALU.mult, ALU.add).then_inc(x_norm, 1)
                taps = Count(tap)

                def convolve(j):
                    order = [(k, half) for half in range(2) for k in range(9)]
                    last = {}
                    for k, half in order if j in (0, NB - 1) else sorted(order):
                        n = H // 2
                        r0 = half * n
                        dst = qkv[:, j % 2, r0 * W:(r0 + n) * W].rearrange("p (r w) -> p r w", w=W)
                        src = pad[:, j % 2, r0 + k // 3:r0 + k // 3 + n, k % 3:k % 3 + W]
                        w = keep["dw"][:, k, j:j + 1]
                        if k == 0:
                            dve.wait_ge(tile_read, NCH * j + min(NCH, NCH // 2 * (half + 1) + 1))
                            ins = dve.tensor_scalar(dst, src, w, b_dw[:, j:j + 1], ALU.mult, ALU.add)
                        else:
                            dve.wait_ge(tap, last[half])
                            ins = dve.scalar_tensor_tensor(dst, src, w, dst, ALU.mult, ALU.add)
                        if k < 8:
                            last[half] = taps.on(ins)
                        elif half == 1:
                            ins.then_inc(conv, 1)
                        else:
                            ins.then_inc(conv_half, 1)
                        if half == 1 and k == 3 and 1 <= j <= NQK:
                            invert(j - 1)
                        if half == 1 and k == 2 and j == NB - 2 and units:
                            dve.wait_ge(den_in, 16)
                            dve.reciprocal(den[:, :], den[:, :]).then_inc(den_inv, 1)
                        if j == NB - 1 and k % 2 == 1:
                            scale(half * 4 + k // 2)

                def scale(i):
                    if i < PIECES:
                        dve.wait_ge(fin_in[i % 2], 16 * (2 + HEADS) * (i // 2 + 1))
                        dve.tensor_tensor(fin_o[i % 2], fin_o[i % 2], fin_r[i % 2], ALU.mult).then_inc(scaled, 1)

                def invert(j):
                    dve.wait_ge(root, j + 1)
                    dve.tensor_scalar(length[:, :], length[:, :], 1e-12, 1.0 / QSCALE, ALU.max, ALU.mult).then_inc(clipped, 1)
                    dve.wait_ge(clipped, j + 1)
                    dve.reciprocal(inv[:, :], length[:, :]).then_inc(inv_ready, 1)

                def normalize(j):
                    dve.wait_ge(inv_b_in, 32 * (j + 1))
                    for i in range(2):
                        cols = slice(i * HALF, (i + 1) * HALF)
                        dve.tensor_tensor(qkv[:, j % 2, cols], qkv[:, j % 2, cols], inv_b[:, cols], ALU.mult).then_inc(unit, 1)
                    if j >= 1:
                        dve.wait_ge(parts_stored, 32 * j)
                    for i in range(2):
                        cols = slice(i * HALF, (i + 1) * HALF)
                        dve.wait_ge(unit, 2 * j + i + 1)
                        dve.tensor_copy(hi[:, cols], qkv[:, j % 2, cols]).then_inc(hi_ready, 1)
                    for i in range(2):
                        cols = slice(i * HALF, (i + 1) * HALF)
                        dve.wait_ge(hi_ready, 2 * j + i + 1)
                        dve.tensor_tensor(lo[:, cols], qkv[:, j % 2, cols], hi[:, cols], ALU.subtract).then_inc(lo_ready, 1)

                for j in range(NB):
                    if j >= 2:
                        dve.wait_ge(lo_ready, 2 * (j - 1))
                    convolve(j)
                    if 1 <= j <= NQK:
                        normalize(j - 1)


def layer1_finish(nc, io, keep, dram, b):
    with Phase(nc, "l1post") as ph:
        o = ph.sb("o", [CB, NCB, L])
        r = ph.sb("r", [CB, NCB, L])
        x = ph.sb("x", [CB, NCB, L])
        den = ph.sb("den", [128, HEADS * L // 128])
        ps = ph.ps("ps", [128, 8, BANK])
        den_in, den_inv, inv_stored = ph.sem("den_in"), ph.sem("den_inv"), ph.sem("inv_stored")
        o_in = [ph.sem(f"o_in{i}") for i in range(NTC)]
        r_in = [ph.sem(f"r_in{i}") for i in range(NTC)]
        scaled, tile_done, ready, stored = ph.sem("scaled"), ph.sem("tile_done"), ph.sem("ready"), ph.sem("stored")
        b_proj = keep["chan"][:, 2, :]
        PER = TC // BANK
        NT = NTC * NCB * PER

        def place(t):
            chunk, rest = divmod(t, NCB * PER)
            mo, c = divmod(rest, PER)
            return mo, slice(chunk * TC + c * BANK, chunk * TC + (c + 1) * BANK)

        with nc.Block(no_gpsimd_drain=True) as block:

            @block.sync
            def _(sp):
                d = dram["den"][ds(b, 1)].rearrange("a h (t l) -> (a h t) l", l=128)
                sp.dma_start(den[:, :], d).then_inc(den_in, 16)
                for i in range(NTC):
                    if i == 1:
                        sp.wait_ge(inv_stored, 16)
                    cols = slice(i * TC, (i + 1) * TC)
                    sp.dma_start(o[:, :, cols], dram["o"][ds(b, 1)].rearrange("a (k p) l -> p (a k) l", p=CB)[:, :, cols]
                                 ).then_inc(o_in[i], 16)
                    sp.dma_start(x[:, :, cols], dram["x1"][ds(b, 1)].rearrange("a k p l -> p (a k) l")[:, :, cols]
                                 ).then_inc(o_in[i], 16)
                dst = io["out"][ds(b, 1)].rearrange("a (k p) l -> p (a k) l", p=CB)
                for i in range(NTC):
                    cols = slice(i * TC, (i + 1) * TC)
                    sp.wait_ge(ready, NCB * PER * (i + 1))
                    sp.dma_start(dst[:, :, cols], x[:, :, cols]).then_inc(stored, 16)
                sp.wait_ge(stored, 16 * NTC)

            @block.scalar
            def _(act):
                act.wait_ge(den_inv, 1)
                act.dma_start(dram["rden"].rearrange("h (t l) -> (h t) l", l=128), den[:, :]).then_inc(inv_stored, 16)
                act.wait_ge(inv_stored, 16)
                for i in range(NTC):
                    cols = slice(i * TC, (i + 1) * TC)
                    for h in range(HEADS):
                        k, half = divmod(h, 2)
                        src = dram["rden"][h:h + 1, cols].partition_broadcast(HD).rearrange("p a l -> p (a l)")
                        act.dma_start(r[half * HD:(half + 1) * HD, k, cols], src).then_inc(r_in[i], 16)

            @block.tensor
            def _(pe):
                for t in range(NT):
                    mo, cols = place(t)
                    pe.wait_ge(scaled, t // (NCB * PER) + 1)
                    if t >= 8:
                        pe.wait_ge(ready, t - 7)
                    for k in range(NCB):
                        mm = pe.matmul(ps[0:CB, t % 8, :], keep["w_proj"][:, k, mo * CB:(mo + 1) * CB],
                                       o[:, k, cols], start=(k == 0), stop=(k == NCB - 1))
                    mm.then_inc(tile_done, 1)

            @block.vector
            def _(dve):
                dve.wait_ge(den_in, 16)
                dve.reciprocal(den[:, :], den[:, :]).then_inc(den_inv, 1)

                def scale(i):
                    cols = slice(i * TC, (i + 1) * TC)
                    dve.wait_ge(o_in[i], 32)
                    dve.wait_ge(r_in[i], 16 * HEADS)
                    dve.tensor_tensor(o[:, :, cols], o[:, :, cols], r[:, :, cols], ALU.mult).then_inc(scaled, 1)

                scale(0)
                for i in range(NTC):
                    if i + 1 < NTC:
                        scale(i + 1)
                    for t in range(NCB * PER * i, NCB * PER * (i + 1)):
                        mo, cols = place(t)
                        dve.wait_ge(tile_done, t + 1)
                        dve.scalar_tensor_tensor(x[:, mo, cols], ps[0:CB, t % 8, :], b_proj[:, mo:mo + 1], x[:, mo, cols],
                                                 ALU.add, ALU.add).then_inc(ready, 1)


def build(nc, io):
    batches = io["x"].shape[0]
    scratch = {
        "u": ([DB, 128, L], F32), "z": ([DB, 128, L], F32), "delta": ([DB, 128, L], F32), "y": ([DB, 128, L], F32),
        "bc": ([2 * NST, L], F32), "inv": ([8, L], F32), "rden": ([HEADS, L], F32),
        "x1": ([batches, NCB, CB, L], F32), "q": ([batches, 2, C, L], F16), "k": ([batches, 2, C, L], F16),
        "v": ([batches, HEADS, 128, KT, HD], F32), "o": ([batches, C, L], F32), "den": ([batches, HEADS, L], F32),
    }
    dram = {k: nc.dram_tensor(f"scratch_{k}", shape, dt, kind="Internal").ap() for k, (shape, dt) in scratch.items()}
    kept = {
        "ident": [128, 128], "group_mean": [CB, CB], "all_mean": [CB, CB], "head_sum": [CB, 2],
        "x_proj": [128, DB, DTR + 2 * NST], "dt_proj": [DTR, DB, 128], "w_proj": [CB, NCB, C],
        "chan": [CB, 3, NCB], "inner": [128, 7, DB], "le": [128, DB, 9], "a": [128, DB, NST],
        "dw": [CB, 11, 6], "w_out": [128, DB, C], "temp": [128, 2, HEADS],
    }
    with ExitStack() as ctx:
        keep = {k: ctx.enter_context(nc.sbuf_tensor(f"keep_{k}", shape, F32)) for k, shape in kept.items()}
        setup(nc, io, keep)

        everything = [(h, chunk) for h in range(HEADS) for chunk in range(NTC)]

        def between(b, units0, units1):
            name = f"between{nc.next_id()}"
            with nc.sbuf_tensor(f"{name}_x", [CB, NCB, L], F32) as x, \
                    nc.sbuf_tensor(f"{name}_stats", [CB, NCB, NCH, 6], F32) as x_stats:
                layer0_finish(nc, io, keep, dram, x, x_stats, b, units0)
                layer1_project(nc, io, keep, dram, x, x_stats, b, units1)

        layer0_project(nc, io, keep, dram, 0)
        scan_alone(nc, keep, dram)
        between(0, [], [])
        if batches > 1:
            with nc.Fori(1, batches) as b:
                layer0_project(nc, io, keep, dram, b)
                scan_and_attend(nc, keep, dram, b - 1, True, everything[:-3])
                between(b, everything[-3:-2], everything[-2:])
        scan_and_attend(nc, keep, dram, batches - 1, False, everything)
        layer1_finish(nc, io, keep, dram, batches - 1)


def lay_out(inputs):
    a = {k.split("_conv_")[-1] if "_conv_" in k else k: np.asarray(v) for k, v in inputs.items()}
    w_dw = a["w_dw"].reshape(3 * C, 9)
    rows = lambda v, p: v.reshape(-1, p).T
    eye = np.eye(128, dtype=np.float32)
    group = np.kron(np.eye(CB // GROUP, dtype=np.float32), np.full((GROUP, GROUP), 1.0 / GROUP, np.float32))
    heads = np.kron(np.eye(2, dtype=np.float32), np.ones((HD, 1), np.float32))
    blocks = lambda w, p: w.reshape(-1, p, w.shape[1]).transpose(1, 0, 2)
    inner = np.stack([rows(a["conv1d_b"], 128), rows(a["dt_proj_b"], 128), rows(a["Dskip"], 128)]
                     + [rows(a["conv1d_w"][:, k], 128) for k in range(4)], axis=1)
    dw = np.stack([rows(w_dw[:, k], CB) for k in range(9)] + [rows(a["b_qkv"], CB), rows(a["b_dw"], CB)], axis=1)
    return {
        "x": a["x"].reshape(-1, C, L),
        "ident": eye,
        "group_mean": group,
        "all_mean": np.full((CB, CB), 1.0 / C, np.float32),
        "head_sum": heads,
        "in_proj_t": blocks(a["in_proj_w"].T, CB),
        "x_proj_t": blocks(a["x_proj_w"].T, 128),
        "dt_proj_t": a["dt_proj_w"].T.reshape(DTR, DB, 128),
        "out_proj": blocks(a["out_proj_w"], CB),
        "proj_out_t": blocks(a["proj_out_w"].T, CB),
        "w_qkv_t": blocks(a["w_qkv"].T, CB),
        "w_proj_t": blocks(a["w_proj"].T, CB),
        "chan": np.stack([rows(a["gn_gamma"], CB), rows(a["gn_beta"], CB), rows(a["b_proj"], CB)], axis=1),
        "inner": inner,
        "le": blocks(a["le_w"].reshape(DIN, 9), 128),
        "a_log": blocks(a["A_log"], 128),
        "dw": dw,
        "temperature": a["temperature"].reshape(HEADS),
    }


def kernel(**inputs):
    import concourse.bacc as bacc
    from concourse.bass_utils import run_bass_kernel_spmd

    nc = bacc.Bacc("TRN2", target_bir_lowering=False, num_devices=1)
    arrays, io = {}, {}
    for name, a in lay_out(inputs).items():
        a = np.ascontiguousarray(a)
        arrays[f"in_{name}"] = a
        io[name] = nc.dram_tensor(f"in_{name}", a.shape, mybir.dt.from_np(a.dtype), kind="ExternalInput").ap()
    batches = io["x"].shape[0]
    io["out"] = nc.dram_tensor("out", (batches, C, L), F32, kind="ExternalOutput").ap()
    build(nc, io)
    r = run_bass_kernel_spmd(nc, [arrays], core_ids=[0])
    return r.results[0]["out"].reshape(batches, C, H, W)
```
